# Optimizing a Trainium2 kernel written in Bass

```python
import numpy as np
import jax
import jax.numpy as jnp

def _softmax(x, axis=-1):
    return jax.nn.softmax(x, axis=axis)

def _gelu(x):
    return jax.nn.gelu(x, approximate=True)

def _silu(x):
    return jax.nn.silu(x)

def _sigmoid(x):
    return jax.nn.sigmoid(x)

def _layernorm(x, axis=-1, eps=1e-05):
    m = jnp.mean(x, axis=axis, keepdims=True)
    v = jnp.var(x, axis=axis, keepdims=True)
    return (x - m) / jnp.sqrt(v + eps)

def _scatter_add(tgt, idx, src, axis=0):
    return tgt.at[idx].add(src)

def _segment_sum(src, seg, n):
    return jax.ops.segment_sum(src, seg, n)
kernel_name = 'mk_decoder_preln_d2_seqx_r8_5ab0f9'

def setup_inputs(seed: int=0):
    np.random.seed(seed)
    _w = jnp.asarray

    def _rec_inputs():
        import jax
        import jax.numpy as jnp
        _rk = jax.random.key(seed)
        x = -0.000125 + 0.9999 * jax.random.normal(jax.random.fold_in(_rk, 1), (2, 256, 512), jnp.float32)
        _lenS = 256 - jax.random.randint(jax.random.fold_in(_rk, 7), (2,), 0, max(1, 256 // 4) + 1, jnp.int32)
        _lenS2 = 512 - jax.random.randint(jax.random.fold_in(_rk, 8), (2,), 0, max(1, 512 // 4) + 1, jnp.int32)
        _ctx_4096P = jax.random.normal(jax.random.fold_in(_rk, 11), (2, 16, 512), jnp.float32)
        _ctx_4096c = jax.random.dirichlet(jax.random.fold_in(_rk, 511), 0.3 * jnp.ones((16,), jnp.float32), (2, 512))
        _ctx_4096t = jnp.einsum('bsk,bkd->bsd', _ctx_4096c, _ctx_4096P)
        _ctx_4096t = _ctx_4096t * jax.lax.rsqrt(jnp.mean(jnp.square(_ctx_4096t)) + 1e-12) * 0.953939
        ctx_4096 = -5.72187e-05 + 0.999849 * (_ctx_4096t + 0.3 * jax.random.normal(jax.random.fold_in(_rk, 611), (2, 512, 512), jnp.float32))
        return (x, ctx_4096)
    x, ctx_4096 = _rec_inputs()

    def _L0_attn_setup():
        import jax, jax.numpy as jnp
        import numpy as np
        N_HEADS = 32
        N_KV_HEADS = 16
        N_EMBD = 512
        HEAD_DIM = N_EMBD // N_HEADS
        GROUPS = N_HEADS // N_KV_HEADS
        KV_DIM = N_KV_HEADS * HEAD_DIM
        SCALE = 1.0 / np.sqrt(np.float32(N_HEADS))
        key = jax.random.key(seed)
        ks = jax.random.split(key, 4)
        B, T, C = (1, 256, N_EMBD)
        s = 1.0 / np.sqrt(np.float32(C))
        return {'x': jax.random.normal(ks[0], (B, T, C), dtype=jnp.float32), 'Wq': jax.random.normal(ks[1], (C, C), dtype=jnp.float32) * s, 'bq': jnp.zeros((C,), dtype=jnp.float32), 'Wk': jax.random.normal(ks[2], (KV_DIM, C), dtype=jnp.float32) * s, 'bk': jnp.zeros((KV_DIM,), dtype=jnp.float32), 'Wv': jax.random.normal(ks[3], (KV_DIM, C), dtype=jnp.float32) * s, 'bv': jnp.zeros((KV_DIM,), dtype=jnp.float32)}
    _L0_attn_all = _L0_attn_setup()
    _L0_attn_in = {k: v for k, v in _L0_attn_all.items() if k in ('Wq', 'bq', 'Wk', 'bk', 'Wv', 'bv')}
    del _L0_attn_all

    def _L0_xattn_setup():
        import jax, jax.numpy as jnp
        import numpy as np
        QMIN = 0.0
        QMAX = 255.0

        def fake_quant(x, scale, zp):
            s = scale.reshape(())
            z = zp.reshape(())
            q = jnp.clip(jnp.round(x / s + z), QMIN, QMAX)
            return (q - z) * s
        key = jax.random.key(seed)
        k1, k2 = jax.random.split(key)
        B, M, K, N = (4, 256, 512, 512)
        x1 = jax.random.normal(k1, (B, M, K), dtype=jnp.float32)
        x2 = jax.random.normal(k2, (B, K, N), dtype=jnp.float32)
        x1_scale = jnp.full((1,), 8.0 / 255.0, dtype=jnp.float32)
        x1_zp = jnp.full((1,), 128.0, dtype=jnp.float32)
        x2_scale = jnp.full((1,), 8.0 / 255.0, dtype=jnp.float32)
        x2_zp = jnp.full((1,), 128.0, dtype=jnp.float32)
        return {'x1': x1, 'x2': x2, 'x1_scale': x1_scale, 'x1_zp': x1_zp, 'x2_scale': x2_scale, 'x2_zp': x2_zp}
    _L0_xattn_all = _L0_xattn_setup()
    _L0_xattn_in = {k: v for k, v in _L0_xattn_all.items() if k in ('x1_scale', 'x1_zp', 'x2_scale', 'x2_zp')}
    del _L0_xattn_all

    def _L0_ffn_setup():
        import jax, jax.numpy as jnp
        import numpy as np
        EPS = 1e-05

        def rms_norm(x):
            return x * jax.lax.rsqrt(jnp.mean(x * x, axis=-1, keepdims=True) + EPS)

        def activation_quant(x):
            scale = 127.0 / jnp.clip(jnp.max(jnp.abs(x), axis=-1, keepdims=True), EPS, None)
            return jnp.clip(jnp.round(x * scale), -128.0, 127.0) / scale

        def weight_quant(w):
            scale = 1.0 / jnp.clip(jnp.mean(jnp.abs(w)), EPS, None)
            return jnp.clip(jnp.round(w * scale), -1.0, 1.0) / scale
        key = jax.random.key(seed)
        k1, k2, k3 = jax.random.split(key, 3)
        B, S, D = (4, 256, 512)
        x = jax.random.normal(k1, (B, S, D), dtype=jnp.float32)
        W = jax.random.normal(k2, (D, D), dtype=jnp.float32) * (1.0 / np.sqrt(D))
        b = jax.random.normal(k3, (D,), dtype=jnp.float32) * 0.02
        return {'x': x, 'W': W, 'b': b}
    _L0_ffn_all = _L0_ffn_setup()
    _L0_ffn_in = {k: v for k, v in _L0_ffn_all.items() if k in ('W', 'b')}
    del _L0_ffn_all

    def _L1_attn_setup():
        import math
        import jax, jax.numpy as jnp
        import numpy as np
        N_HEADS = 32
        ALIBI_BIAS_MAX = 8

        def _alibi_slopes(n_heads, alibi_bias_max=8):
            _n = 2 ** math.ceil(math.log2(n_heads))
            m = jnp.arange(1, _n + 1, dtype=jnp.float32) * (alibi_bias_max / _n)
            slopes = 1.0 / jnp.power(2.0, m)
            if _n != n_heads:
                slopes = jnp.concatenate([slopes[1::2], slopes[::2]])[:n_heads]
            return slopes
        key = jax.random.key(seed)
        k1, k2, k3 = jax.random.split(key, 3)
        B, S, D = (1, 256, 512)
        x = jax.random.normal(k1, (B, S, D), dtype=jnp.float32)
        w_qkv = jax.random.normal(k2, (3 * D, D), dtype=jnp.float32) * 0.02
        b_qkv = jnp.zeros((3 * D,), dtype=jnp.float32)
        w_out = jax.random.normal(k3, (D, D), dtype=jnp.float32) * 0.02
        b_out = jnp.zeros((D,), dtype=jnp.float32)
        return {'x': x, 'w_qkv': w_qkv, 'b_qkv': b_qkv, 'w_out': w_out, 'b_out': b_out}
    _L1_attn_all = _L1_attn_setup()
    _L1_attn_in = {k: v for k, v in _L1_attn_all.items() if k in ('w_qkv', 'b_qkv', 'w_out', 'b_out')}
    del _L1_attn_all

    def _L1_xattn_setup():
        import jax, jax.numpy as jnp
        import numpy as np
        HEADS = 32
        KV_HEADS = 8
        HEAD_DIM = 128
        EPS = 1e-06

        def rms_norm(x, w):
            var = jnp.mean(jnp.square(x.astype(jnp.float32)), axis=-1, keepdims=True)
            return (x.astype(jnp.float32) * jax.lax.rsqrt(var + EPS)).astype(x.dtype) * w
        key = jax.random.key(seed)
        ks = jax.random.split(key, 6)
        bsz, n_lat, seq, hidden = (8, 64, 512, 512)
        return {'latents': jax.random.normal(ks[0], (bsz, n_lat, hidden), jnp.float32), 'context': jax.random.normal(ks[1], (bsz, seq, hidden), jnp.float32), 'Wq': jax.random.normal(ks[2], (hidden, HEADS * HEAD_DIM), jnp.float32) * 0.02, 'Wk': jax.random.normal(ks[3], (hidden, KV_HEADS * HEAD_DIM), jnp.float32) * 0.02, 'Wv': jax.random.normal(ks[4], (hidden, KV_HEADS * HEAD_DIM), jnp.float32) * 0.02, 'Wo': jax.random.normal(ks[5], (HEADS * HEAD_DIM, hidden), jnp.float32) * 0.02, 'q_norm_w': jnp.ones((HEAD_DIM,), jnp.float32), 'k_norm_w': jnp.ones((HEAD_DIM,), jnp.float32)}
    _L1_xattn_all = _L1_xattn_setup()
    _L1_xattn_in = {k: v for k, v in _L1_xattn_all.items() if k in ('Wq', 'Wk', 'Wv', 'Wo', 'q_norm_w', 'k_norm_w')}
    del _L1_xattn_all

    def _L1_ffn_setup():
        import jax, jax.numpy as jnp
        import numpy as np
        SCALING = 32.0 / 16.0
        key = jax.random.key(seed)
        ks = jax.random.split(key, 7)
        B, T, D, O, R, E = (4, 256, 512, 512, 16, 8)
        x = jax.random.normal(ks[0], (B, T, D), dtype=jnp.float32)
        base_W = jax.random.normal(ks[1], (O, D), dtype=jnp.float32) * D ** (-0.5)
        base_b = jax.random.normal(ks[2], (O,), dtype=jnp.float32) * 0.01
        router_W = jax.random.normal(ks[3], (2 * E - 1, D), dtype=jnp.float32) * D ** (-0.5)
        router_b = jax.random.normal(ks[4], (2 * E - 1,), dtype=jnp.float32) * 0.01
        A = jax.random.normal(ks[5], (E, R, D), dtype=jnp.float32) * D ** (-0.5)
        Bm = jax.random.normal(ks[6], (E, O, R), dtype=jnp.float32) * R ** (-0.5)
        assigned_idx = 0
        others = [i for i in range(E) if i != assigned_idx]
        expert_map = jnp.array([assigned_idx] * E + others, dtype=jnp.int32)
        return {'x': x, 'base_W': base_W, 'base_b': base_b, 'router_W': router_W, 'router_b': router_b, 'A': A, 'B': Bm, 'expert_map': expert_map}
    _L1_ffn_all = _L1_ffn_setup()
    _L1_ffn_in = {k: v for k, v in _L1_ffn_all.items() if k in ('base_W', 'base_b', 'router_W', 'router_b', 'A', 'B', 'expert_map')}
    del _L1_ffn_all
    return {'x': x, 'ctx_4096': ctx_4096, 'L0_attn_Wq': _L0_attn_in['Wq'], 'L0_attn_bq': _L0_attn_in['bq'], 'L0_attn_Wk': _L0_attn_in['Wk'], 'L0_attn_bk': _L0_attn_in['bk'], 'L0_attn_Wv': _L0_attn_in['Wv'], 'L0_attn_bv': _L0_attn_in['bv'], 'L0_xattn_x1_scale': _L0_xattn_in['x1_scale'], 'L0_xattn_x1_zp': _L0_xattn_in['x1_zp'], 'L0_xattn_x2_scale': _L0_xattn_in['x2_scale'], 'L0_xattn_x2_zp': _L0_xattn_in['x2_zp'], 'L0_ffn_W': _L0_ffn_in['W'], 'L0_ffn_b': _L0_ffn_in['b'], 'L1_attn_w_qkv': _L1_attn_in['w_qkv'], 'L1_attn_b_qkv': _L1_attn_in['b_qkv'], 'L1_attn_w_out': _L1_attn_in['w_out'], 'L1_attn_b_out': _L1_attn_in['b_out'], 'L1_xattn_Wq': _L1_xattn_in['Wq'], 'L1_xattn_Wk': _L1_xattn_in['Wk'], 'L1_xattn_Wv': _L1_xattn_in['Wv'], 'L1_xattn_Wo': _L1_xattn_in['Wo'], 'L1_xattn_q_norm_w': _L1_xattn_in['q_norm_w'], 'L1_xattn_k_norm_w': _L1_xattn_in['k_norm_w'], 'L1_ffn_base_W': _L1_ffn_in['base_W'], 'L1_ffn_base_b': _L1_ffn_in['base_b'], 'L1_ffn_router_W': _L1_ffn_in['router_W'], 'L1_ffn_router_b': _L1_ffn_in['router_b'], 'L1_ffn_A': _L1_ffn_in['A'], 'L1_ffn_B': _L1_ffn_in['B'], 'L1_ffn_expert_map': _L1_ffn_in['expert_map']}

def reference(x, ctx_4096, L0_attn_Wq, L0_attn_bq, L0_attn_Wk, L0_attn_bk, L0_attn_Wv, L0_attn_bv, L0_xattn_x1_scale, L0_xattn_x1_zp, L0_xattn_x2_scale, L0_xattn_x2_zp, L0_ffn_W, L0_ffn_b, L1_attn_w_qkv, L1_attn_b_qkv, L1_attn_w_out, L1_attn_b_out, L1_xattn_Wq, L1_xattn_Wk, L1_xattn_Wv, L1_xattn_Wo, L1_xattn_q_norm_w, L1_xattn_k_norm_w, L1_ffn_base_W, L1_ffn_base_b, L1_ffn_router_W, L1_ffn_router_b, L1_ffn_A, L1_ffn_B, L1_ffn_expert_map):
    import jax
    import jax.numpy as jnp

    def _L0_attn_ref(x, Wq, bq, Wk, bk, Wv, bv):
        import jax, jax.numpy as jnp
        import numpy as np
        N_HEADS = 32
        N_KV_HEADS = 16
        N_EMBD = 512
        HEAD_DIM = N_EMBD // N_HEADS
        GROUPS = N_HEADS // N_KV_HEADS
        KV_DIM = N_KV_HEADS * HEAD_DIM
        SCALE = 1.0 / np.sqrt(np.float32(N_HEADS))
        B, T, C = x.shape
        q = (x @ Wq.T + bq).reshape(B, T, N_HEADS, HEAD_DIM)
        k = (x @ Wk.T + bk).reshape(B, T, N_KV_HEADS, HEAD_DIM)
        v = (x @ Wv.T + bv).reshape(B, T, N_KV_HEADS, HEAD_DIM)
        q = q.transpose(0, 2, 1, 3).reshape(B, GROUPS, N_KV_HEADS, T, HEAD_DIM)
        k = k.transpose(0, 2, 1, 3)
        v = v.transpose(0, 2, 1, 3)
        scores = jnp.einsum('bgkqd,bkld->bgkql', q, k) * SCALE
        causal = jnp.tril(jnp.ones((T, T), dtype=bool))
        scores = jnp.where(causal, scores, jnp.float32(-jnp.inf))
        w = jax.nn.softmax(scores, axis=-1)
        out = jnp.einsum('bgkql,bkld->bgkqd', w, v)
        out = out.reshape(B, N_HEADS, T, HEAD_DIM).transpose(0, 2, 1, 3).reshape(B, T, C)
        return out

    def _L0_xattn_ref(x1, x2, x1_scale, x1_zp, x2_scale, x2_zp):
        import jax, jax.numpy as jnp
        import numpy as np
        QMIN = 0.0
        QMAX = 255.0

        def fake_quant(x, scale, zp):
            s = scale.reshape(())
            z = zp.reshape(())
            q = jnp.clip(jnp.round(x / s + z), QMIN, QMAX)
            return (q - z) * s
        q1 = fake_quant(x1, x1_scale, x1_zp)
        q2 = fake_quant(x2, x2_scale, x2_zp)
        return jnp.matmul(q1, q2)

    def _L0_ffn_ref(x, W, b):
        import jax, jax.numpy as jnp
        import numpy as np
        EPS = 1e-05

        def rms_norm(x):
            return x * jax.lax.rsqrt(jnp.mean(x * x, axis=-1, keepdims=True) + EPS)

        def activation_quant(x):
            scale = 127.0 / jnp.clip(jnp.max(jnp.abs(x), axis=-1, keepdims=True), EPS, None)
            return jnp.clip(jnp.round(x * scale), -128.0, 127.0) / scale

        def weight_quant(w):
            scale = 1.0 / jnp.clip(jnp.mean(jnp.abs(w)), EPS, None)
            return jnp.clip(jnp.round(w * scale), -1.0, 1.0) / scale
        xn = rms_norm(x)
        xq = xn + jax.lax.stop_gradient(activation_quant(xn) - xn)
        wq = W + jax.lax.stop_gradient(weight_quant(W) - W)
        y = jnp.einsum('bsd,od->bso', xq, wq) + b
        return x + jax.nn.gelu(y, approximate=False)

    def _L1_attn_ref(x, w_qkv, b_qkv, w_out, b_out):
        import math
        import jax, jax.numpy as jnp
        import numpy as np
        N_HEADS = 32
        ALIBI_BIAS_MAX = 8

        def _alibi_slopes(n_heads, alibi_bias_max=8):
            _n = 2 ** math.ceil(math.log2(n_heads))
            m = jnp.arange(1, _n + 1, dtype=jnp.float32) * (alibi_bias_max / _n)
            slopes = 1.0 / jnp.power(2.0, m)
            if _n != n_heads:
                slopes = jnp.concatenate([slopes[1::2], slopes[::2]])[:n_heads]
            return slopes
        B, S, D = x.shape
        H = N_HEADS
        hd = D // H
        qkv = jnp.einsum('bsd,od->bso', x, w_qkv) + b_qkv
        q, k, v = jnp.split(qkv, 3, axis=-1)
        q = q.reshape(B, S, H, hd)
        k = k.reshape(B, S, H, hd)
        v = v.reshape(B, S, H, hd)
        scale = 1.0 / math.sqrt(hd)
        scores = jnp.einsum('bqhd,bkhd->bhqk', q, k) * scale
        slopes = _alibi_slopes(H, ALIBI_BIAS_MAX)
        positions = jnp.arange(1 - S, 1, dtype=jnp.float32)
        alibi = slopes[:, None] * positions[None, :]
        scores = scores + alibi[None, :, None, :]
        causal = jnp.arange(S)[:, None] >= jnp.arange(S)[None, :]
        scores = jnp.where(causal[None, None, :, :], scores, jnp.float32(-1000000000.0))
        attn = jax.nn.softmax(scores, axis=-1)
        out = jnp.einsum('bhqk,bkhd->bqhd', attn, v).reshape(B, S, D)
        return jnp.einsum('bsd,od->bso', out, w_out) + b_out

    def _L1_xattn_ref(latents, context, Wq, Wk, Wv, Wo, q_norm_w, k_norm_w):
        import jax, jax.numpy as jnp
        import numpy as np
        HEADS = 32
        KV_HEADS = 8
        HEAD_DIM = 128
        EPS = 1e-06

        def rms_norm(x, w):
            var = jnp.mean(jnp.square(x.astype(jnp.float32)), axis=-1, keepdims=True)
            return (x.astype(jnp.float32) * jax.lax.rsqrt(var + EPS)).astype(x.dtype) * w
        bsz, q_len, hidden = latents.shape
        kv = jnp.concatenate([context, latents], axis=1)
        kv_len = kv.shape[1]
        groups = HEADS // KV_HEADS
        q = (latents @ Wq).reshape(bsz, q_len, HEADS, HEAD_DIM).transpose(0, 2, 1, 3)
        k = (kv @ Wk).reshape(bsz, kv_len, KV_HEADS, HEAD_DIM).transpose(0, 2, 1, 3)
        v = (kv @ Wv).reshape(bsz, kv_len, KV_HEADS, HEAD_DIM).transpose(0, 2, 1, 3)
        q = rms_norm(q, q_norm_w)
        k = rms_norm(k, k_norm_w)
        qg = q.reshape(bsz, KV_HEADS, groups, q_len, HEAD_DIM)
        scale = 1.0 / np.sqrt(HEAD_DIM)
        scores = jnp.einsum('bhgqd,bhkd->bhgqk', qg, k) * scale
        probs = jax.nn.softmax(scores.astype(jnp.float32), axis=-1).astype(q.dtype)
        out = jnp.einsum('bhgqk,bhkd->bhgqd', probs, v)
        out = out.reshape(bsz, HEADS, q_len, HEAD_DIM).transpose(0, 2, 1, 3)
        out = out.reshape(bsz, q_len, HEADS * HEAD_DIM)
        return out @ Wo

    def _L1_ffn_ref(x, base_W, base_b, router_W, router_b, A, B, expert_map):
        import jax, jax.numpy as jnp
        import numpy as np
        SCALING = 32.0 / 16.0
        E = A.shape[0]
        base_out = jnp.einsum('btd,od->bto', x, base_W) + base_b
        logits = jnp.einsum('btd,nd->btn', x, router_W) + router_b
        probs = jax.nn.softmax(logits, axis=-1)
        topk_p, topk_i = jax.lax.top_k(probs, E)
        mapped = expert_map[topk_i]
        onehot = (mapped[..., None] == jnp.arange(E)).astype(x.dtype)
        w = jnp.einsum('btk,btke->bte', topk_p, onehot)
        h = jnp.einsum('btd,erd->bter', x, A)
        lora = jnp.einsum('bter,eor->bto', h * w[..., None], B) * SCALING
        return base_out + lora
    x = x + _L0_attn_ref(_layernorm(x, axis=-1), L0_attn_Wq, L0_attn_bq, L0_attn_Wk, L0_attn_bk, L0_attn_Wv, L0_attn_bv)
    x = x + _L0_xattn_ref(_layernorm(x, axis=-1), ctx_4096, L0_xattn_x1_scale, L0_xattn_x1_zp, L0_xattn_x2_scale, L0_xattn_x2_zp)
    x = x + _L0_ffn_ref(_layernorm(x, axis=-1), L0_ffn_W, L0_ffn_b)
    x = x + _L1_attn_ref(_layernorm(x, axis=-1), L1_attn_w_qkv, L1_attn_b_qkv, L1_attn_w_out, L1_attn_b_out)
    x = x + _L1_xattn_ref(_layernorm(x, axis=-1), ctx_4096, L1_xattn_Wq, L1_xattn_Wk, L1_xattn_Wv, L1_xattn_Wo, L1_xattn_q_norm_w, L1_xattn_k_norm_w)
    x = x + _L1_ffn_ref(_layernorm(x, axis=-1), L1_ffn_base_W, L1_ffn_base_b, L1_ffn_router_W, L1_ffn_router_b, L1_ffn_A, L1_ffn_B, L1_ffn_expert_map)
    return x

_drawn_inputs = setup_inputs


def setup_inputs(seed=0):
    import zlib

    import numpy as np

    out = dict(_drawn_inputs(seed))
    spreads = {'L0_attn_bq': (0.0, 0.453),
     'L0_attn_bk': (0.0, 2.0),
     'L0_attn_bv': (0.0, 0.1),
     'L1_attn_b_qkv': (0.0, 0.8),
     'L1_attn_b_out': (0.0, 0.8),
     'L1_xattn_q_norm_w': (1.0, 0.6),
     'L1_xattn_k_norm_w': (1.0, 0.6)}
    factors = {'L0_ffn_W': 3.097,
     'L0_ffn_b': 40.11,
     'L1_attn_w_qkv': 8.0,
     'L1_attn_w_out': 8.0,
     'L1_xattn_Wq': 8.0,
     'L1_xattn_Wk': 8.0,
     'L1_xattn_Wv': 5.268,
     'L1_xattn_Wo': 5.315,
     'L1_ffn_base_b': 64.0,
     'L1_ffn_router_b': 200.0,
     'L1_ffn_router_W': 2.902}
    for name, (base, spread) in spreads.items():
        noise = np.random.default_rng([zlib.crc32(name.encode()), seed]).standard_normal(out[name].shape)
        drawn = base * np.exp(spread * noise) if base else spread * noise
        out[name] = jnp.asarray(drawn.astype(out[name].dtype))
    for name, factor in factors.items():
        out[name] = (out[name] * factor).astype(out[name].dtype)
    return out
```

```python
from contextlib import ExitStack

import numpy as np

import concourse.bass as bass
from concourse import mybir

F32 = mybir.dt.float32
BF16 = mybir.dt.bfloat16
I32 = mybir.dt.int32
ALU = mybir.AluOpType
ACT = mybir.ActivationFunctionType
AX = mybir.AxisListType

P = 128
D = 512
NB = 2
SEQ = 256
T = NB * SEQ // P
C = D // P
CTX = 512
CT = NB * CTX // P
HD = 16
HG = P // HD
LN_EPS = 1e-5
ROUND = 12582912.0
NEG = -1.0e30

XD = 128
KVH = 8
GQ = 4
KT_N = (CTX + SEQ) // P
KEYS = KT_N * P

NE = 8
RANK = 16
ROUTES = 2 * NE - 1


def decoder_program(
    nc, x, ctx_4096, a0_wq, a0_bq, a0_wk, a0_bk, a0_wv, a0_bv, m0_s1, m0_z1, m0_s2, m0_z2, f0_w, f0_b,
    a1_wqkv, a1_bqkv, a1_wout, a1_bout, x1_wq, x1_wk, x1_wv, x1_wo, x1_qn, x1_kn,
    f1_w, f1_b, f1_rw, f1_rb, f1_a, f1_bm, f1_map, out,
):
    ctx = ExitStack()

    def sb(name, shape, dt=F32):
        return ctx.enter_context(nc.sbuf_tensor(name, shape, dt))

    def sem(name):
        return ctx.enter_context(nc.semaphore(name))

    with ctx:
        X = sb("X", [P, T, D])
        XN = sb("XN", [P, T, D])
        XT = sb("XT", [P, C, T * P])
        CX = sb("CX", [P, CT, D])
        CXT = sb("CXT", [P, C, CT * P])

        shared = sb("shared", [P, 2 * GQ * KEYS * 2])

        def shared_f32(at, n, **kw):
            return shared[:, at:at + n].rearrange("p (a b) -> p a b", **kw)

        def shared_bf16(at, n, **kw):
            return shared[:, at:at + n // 2].bitcast(BF16).rearrange("p (a b) -> p a b", **kw)

        TMP = shared_f32(0, T * D, a=T)
        G = shared_f32(2048, T * D, a=T)
        FW = shared_f32(4096, C * D, a=C)
        CXQ = shared_bf16(6144, CT * D, a=CT)
        XQ = shared_bf16(8192, T * D, a=T)
        XQT = shared_bf16(9216, C * T * P, a=C)
        WQT = shared_bf16(10240, C * D, a=C)
        WQN = shared_bf16(11264, C * D, a=C)
        PX = shared[:, 0:6144].rearrange("p (s h k) -> p s h k", s=2, h=GQ)
        PXT = shared[:, 6144:12288].rearrange("p (s k q) -> p s k q", s=2, k=KT_N)

        ident = sb("ident", [P, P])
        identb = sb("identb", [P, P], BF16)
        ones = sb("ones", [P, P])
        onesb = sb("onesb", [P, 1], BF16)
        causal = sb("causal", [P, 2 * P])
        neghalf = sb("neghalf", [P, 32])
        pidx = sb("pidx", [P, 1], I32)
        podd = sb("podd", [P, 1], I32)
        evenodd = sb("evenodd", [P, 2])

        lnst = sb("lnst", [P, T, 6])
        lnmv = sb("lnmv", [P, T, 2])
        lnve = sb("lnve", [P, T])
        lnrs = sb("lnrs", [P, T])

        W0 = sb("W0", [P, 4, D])
        WT = sb("WT", [P, 4, C, P])
        WO = sb("WO", [P, C, P])
        WOT = sb("WOT", [P, D])
        bqk = sb("bqk", [P, 3])
        bvr = sb("bvr", [P, P])
        KQ = sb("KQ", [P, 4 * T * P])
        KM = KQ[:, 0:2 * T * P].rearrange("p (e t) -> p e t", e=2)
        QT = KQ[:, 2 * T * P:].rearrange("p (a t) -> p a t", a=2)
        VN = sb("VN", [P, T, P])
        NS = 4
        units = sb("units", [P, 3 * NS * 2 * P])

        def units_at(n):
            return units[:, n * NS * 2 * P:(n + 1) * NS * 2 * P].rearrange("p (n k) -> p n k", n=NS)

        SS = units_at(0)
        nmax = sb("nmax", [P, NS])
        PR = units_at(1)
        PRT = units_at(2)
        rsum = sb("rsum", [P, 2, HG])
        rinv = sb("rinv", [P, 2, HG])
        osc = sb("osc", [P, P])
        AT = sb("AT", [P, T, P])
        ATT = sb("ATT", [P, T * P])
        ALB = sb("ALB", [P, HG, 2 * P])
        posr = sb("posr", [P, 2 * P])

        qs = sb("qs", [P, 4])
        qsr = sb("qsr", [P, 2])
        qc = sb("qc", [P, 4])
        colr = sb("colr", [1, NB, D])
        rowc = sb("rowc", [P, T])
        fb = sb("fb", [P, D])
        boutb = sb("boutb", [P, D])
        wab = sb("wab", [P, 1])
        wsc = sb("wsc", [P, 2])
        msq0 = sb("msq0", [P, T])
        msq = sb("msq", [P, T])
        mab = sb("mab", [P, T])
        rrs = sb("rrs", [P, T])
        amx = sb("amx", [P, T])
        ascl = sb("ascl", [P, T])
        adq = sb("adq", [P, T])

        WKV = sb("WKV", [P, C, 2 * XD])
        WQ1 = W0
        WO1 = sb("WO1", [P, GQ, D])
        KVN = units[:].rearrange("p (k d) -> p k d", k=NB * KT_N)
        QN = XN
        KTX = KQ[:, 0:NB * KEYS]
        QTX = ALB[:].rearrange("p h k -> p (h k)").rearrange("p (h t) -> p h t", h=GQ)
        OT = sb("OT", [P, GQ * P])
        SQJ = sb("SQJ", [P, 2, P])
        ssx = sb("ssx", [P, 32])
        rx = sb("rx", [P, 32])
        cq = sb("cq", [P, 2, T * GQ])
        wn = sb("wn", [P, 2])
        wqk = sb("wqk", [P, 1])
        xmx = sb("xmx", [P, T * GQ])
        xnb = sb("xnb", [P, T * GQ])
        xsum = sb("xsum", [P, T * GQ])
        xri = sb("xri", [P, T * GQ])

        RW = sb("RW", [ROUTES, D])
        AW = sb("AW", [P, D])
        BW = sb("BW", [P, C, NE, RANK])
        F1T = WT[:].rearrange("p m c f -> p m (c f)")
        RT = sb("RT", [P, C, P + 16])
        BT = units[:, 0:D]
        f1b = sb("f1b", [P, D])
        rbb = sb("rbb", [P, ROUTES])
        mapi = sb("mapi", [ROUTES, 1], I32)
        mapf = sb("mapf", [ROUTES, 1])
        expi = sb("expi", [ROUTES, NE, RANK])
        oexp = sb("oexp", [ROUTES, NE * RANK])
        lg = sb("lg", [P, T, ROUTES])
        lmx = sb("lmx", [P, T])
        lsum = sb("lsum", [P, T])
        pr = sb("pr", [P, T, 16])
        top8 = sb("top8", [P, T, 8])
        rep = sb("rep", [P, T, 16])
        selp = sb("selp", [P, T, 16])
        selT = sb("selT", [ROUTES, T * P])
        wexp = units[:, D:D + T * P]
        hT = units[:, 2 * D:2 * D + T * P]

        pair = [ctx.enter_context(nc.psum_tensor(f"pair{i}", [P, 1024], F32)) for i in range(2)]
        S = [pair[0][:, 0:512], pair[0][:, 512:1024], pair[1][:, 0:512], pair[1][:, 512:1024]]
        TB = [ctx.enter_context(nc.psum_tensor(f"turn{i}", [P, 512], F32)) for i in range(2)]
        Sb, TBb = [s.bitcast(BF16) for s in S], [b[:].bitcast(BF16) for b in TB]
        OB = [ctx.enter_context(nc.psum_tensor(f"acc{i}", [P, 512], F32)) for i in range(2)]

        x_in, ctx_in, fw_in, out_done = sem("x_in"), sem("ctx_in"), sem("fw_in"), sem("out_done")
        consts = sem("consts")
        NCONST = 8
        zeroed, identb_done, qs_ready = sem("zeroed"), sem("identb_done"), sem("qscales_ready")
        ln_stat, ln_aggr, ln_var, ln_rstd, ln_norm = (sem(f"ln_{n}") for n in ("stat", "aggr", "var", "rstd", "norm"))
        ln_turned, xt_act, xt_dve = sem("ln_turned"), sem("xt_act"), sem("xt_dve")
        dve_step = sem("dve_step")
        ctx_turned, cxt_ready = sem("ctx_turned"), sem("cxt_ready")


        class Steps:

            def __init__(self, eng, s, base=0):
                self.eng, self.s, self.base, self.n = eng, s, base, 0

            def __call__(self, ins):
                self.n += 1
                ins.then_inc(self.s, 1)
                self.eng.wait_ge(self.s, self.base + self.n)

        def self_units(na):
            return [(a, b, qt, j) for a in range(na) for b in range(NB) for qt in range(2) for j in range(HG)]

        LAG_T, LAG_V = 2, 3

        class SelfSems:

            def __init__(self, n):
                self.w_in = sem(f"{n}_w_in")
                self.b_in = sem(f"{n}_b_in")
                self.w_turned = sem(f"{n}_w_turned")
                self.wt_act = sem(f"{n}_wt_act")
                self.wt_dve = sem(f"{n}_wt_dve")
                self.proj = sem(f"{n}_proj")
                self.qkv = sem(f"{n}_qkv")
                self.scores = sem(f"{n}_scores")
                self.masked = sem(f"{n}_masked")
                self.exps = sem(f"{n}_exps")
                self.p_turned = sem(f"{n}_p_turned")
                self.pt = sem(f"{n}_pt")
                self.pv = sem(f"{n}_pv")
                self.o = sem(f"{n}_o")
                self.steps = sem(f"{n}_steps")
                self.first = sem(f"{n}_first")

        a0 = SelfSems("a0")
        a1 = SelfSems("a1")
        a1_albi, a1_turned, a1_att, a1_y, a1_yadd = (sem(f"a1_{n}") for n in ("alibi", "att_turned", "att", "y", "yadd"))
        a1_wot_turned, a1_wot, a1_wo_in, a1_badd = (sem(f"a1_{n}") for n in ("wot_turned", "wot", "wo_in", "b_out"))

        def self_pe(pe, i, s, na):
            U = self_units(na)
            n, G = len(U), len(U) // HG
            for st in range(n + LAG_V):
                if st < n:
                    a, b, qt, j = U[st]
                    if st >= NS:
                        pe.wait_ge(s.masked, i * n + st - NS + 1)
                    r = 32 * (j // 2)
                    q0 = b * SEQ + qt * P
                    nc.tensor.matmul(S[st % NS][:, 0:P * (qt + 1)], QT[r:r + 32, a, q0:q0 + P],
                                     KM[r:r + 32, j % 2, b * SEQ:b * SEQ + P * (qt + 1)],
                                     start=True, stop=True).then_inc(s.scores, 1)
                u = st - LAG_T
                if 0 <= u < n:
                    qt = U[u][2]
                    pe.wait_ge(s.exps, i * n + u + 1)
                    if u >= 2:
                        pe.wait_ge(s.pt, i * n + u - 1)
                    for k in range(qt + 1):
                        mm = nc.tensor.transpose(TB[u % 2][:, k * P:(k + 1) * P], PR[:, u % NS, k * P:(k + 1) * P],
                                                 ident[:])
                    mm.then_inc(s.p_turned, 1)
                u = st - LAG_V
                if 0 <= u < n:
                    a, b, qt, j = U[u]
                    g = u // HG
                    if j == 0 and g >= 2:
                        pe.wait_ge(s.o, i * G + g)
                    pe.wait_ge(s.pt, i * n + u + 1)
                    for k in range(qt + 1):
                        mm = nc.tensor.matmul(OB[g % 2][:, j * HD:(j + 1) * HD], PRT[:, u % NS, k * P:(k + 1) * P],
                                              VN[:, 2 * b + k, j * HD:(j + 1) * HD], start=(k == 0), stop=(k == qt))
                    mm.then_inc(s.pv, 1)

        def self_act(act, i, s, na):
            U = self_units(na)
            n, G = len(U), len(U) // HG
            for u, (a, b, qt, j) in enumerate(U):
                w = P * (qt + 1)
                act.wait_ge(s.masked, i * n + u + 1)
                if u >= NS:
                    act.wait_ge(s.p_turned, i * n + u - NS + 1)
                if j == 0 and u // HG >= 2:
                    act.wait_ge(s.o, i * G + u // HG)
                nc.scalar.activation(PR[:, u % NS, 0:w], SS[:, u % NS, 0:w], ACT.Exp, bias=nmax[:, u % NS:u % NS + 1],
                                     scale=-1.0, accum_out=rsum[:, (u // HG) % 2, j:j + 1]).then_inc(s.exps, 1)

        def self_dve(dve, i, s, na, bias_of, finish):
            U = self_units(na)
            n, G = len(U), len(U) // HG
            per = 2 if s is a0 else 1
            steps = Steps(dve, s.steps, i * G * per)
            dsteps = Steps(dve, s.first, i * LAG_T)
            for st in range(n + LAG_V):
                u = st - LAG_T
                if st < n:
                    dve.wait_ge(s.scores, i * n + st + 1)
                    if st >= NS:
                        dve.wait_ge(s.exps, i * n + st - NS + 1)
                if 0 <= u < n:
                    w = P * (U[u][2] + 1)
                    dve.wait_ge(s.p_turned, i * n + u + 1)
                    if u >= NS:
                        dve.wait_ge(s.pv, i * n + u - NS + 1)
                    nc.vector.tensor_copy(PRT[:, u % NS, 0:w], TB[u % 2][:, 0:w]).then_inc(s.pt, 1)
                if st < n:
                    a, b, qt, j = U[st]
                    w = P * (qt + 1)
                    bias, ns = bias_of(j)[:, 2 * P - w:2 * P], nmax[:, st % NS:st % NS + 1]
                    if st < LAG_T:
                        dsteps(nc.vector.scalar_tensor_tensor(out=SS[:, st % NS, 0:w], in0=S[st % NS][:, 0:w],
                                                              scalar=-1.0, in1=bias, op0=ALU.mult, op1=ALU.subtract))
                        nc.vector.tensor_reduce(ns, SS[:, st % NS, 0:w], AX.X, ALU.min).then_inc(s.masked, 1)
                    else:
                        nc.vector.tensor_tensor_reduce(
                            out=SS[:, st % NS, 0:w], in0=S[st % NS][:, 0:w], in1=bias, scale=-1.0, scalar=3.0e38,
                            op0=ALU.add, op1=ALU.min, accum_out=ns).then_inc(s.masked, 1)
                u = st - LAG_V
                if 0 <= u < n and U[u][3] == HG - 1:
                    a, b, qt, j = U[u]
                    g = u // HG
                    dve.wait_ge(s.pv, i * n + u + 1)
                    steps(nc.vector.reciprocal(rinv[:, g % 2, :], rsum[:, g % 2, :]))
                    finish(i, a, 2 * b + qt, i * G + g, steps,
                           OB[g % 2][:, 0:P].rearrange("p (h d) -> p h d", h=HG),
                           rinv[:, g % 2, :].unsqueeze(2).to_broadcast([P, HG, HD])).then_inc(s.o, 1)

        def turn_weights(pe, i, s, nw):
            pe.wait_ge(s.w_in, i * 16 * nw + 16 * nw)
            for m in range(nw):
                if m >= 2:
                    pe.wait_ge(s.wt_act if m % 2 == 0 else s.wt_dve, i * (nw - nw // 2 if m % 2 == 0 else nw // 2) + m // 2)
                for c in range(C):
                    mm = nc.tensor.transpose(TB[m % 2][:, c * P:(c + 1) * P], W0[:, m, c * P:(c + 1) * P], ident[:])
                mm.then_inc(s.w_turned, 1)

        def project_qkv(pe, i, s, nw):
            pe.wait_ge(s.wt_act, i * (nw - nw // 2) + (nw - nw // 2))
            pe.wait_ge(s.wt_dve, i * (nw // 2) + nw // 2)
            for n, m in enumerate([0] + list(range(2, nw))):
                for c in range(C):
                    mm = nc.tensor.matmul(S[n], WT[:, m, c, :], XT[:, c, :], start=(c == 0), stop=(c == C - 1))
                mm.then_inc(s.proj, 1)
            for t in range(T):
                for c in range(C):
                    mm = nc.tensor.matmul(S[3][:, t * P:(t + 1) * P], XT[:, c, t * P:(t + 1) * P], WT[:, 1, c, :],
                                          start=(c == 0), stop=(c == C - 1))
            mm.then_inc(s.proj, 1)

        def qkv_dve(dve, i, s, nw, scale):
            dve.wait_ge(s.b_in, i * 16 * nw + 16 * nw)
            dve.wait_ge(s.proj, i * nw + 1)
            for e in range(2):
                nc.vector.tensor_scalar(KM[:, e, :], S[0], bqk[:, 0:1], evenodd[:, e:e + 1], ALU.add,
                                        ALU.mult).then_inc(s.qkv, 1)
            for m in range(nw - 2):
                dve.wait_ge(s.proj, i * nw + 2 + m)
                nc.vector.tensor_scalar(QT[:, m, :], S[1 + m], bqk[:, 1 + m:2 + m], scale, ALU.add,
                                        ALU.mult).then_inc(s.qkv, 1)
            dve.wait_ge(s.proj, i * nw + nw)
            nc.vector.tensor_tensor(VN[:], S[3].rearrange("p (t f) -> p t f", t=T),
                                    bvr[:].unsqueeze(1).to_broadcast([P, T, P]), ALU.add).then_inc(s.qkv, 1)

        m0_norm, m0_turned, m0_xqt = sem("m0_quantised"), sem("m0_turned"), sem("m0_xqt")
        m0_col, m0_colr, m0_prod = sem("m0_colsum"), sem("m0_colrow"), sem("m0_product")
        f0_wabs, f0_wtot, f0_wscale, f0_wq, f0_wturned, f0_wqt = (
            sem(f"f0_{n}") for n in ("wabs", "wtotal", "wscale", "wquant", "wturned", "wqt"))
        f0_ms, f0_rms, f0_q, f0_turned, f0_xqt, f0_prod, f0_y, f0_gelu, f0_sq = (
            sem(f"f0_{n}") for n in ("meansq", "rms", "quantised", "turned", "xqt", "product", "y", "gelu", "squares"))
        xw_kv, xw_q, xw_o = sem("x1_wkv_in"), sem("x1_wq_in"), sem("x1_wo_in")
        x_proj, x_nat, x_ms, x_r, x_kn, x_turned, x_tr = (
            sem(f"x1_{n}") for n in ("proj", "natural", "meansq", "rms", "k_normed", "qk_turned", "qkt"))
        x_sc, x_nb, x_exp, x_p, x_pt, x_pta, x_ptv, x_pv, x_ot, x_y, x_ya, x_steps = (
            sem(f"x1_{n}") for n in ("scores", "neg_bias", "exps", "probs", "p_turned", "pt_act", "pt_dve",
                                     "pv", "ot", "y", "yadd", "steps"))
        x_wqk = sem("x1_wqk")
        g_in, g_turned, g_wt, g_h, g_hT, g_lg, g_lgd, g_exp, g_sel, g_selturned, g_selT, g_w, g_wexp, g_y, g_oexp = (
            sem(f"f1_{n}") for n in ("in", "turned", "wt", "h", "hT", "logits", "logits_max", "exps", "sel",
                                     "sel_turned", "selT", "w", "wexp", "y", "oexp"))
        ctx_q = sem("ctx_quantised")
        m0_q1, m0_q2, m0_y, f0_q1, f0_q2, f0_mab, f0_x1 = (
            sem(n) for n in ("m0_scaled", "m0_clipped", "m0_added", "f0_scaled", "f0_clipped", "f0_maxabs", "f0_added"))
        x_sq, x_ri, f1_bdone, g_out = sem("x1_squares"), sem("x1_rsum_inv"), sem("f1_bias_added"), sem("f1_out")

        block = ctx.enter_context(nc.Block())


        def ln_dve(dve, n):
            for t in range(T):
                nc.vector.bn_stats(lnst[:, t, :], X[:, t, :]).then_inc(ln_stat, 1)
            for t in range(T):
                dve.wait_ge(ln_stat, n * T + t + 1)
                nc.vector.bn_aggr(lnmv[:, t, :], lnst[:, t, :]).then_inc(ln_aggr, 1)
            dve.wait_ge(ln_aggr, n * T + T)
            nc.vector.tensor_scalar(lnve[:], lnmv[:, :, 1], LN_EPS, None, ALU.add).then_inc(ln_var, 1)
            dve.wait_ge(ln_rstd, n + 1)
            for t in range(T):
                nc.vector.tensor_scalar(XN[:, t, :], X[:, t, :], lnmv[:, t, 0:1], lnrs[:, t:t + 1], ALU.subtract,
                                        ALU.mult).then_inc(ln_norm, 1)

        def ln_pool(pool, n):
            pool.wait_ge(ln_var, n + 1)
            nc.gpsimd.tensor_tensor(lnrs[:], lnve[:], neghalf[:, 0:T], ALU.pow).then_inc(ln_rstd, 1)

        def ln_pe(pe, n, k):
            pe.wait_ge(ln_norm, n * T + T)
            for c in range(C):
                for t in range(T):
                    mm = nc.tensor.transpose(S[c][:, t * P:(t + 1) * P], XN[:, t, c * P:(c + 1) * P], ident[:])
                mm.then_inc(ln_turned, 1)

        def ln_act(act, k):
            for c in (0, 2):
                act.wait_ge(ln_turned, k * C + c + 1)
                nc.scalar.copy(XT[:, c, :], S[c]).then_inc(xt_act, 1)

        def ln_copy_dve(dve, k):
            for c in (1, 3):
                dve.wait_ge(ln_turned, k * C + c + 1)
                nc.vector.tensor_copy(XT[:, c, :], S[c]).then_inc(xt_dve, 1)

        def xt_ready(pe, k):
            pe.wait_ge(xt_act, 2 * k + 2)
            pe.wait_ge(xt_dve, 2 * k + 2)

        m0_in, f0_bin, a1_boutin, x1_nin, f1_bin = (sem(f"{n}_in") for n in ("m0s", "f0b", "a1bout", "x1norm", "f1b"))

        @block.sync
        def _(sp):
            sp.dma_start(X[:], x.rearrange("b (t p) d -> p (b t) d", p=P)).then_inc(x_in, 16)

            with sp.Fori(0, 2) as i:
                sp.wait_ge(a0.w_turned, i * 4 + 1)
                wq = a0_wq.rearrange("(a i p) d -> a i p d", p=P, i=2)
                sp.dma_start(W0[:, 0, :], a0_wk.rearrange("(i p) d -> i p d", p=P)[i]).then_inc(a0.w_in, 16)
                sp.dma_start(W0[:, 1, :], a0_wv.rearrange("(i p) d -> i p d", p=P)[i]).then_inc(a0.w_in, 16)
                for a in range(2):
                    sp.dma_start(W0[:, 2 + a, :], wq[a][i]).then_inc(a0.w_in, 16)
                sp.wait_ge(a0.qkv, i * 5 + 1)
                bq = a0_bq.rearrange("(a i p o) -> a i p o", p=P, i=2, o=1)
                sp.dma_start(bqk[:, 0:1], a0_bk.rearrange("(i p o) -> i p o", p=P, o=1)[i]).then_inc(a0.b_in, 16)
                for a in range(2):
                    sp.dma_start(bqk[:, 1 + a:2 + a], bq[a][i]).then_inc(a0.b_in, 16)
                sp.dma_start(bvr[:], a0_bv.rearrange("(i p) -> i p", p=P)[i].partition_broadcast(P)
                             ).then_inc(a0.b_in, 16)

            with sp.Fori(0, C) as i:
                sp.wait_ge(a0.w_turned, 9)
                sp.wait_ge(a1.w_turned, i * 3 + 1)
                w = a1_wqkv.rearrange("(m i p) d -> m i p d", m=3, p=P)
                bb = a1_bqkv.rearrange("(m i p o) -> m i p o", m=3, p=P, o=1)
                for m, src in enumerate((1, 2, 0)):
                    sp.dma_start(W0[:, m, :], w[src][i]).then_inc(a1.w_in, 16)
                sp.wait_ge(a1_wot_turned, i + 1)
                sp.dma_start(WO[:], a1_wout.rearrange("(c p) (i f) -> i p c f", p=P, f=P)[i]).then_inc(a1_wo_in, 16)
                sp.wait_ge(a0.qkv, 11)
                sp.wait_ge(a1.qkv, i * 4 + 1)
                sp.dma_start(bqk[:, 0:1], bb[1][i]).then_inc(a1.b_in, 16)
                sp.dma_start(bqk[:, 1:2], bb[0][i]).then_inc(a1.b_in, 16)
                sp.dma_start(bvr[:], a1_bqkv.rearrange("(m i p) -> m i p", m=3, p=P)[2][i].partition_broadcast(P)
                             ).then_inc(a1.b_in, 16)

            sp.wait_ge(ctx_turned, CT)
            sp.wait_ge(ctx_q, 3)
            sp.dma_start(CX[:, 0:C, :], f1_w.rearrange("(c p) d -> p c d", p=P)).then_inc(g_in, 16)
            sp.dma_start(AW[:], f1_a.rearrange("e r d -> (e r) d")).then_inc(g_in, 16)
            sp.dma_start(RW[:], f1_rw).then_inc(g_in, 16)
            for c in range(C):
                sp.dma_start(BW[:, c], f1_bm.rearrange("e (c p) r -> c p e r", p=P)[c]).then_inc(g_in, 16)

            sp.wait_ge(a1.w_turned, 13)
            with sp.Fori(0, KVH) as i:
                sp.wait_ge(x_proj, i * 10 + 1)
                kvw = WKV[:].rearrange("p c (m d) -> p m c d", m=2)
                sp.dma_start(kvw[:, 0], x1_wk.rearrange("(c p) (i d) -> i p c d", p=P, d=XD)[i]).then_inc(xw_kv, 16)
                sp.dma_start(kvw[:, 1], x1_wv.rearrange("(c p) (i d) -> i p c d", p=P, d=XD)[i]).then_inc(xw_kv, 16)
                sp.dma_start(WQ1[:], x1_wq.rearrange("(c p) (i d) -> i p c d", p=P, d=GQ * XD)[i]).then_inc(xw_q, 16)
                sp.wait_ge(x_y, i * T + 1)
                sp.dma_start(WO1[:], x1_wo.rearrange("(i h p) d -> i p h d", h=GQ, p=XD)[i]).then_inc(xw_o, 16)
            for t in range(T):
                sp.wait_ge(g_out, t + 1)
                sp.dma_start(out.rearrange("b (t p) d -> p (b t) d", p=P)[:, t], X[:, t, :]).then_inc(out_done, 16)
            sp.wait_ge(out_done, 16 * T)

        @block.gpsimd
        def _(pool):
            pool.dma_start(CX[:], ctx_4096.rearrange("b (k p) d -> p (b k) d", p=P)).then_inc(ctx_in, 16)
            for n, a in enumerate((m0_s1, m0_z1, m0_s2, m0_z2)):
                pool.dma_start(qs[:, n:n + 1], a.partition_broadcast(P)).then_inc(m0_in, 16)
            pool.dma_start(FW[:], f0_w.rearrange("(c p) d -> p c d", p=P)).then_inc(fw_in, 16)
            pool.dma_start(fb[:], f0_b.partition_broadcast(P)).then_inc(f0_bin, 16)
            pool.dma_start(boutb[:], a1_bout.partition_broadcast(P)).then_inc(a1_boutin, 16)
            pool.dma_start(wn[:, 0:1], x1_qn.rearrange("(p o) -> p o", o=1)).then_inc(x1_nin, 16)
            pool.dma_start(wn[:, 1:2], x1_kn.rearrange("(p o) -> p o", o=1)).then_inc(x1_nin, 16)
            pool.dma_start(f1b[:], f1_b.partition_broadcast(P)).then_inc(f1_bin, 16)
            pool.dma_start(rbb[:], f1_rb.partition_broadcast(P)).then_inc(f1_bin, 16)
            pool.dma_start(mapi[:], f1_map.rearrange("(p o) -> p o", o=1)).then_inc(f1_bin, 16)

            nc.gpsimd.memset(ident[:], 0.0).then_inc(zeroed, 1)
            nc.gpsimd.memset(causal[:], 0.0).then_inc(zeroed, 1)
            nc.gpsimd.memset(neghalf[:], -0.5).then_inc(consts, 1)
            nc.gpsimd.memset(ones[:], 1.0).then_inc(consts, 1)
            nc.gpsimd.memset(onesb[:], 1.0).then_inc(consts, 1)
            nc.gpsimd.iota(pidx[:], [[0, 1]], base=0, channel_multiplier=1).then_inc(consts, 1)
            nc.gpsimd.iota(posr[:], [[1, 2 * P]], base=1 - SEQ, channel_multiplier=0,
                           allow_small_or_imprecise_dtypes=True).then_inc(consts, 1)
            nc.gpsimd.iota(expi[:], [[1, NE], [0, RANK]], base=0, channel_multiplier=0,
                           allow_small_or_imprecise_dtypes=True).then_inc(consts, 1)
            pool.wait_ge(zeroed, 2)
            nc.gpsimd.affine_select(out=ident[:], in_=ident[:], compare_op=ALU.not_equal, fill=1.0, base=0,
                                    pattern=[[-1, P]], channel_multiplier=1).then_inc(consts, 1)
            nc.gpsimd.affine_select(out=causal[:, P:2 * P], in_=causal[:, P:2 * P], compare_op=ALU.is_ge, fill=NEG,
                                    base=0, pattern=[[-1, P]], channel_multiplier=1).then_inc(consts, 1)
            pool.wait_ge(consts, NCONST)
            nc.gpsimd.tensor_copy(identb[:], ident[:]).then_inc(identb_done, 1)

            ln_pool(pool, 0)
            tmp = CXT[:].rearrange("p c n -> p (c n)")
            pool.wait_ge(ctx_in, 16)
            pool.wait_ge(qs_ready, 1)
            nc.gpsimd.tensor_scalar(tmp, CX[:].rearrange("p c n -> p (c n)"), qsr[:, 1:2], qs[:, 3:4], ALU.mult,
                                    ALU.add).then_inc(ctx_q, 1)
            pool.wait_ge(ctx_q, 1)
            nc.gpsimd.tensor_scalar(tmp, tmp, 0.0, 255.0, ALU.max, ALU.min).then_inc(ctx_q, 1)
            pool.wait_ge(ctx_q, 2)
            nc.gpsimd.tensor_scalar(CXQ[:].rearrange("p c n -> p (c n)"), tmp, ROUND, ROUND + 128.0, ALU.add,
                                    ALU.subtract).then_inc(ctx_q, 1)
            ln_pool(pool, 1)
            fwf = FW[:].rearrange("p c n -> p (c n)")
            pool.wait_ge(f0_wscale, 1)
            nc.gpsimd.tensor_scalar(fwf, fwf, wsc[:, 1:2], 1.0, ALU.mult, ALU.min).then_inc(f0_wq, 1)
            pool.wait_ge(f0_wq, 1)
            nc.gpsimd.tensor_scalar(fwf, fwf, -1.0, ROUND, ALU.max, ALU.add).then_inc(f0_wq, 1)
            pool.wait_ge(f0_wq, 2)
            nc.gpsimd.tensor_scalar(WQN[:].rearrange("p c n -> p (c n)"), fwf, ROUND, None,
                                    ALU.subtract).then_inc(f0_wq, 1)
            ln_pool(pool, 2)
            pool.wait_ge(f0_ms, 1)
            nc.gpsimd.tensor_tensor(rrs[:], msq[:], neghalf[:, 0:T], ALU.pow).then_inc(f0_rms, 1)
            ln_pool(pool, 3)
            ln_pool(pool, 4)
            with pool.Fori(0, KVH) as i:
                pool.wait_ge(x_ms, 2 * i + 1)
                nc.gpsimd.tensor_tensor(rx[:, 0:12], ssx[:, 0:12], neghalf[:, 0:12], ALU.pow).then_inc(x_r, 1)
                pool.wait_ge(x_ms, 2 * i + 2)
                nc.gpsimd.tensor_tensor(rx[:, 12:28], ssx[:, 12:28], neghalf[:, 0:16], ALU.pow).then_inc(x_r, 1)
            ln_pool(pool, 5)

        @block.tensor
        def _(pe):
            for s in (a0.w_turned, a1.w_turned, a1_wot_turned, x_proj, x_y):
                pe.sem_inc(s, 1)
            pe.wait_ge(consts, NCONST)
            pe.wait_ge(identb_done, 1)
            ln_pe(pe, 0, 0)
            xt_ready(pe, 0)
            with pe.Fori(0, 2) as i:
                pe.wait_ge(a0.o, i * 8 + 1)
                turn_weights(pe, i, a0, 4)
                project_qkv(pe, i, a0, 4)
                pe.wait_ge(a0.qkv, i * 5 + 5 + 1)
                self_pe(pe, i, a0, 2)

            pe.wait_ge(fw_in, 16)
            pe.wait_ge(f0_wabs, 1)
            pe.wait_ge(a0.o, 17)
            nc.tensor.matmul(OB[1][:, 0:1], ones[:], wab[:], start=True, stop=True).then_inc(f0_wtot, 1)
            pe.wait_ge(ctx_in, 16)
            for k in range(CT):
                if k >= 2:
                    pe.wait_ge(cxt_ready, k - 1)
                for c in range(C):
                    mm = nc.tensor.transpose(TB[k % 2][:, c * P:(c + 1) * P], CX[:, k, c * P:(c + 1) * P], ident[:])
                mm.then_inc(ctx_turned, 1)
            pe.wait_ge(m0_norm, T)
            for c in range(C):
                for t in range(T):
                    mm = nc.tensor.transpose(Sb[c][:, t * P:(t + 1) * P], XQ[:, t, c * P:(c + 1) * P], identb[:])
                mm.then_inc(m0_turned, 1)
            pe.wait_ge(ctx_q, 3)
            pe.wait_ge(cxt_ready, CT)
            for b in range(NB):
                for k in range(C):
                    mm = nc.tensor.matmul(TB[b][0:1, :], onesb[:], CXQ[:, C * b + k, :], start=(k == 0),
                                          stop=(k == C - 1))
                mm.then_inc(m0_col, 1)
            pe.wait_ge(m0_xqt, C)
            for t in range(T):
                for c in range(C):
                    mm = nc.tensor.matmul(OB[0][:, t:t + 1], XQT[:, c, t * P:(t + 1) * P], onesb[:],
                                          start=(c == 0), stop=(c == C - 1))
            mm.then_inc(m0_col, 1)
            pe.wait_ge(m0_colr, NB)
            for t in range(T):
                b = t // 2
                for c in range(C):
                    nc.tensor.matmul(S[t], XQT[:, c, t * P:(t + 1) * P], CXQ[:, C * b + c, :], start=(c == 0),
                                     stop=False)
                nc.tensor.matmul(S[t], ones[0:1, :], colr[0:1, b, :], start=False, stop=True).then_inc(m0_prod, 1)
            pe.wait_ge(f0_wq, 3)
            for c in range(C):
                if c >= 2:
                    pe.wait_ge(f0_wqt, c - 1)
                for o in range(C):
                    mm = nc.tensor.transpose(TBb[c % 2][:, o * P:(o + 1) * P], WQN[:, o, c * P:(c + 1) * P], identb[:])
                mm.then_inc(f0_wturned, 1)

            pe.wait_ge(f0_q, T)
            for c in range(C):
                for t in range(T):
                    mm = nc.tensor.transpose(Sb[c][:, t * P:(t + 1) * P], XQ[:, t, c * P:(c + 1) * P], identb[:])
                mm.then_inc(f0_turned, 1)
            pe.wait_ge(f0_xqt, C)
            pe.wait_ge(f0_wqt, C)
            for t in range(T):
                for c in range(C):
                    mm = nc.tensor.matmul(S[t], XQT[:, c, t * P:(t + 1) * P], WQT[:, c, :], start=(c == 0),
                                          stop=(c == C - 1))
                mm.then_inc(f0_prod, 1)

            ln_pe(pe, 3, 1)
            xt_ready(pe, 1)
            with pe.Fori(0, C) as i:
                pe.wait_ge(a1.o, i * 4 + 1)
                pe.wait_ge(a1_yadd, i * T + 1)
                turn_weights(pe, i, a1, 3)
                pe.wait_ge(a1_wo_in, i * 16 + 16)
                pe.wait_ge(a1.wt_dve, i + 1)
                for c in range(C):
                    mm = nc.tensor.transpose(TB[1][:, c * P:(c + 1) * P], WO[:, c, :], ident[:])
                mm.then_inc(a1_wot_turned, 1)
                project_qkv(pe, i, a1, 3)
                pe.wait_ge(a1.qkv, i * 4 + 4 + 1)
                pe.wait_ge(a1_wot, i + 1)
                self_pe(pe, i, a1, 1)
                pe.wait_ge(a1.o, i * 4 + 4 + 1)
                for t in range(T):
                    mm = nc.tensor.transpose(TB[0][:, t * P:(t + 1) * P], AT[:, t, :], ident[:])
                mm.then_inc(a1_turned, 1)
                pe.wait_ge(a1_att, i + 1)
                for t in range(T):
                    nc.tensor.matmul(S[t], ATT[:, t * P:(t + 1) * P], WOT[:], start=True, stop=True).then_inc(a1_y, 1)

            ln_pe(pe, 4, 2)
            xt_ready(pe, 2)
            with pe.Fori(0, KVH) as i:
                pe.wait_ge(x_exp, i * 16 + 1)
                pe.wait_ge(xw_kv, i * 32 + 32)
                for n in range(6):
                    if n >= 4:
                        pe.wait_ge(x_nat, i * 10 + n - 3)
                    for m in range(2):
                        kt = 2 * n + m
                        b, k = kt // KT_N, kt % KT_N
                        for c in range(C):
                            src = (CXT[:, c, b * CTX + k * P:b * CTX + (k + 1) * P] if k < CTX // P else
                                   XT[:, c, b * SEQ + (k - CTX // P) * P:b * SEQ + (k - CTX // P + 1) * P])
                            mm = nc.tensor.matmul(S[n % 4][:, m * 2 * XD:(m + 1) * 2 * XD], src, WKV[:, c, :],
                                                  start=(c == 0), stop=(c == C - 1))
                    mm.then_inc(x_proj, 1)
                pe.wait_ge(xw_q, i * 16 + 16)
                for t in range(T):
                    n = 6 + t
                    pe.wait_ge(x_nat, i * 10 + n - 3)
                    for c in range(C):
                        mm = nc.tensor.matmul(S[n % 4], XT[:, c, t * P:(t + 1) * P], WQ1[:, c, :], start=(c == 0),
                                              stop=(c == C - 1))
                    mm.then_inc(x_proj, 1)
                pe.wait_ge(x_kn, i * 12 + 12)
                for m in range(7):
                    if m >= 2:
                        pe.wait_ge(x_tr, i * 7 + m - 1)
                    if m == 3:
                        pe.wait_ge(x_nat, i * 10 + 10)
                    for k in range(4):
                        src = KVN[:, 4 * m + k, 0:XD] if m < 3 else QN[:, k, (m - 3) * XD:(m - 2) * XD]
                        mm = nc.tensor.transpose(TB[m % 2][:, k * P:(k + 1) * P], src, ident[:])
                    mm.then_inc(x_turned, 1)
                pe.wait_ge(x_tr, i * 7 + 7)

                def scores(g, h):
                    u = GQ * g + h
                    if u >= 2:
                        pe.wait_ge(x_exp, i * 16 + u)
                    b = g // 2
                    nc.tensor.matmul(pair[u % 2][:, 0:512], QTX[:, h, g * P:(g + 1) * P],
                                     KTX[:, b * KEYS:b * KEYS + 512], start=True, stop=True)
                    nc.tensor.matmul(pair[u % 2][:, 512:KEYS], QTX[:, h, g * P:(g + 1) * P],
                                     KTX[:, b * KEYS + 512:(b + 1) * KEYS], start=True, stop=True).then_inc(x_sc, 1)

                def turn_probs(g, k):
                    m = KT_N * g + k
                    if k == 0:
                        pe.wait_ge(x_p, i * 16 + GQ * (g + 1))
                    if m >= 2:
                        pe.wait_ge(x_pta if m % 2 == 0 else x_ptv, i * 12 + m // 2)
                    for h in range(GQ):
                        mm = nc.tensor.transpose(TB[m % 2][:, h * P:(h + 1) * P], PX[:, g % 2, h, k * P:(k + 1) * P],
                                                 ident[:])
                    mm.then_inc(x_pt, 1)

                def probs_v(g, k):
                    m = KT_N * g + k
                    if k == 0:
                        pe.wait_ge(x_ot, i * T + g + 1)
                    pe.wait_ge(x_pta if m % 2 == 0 else x_ptv, i * 12 + m // 2 + 1)
                    mm = nc.tensor.matmul(OB[0][:], KVN[:, KT_N * (g // 2) + k, XD:2 * XD], PXT[:, g % 2, k, :],
                                          start=(k == 0), stop=(k == KT_N - 1))
                    if k == KT_N - 1:
                        mm.then_inc(x_pv, 1)

                def project_out(g):
                    pe.wait_ge(x_ot, i * T + g + 2)
                    pe.wait_ge(x_ya, i * T + g + 1)
                    if g == 0:
                        pe.wait_ge(xw_o, i * 16 + 16)
                    for h in range(GQ):
                        mm = nc.tensor.matmul(OB[1][:], OT[:, h * P:(h + 1) * P], WO1[:, h, :], start=(h == 0),
                                              stop=(h == GQ - 1))
                    mm.then_inc(x_y, 1)

                for h in range(GQ):
                    scores(0, h)
                for g in range(T):
                    for k in range(KT_N):
                        turn_probs(g, k)
                        if k >= 1:
                            probs_v(g, k - 1)
                        if g + 1 < T and k < GQ:
                            scores(g + 1, k)
                        if k == 1 and g >= 1:
                            pass
                    probs_v(g, KT_N - 1)
                    project_out(g)

            pe.wait_ge(g_in, 16 * (3 + C))
            for m in range(9):
                if m >= 2:
                    pe.wait_ge(g_wt, m - 1)
                for o in range(C):
                    if m < 4:
                        mm = nc.tensor.transpose(TB[m % 2][:, o * P:(o + 1) * P], CX[:, o, m * P:(m + 1) * P], ident[:])
                    elif m < 8 and o == 0:
                        c = m - 4
                        nc.tensor.transpose(TB[m % 2][:, 0:P], AW[:, c * P:(c + 1) * P], ident[:])
                        mm = nc.tensor.transpose(TB[m % 2][:, P:P + ROUTES], RW[:, c * P:(c + 1) * P],
                                                 ident[0:ROUTES, 0:ROUTES])
                    elif m == 8:
                        mm = nc.tensor.transpose(TB[0][:, o * P:(o + 1) * P], BW[:, o].rearrange("p e r -> p (e r)"),
                                                 ident[:])
                mm.then_inc(g_turned, 1)
            ln_pe(pe, 5, 3)
            xt_ready(pe, 3)
            pe.wait_ge(g_wt, 9)
            for t in range(T):
                for c in range(C):
                    mm = nc.tensor.matmul(OB[1][:, t * 16:t * 16 + ROUTES], XT[:, c, t * P:(t + 1) * P],
                                          RT[:, c, P:P + ROUTES], start=(c == 0), stop=(c == C - 1))
            mm.then_inc(g_lg, 1)
            for c in range(C):
                mm = nc.tensor.matmul(OB[0][:], RT[:, c, 0:P], XT[:, c, :], start=(c == 0), stop=(c == C - 1))
            mm.then_inc(g_h, 1)
            for t in range(T):
                for c in range(C):
                    nc.tensor.matmul(S[t], XT[:, c, t * P:(t + 1) * P], F1T[:, c, :], start=(c == 0), stop=False)
            pe.wait_ge(g_sel, 1)
            for t in range(T):
                mm = nc.tensor.transpose(TB[0][0:ROUTES, t * P:(t + 1) * P], selp[:, t, 0:ROUTES], ident[:])
            mm.then_inc(g_selturned, 1)
            pe.wait_ge(g_selT, 1)
            pe.wait_ge(g_oexp, 2)
            nc.tensor.matmul(TB[1][:], oexp[:], selT[:], start=True, stop=True).then_inc(g_w, 1)
            pe.wait_ge(g_hT, 1)
            for t in range(T):
                nc.tensor.matmul(S[t], hT[:, t * P:(t + 1) * P], BT[:], start=False, stop=True).then_inc(g_y, 1)

        @block.scalar
        def _(act):
            def turned_weights(i, s, nw):
                k = nw - nw // 2
                for m in range(0, nw, 2):
                    act.wait_ge(s.w_turned, i * nw + m + 2)
                    nc.scalar.copy(WT[:, m].rearrange("p c f -> p (c f)"), TB[0][:]).then_inc(s.wt_act, 1)

            for s in (x_exp, x_ot):
                act.sem_inc(s, 1)
            ln_act(act, 0)
            with act.Fori(0, 2) as i:
                turned_weights(i, a0, 4)
                self_act(act, i, a0, 2)
            act.wait_ge(ctx_q, 3)
            for k in range(CT):
                act.wait_ge(ctx_turned, k + 1)
                nc.scalar.copy(CXT[:, :, k * P:(k + 1) * P], TB[k % 2][:].rearrange("p (c n) -> p c n", c=C)
                               ).then_inc(cxt_ready, 1)
            for c in range(C):
                act.wait_ge(m0_turned, c + 1)
                nc.scalar.copy(XQT[:, c, :], Sb[c][:, 0:512]).then_inc(m0_xqt, 1)
            for c in range(C):
                act.wait_ge(f0_wturned, c + 1)
                nc.scalar.copy(WQT[:, c, :], TBb[c % 2][:, 0:512]).then_inc(f0_wqt, 1)
            for t in range(T):
                act.wait_ge(ln_norm, 2 * T + t + 1)
                nc.scalar.activation(G[:, t, :], XN[:, t, :], ACT.Square, accum_out=msq0[:, t:t + 1]).then_inc(f0_sq, 1)
            for c in range(C):
                act.wait_ge(f0_turned, c + 1)
                nc.scalar.copy(XQT[:, c, :], Sb[c][:, 0:512]).then_inc(f0_xqt, 1)
            for t in range(T):
                act.wait_ge(f0_y, t + 1)
                nc.scalar.activation(G[:, t, :], TMP[:, t, :], ACT.Gelu).then_inc(f0_gelu, 1)

            ln_act(act, 1)
            with act.Fori(0, C) as i:
                turned_weights(i, a1, 3)
                self_act(act, i, a1, 1)
                act.wait_ge(a1_turned, i + 1)
                nc.scalar.copy(ATT[:], TB[0][:]).then_inc(a1_att, 1)

            ln_act(act, 2)
            with act.Fori(0, KVH) as i:
                for n in range(10):
                    act.wait_ge(x_proj, i * 10 + n + 2)
                    dst = (KVN[:, 2 * n:2 * n + 2, :].rearrange("p k d -> p (k d)") if n < 6 else QN[:, n - 6, :])
                    nc.scalar.copy(dst, S[n % 4]).then_inc(x_nat, 1)
                for m in range(7):
                    act.wait_ge(x_turned, i * 7 + m + 1)
                    if m < 3:
                        nc.scalar.activation(KTX[:, m * 512:(m + 1) * 512], TB[m % 2][:], ACT.Copy,
                                             scale=wqk[:, 0:1]).then_inc(x_tr, 1)
                    else:
                        nc.scalar.copy(QTX[:, m - 3, :], TB[m % 2][:]).then_inc(x_tr, 1)

                def exps(g, h):
                    u = GQ * g + h
                    act.wait_ge(x_nb, i * 16 + u + 1)
                    if h == 0 and g >= 2:
                        act.wait_ge(x_pt, i * 24 + KT_N * (g - 1))
                    nc.scalar.activation(PX[:, g % 2, h, :], pair[u % 2][:, 0:KEYS], ACT.Exp, bias=xnb[:, u:u + 1],
                                         scale=cq[:, 0, u:u + 1], accum_out=xsum[:, u:u + 1]).then_inc(x_exp, 1)

                for h in range(GQ):
                    exps(0, h)
                for g in range(T):
                    for k in range(KT_N):
                        m = KT_N * g + k
                        if m % 2 == 0:
                            act.wait_ge(x_pt, i * 24 + m + 1)
                            nc.scalar.copy(PXT[:, g % 2, k, :], TB[0][:]).then_inc(x_pta, 1)
                        if g + 1 < T and k < GQ:
                            exps(g + 1, k)
                    act.wait_ge(x_pv, i * T + g + 1)
                    nc.scalar.copy(OT[:], OB[0][:]).then_inc(x_ot, 1)

            for m in range(9):
                act.wait_ge(g_turned, m + 1)
                if m < 4:
                    nc.scalar.copy(F1T[:, m, :], TB[m % 2][:]).then_inc(g_wt, 1)
                elif m < 8:
                    nc.scalar.copy(RT[:, m - 4, 0:P + ROUTES], TB[m % 2][:, 0:P + ROUTES]).then_inc(g_wt, 1)
                else:
                    nc.scalar.copy(BT[:], TB[0][:]).then_inc(g_wt, 1)
            ln_act(act, 3)
            act.wait_ge(g_lgd, 2)
            for t in range(T):
                nc.scalar.activation(pr[:, t, 0:ROUTES], lg[:, t, :], ACT.Exp, bias=lmx[:, t:t + 1],
                                     accum_out=lsum[:, t:t + 1]).then_inc(g_exp, 1)
            act.wait_ge(g_selturned, 1)
            nc.scalar.copy(selT[:], TB[0][0:ROUTES, :]).then_inc(g_selT, 1)
            act.wait_ge(g_w, 1)
            nc.scalar.mul(wexp[:], TB[1][:], 2.0).then_inc(g_wexp, 1)

        @block.vector
        def _(dve):
            for s in (a0.qkv, a0.o, a1.qkv, a1.o, a1_yadd, x_ya, x_sq):
                dve.sem_inc(s, 1)
            steps = Steps(dve, dve_step)
            dve.wait_ge(consts, NCONST)
            steps(nc.vector.tensor_scalar(podd[:], pidx[:], 4, 1, ALU.logical_shift_right, ALU.bitwise_and))
            steps(nc.vector.tensor_copy(evenodd[:, 1:2], podd[:]))
            steps(nc.vector.tensor_scalar(evenodd[:, 0:1], evenodd[:, 1:2], -1.0, 1.0, ALU.mult, ALU.add))
            dve.wait_ge(x_in, 16)
            ln_dve(dve, 0)
            ln_copy_dve(dve, 0)
            dve.wait_ge(m0_in, 64)
            steps(nc.vector.reciprocal(qsr[:, 0:1], qs[:, 0:1]))
            nc.vector.reciprocal(qsr[:, 1:2], qs[:, 2:3]).then_inc(qs_ready, 1)
            steps(nc.vector.tensor_scalar(qc[:, 0:1], qs[:, 1:2], -1.0, 128.0, ALU.mult, ALU.add))
            steps(nc.vector.tensor_scalar(qc[:, 3:4], qs[:, 3:4], -1.0, 128.0, ALU.mult, ALU.add))
            steps(nc.vector.tensor_scalar(qc[:, 1:2], qc[:, 0:1], qc[:, 3:4], float(D), ALU.mult, ALU.mult))
            steps(nc.vector.tensor_tensor(qc[:, 2:3], qs[:, 0:1], qs[:, 2:3], ALU.mult))
            dve.wait_ge(fw_in, 16)
            nc.vector.tensor_reduce(wab[:], FW[:], AX.XY, ALU.add, apply_absolute_value=True).then_inc(f0_wabs, 1)
            for j in range(HG):
                slope = float(np.float32(1.0) / np.power(np.float32(2.0), np.float32((j + 1) * 8.0 / 32)))
                nc.vector.scalar_tensor_tensor(out=ALB[:, j, :], in0=posr[:], scalar=slope, in1=causal[:],
                                               op0=ALU.mult, op1=ALU.add).then_inc(a1_albi, 1)

            def turned_weights(i, s, nw):
                for m in range(1, nw, 2):
                    dve.wait_ge(s.w_turned, i * nw + m + 2)
                    nc.vector.tensor_copy(WT[:, m].rearrange("p c f -> p (c f)"), TB[1][:]).then_inc(s.wt_dve, 1)

            def into_x(i, a, t, done, steps, o, r):
                steps(nc.vector.tensor_tensor(osc[:].rearrange("p (h d) -> p h d", h=HG), o, r, ALU.mult))
                dve.wait_ge(a0.o, done + 1)
                dst = X[:, t, :].rearrange("p (a i f) -> p a i f", a=2, i=2)[:, a, i, :]
                return nc.vector.tensor_tensor(dst, dst, osc[:], ALU.add)

            with dve.Fori(0, 2) as i:
                turned_weights(i, a0, 4)
                qkv_dve(dve, i, a0, 4, float(1.0 / np.sqrt(np.float32(32))))
                self_dve(dve, i, a0, 2, lambda j: causal, into_x)
            dve.wait_ge(a0.o, 17)

            dve.wait_ge(f0_wtot, 1)
            steps(nc.vector.tensor_scalar(wsc[:, 0:1], OB[1][:, 0:1], 1.0 / (D * D), 1e-5, ALU.mult, ALU.max))
            nc.vector.reciprocal(wsc[:, 1:2], wsc[:, 0:1]).then_inc(f0_wscale, 1)
            ln_dve(dve, 1)
            dve.wait_ge(ln_norm, 2 * T)
            for t in range(T):
                nc.vector.tensor_scalar(TMP[:, t, :], XN[:, t, :], qsr[:, 0:1], qs[:, 1:2], ALU.mult,
                                        ALU.add).then_inc(m0_q1, 1)
            for t in range(T):
                dve.wait_ge(m0_q1, t + 1)
                nc.vector.tensor_scalar(TMP[:, t, :], TMP[:, t, :], 0.0, 255.0, ALU.max, ALU.min).then_inc(m0_q2, 1)
            for t in range(T):
                dve.wait_ge(m0_q2, t + 1)
                nc.vector.tensor_scalar(XQ[:, t, :], TMP[:, t, :], ROUND, ROUND + 128.0, ALU.add,
                                        ALU.subtract).then_inc(m0_norm, 1)
            for b in range(NB):
                dve.wait_ge(m0_col, b + 1)
                nc.vector.tensor_scalar(colr[0:1, b, :], TB[b][0:1, :], qc[0:1, 0:1], qc[0:1, 1:2], ALU.mult,
                                        ALU.add).then_inc(m0_colr, 1)
            dve.wait_ge(m0_col, NB + 1)
            steps(nc.vector.tensor_scalar(rowc[:], OB[0][:, 0:T], qc[:, 3:4], None, ALU.mult))
            for t in range(T):
                dve.wait_ge(m0_prod, t + 1)
                nc.vector.tensor_scalar(TMP[:, t, :], S[t], rowc[:, t:t + 1], qc[:, 2:3], ALU.add,
                                        ALU.mult).then_inc(m0_y, 1)
                dve.wait_ge(m0_y, 2 * t + 1)
                nc.vector.tensor_tensor(X[:, t, :], X[:, t, :], TMP[:, t, :], ALU.add).then_inc(m0_y, 1)
            dve.wait_ge(m0_y, 2 * T)

            ln_dve(dve, 2)
            for t in range(T):
                dve.wait_ge(ln_norm, 2 * T + t + 1)
                nc.vector.tensor_reduce(mab[:, t:t + 1], XN[:, t, :], AX.X, ALU.max,
                                        apply_absolute_value=True).then_inc(f0_mab, 1)
            dve.wait_ge(f0_sq, T)
            nc.vector.tensor_scalar(msq[:], msq0[:], 1.0 / D, 1e-5, ALU.mult, ALU.add).then_inc(f0_ms, 1)
            dve.wait_ge(f0_rms, 1)
            dve.wait_ge(f0_mab, T)
            steps(nc.vector.tensor_tensor(amx[:], mab[:], rrs[:], ALU.mult))
            steps(nc.vector.tensor_scalar(amx[:], amx[:], 1e-5, None, ALU.max))
            steps(nc.vector.reciprocal(ascl[:], amx[:]))
            steps(nc.vector.tensor_scalar(ascl[:], ascl[:], 127.0, None, ALU.mult))
            steps(nc.vector.tensor_scalar(adq[:], amx[:], 1.0 / 127.0, wsc[:, 0:1], ALU.mult, ALU.mult))
            for t in range(T):
                nc.vector.tensor_scalar(TMP[:, t, :], XN[:, t, :], rrs[:, t:t + 1], ascl[:, t:t + 1], ALU.mult,
                                        ALU.mult).then_inc(f0_q1, 1)
            for t in range(T):
                dve.wait_ge(f0_q1, t + 1)
                nc.vector.tensor_scalar(TMP[:, t, :], TMP[:, t, :], -128.0, 127.0, ALU.max, ALU.min).then_inc(f0_q2, 1)
            for t in range(T):
                dve.wait_ge(f0_q2, t + 1)
                nc.vector.tensor_scalar(XQ[:, t, :], TMP[:, t, :], ROUND, ROUND, ALU.add,
                                        ALU.subtract).then_inc(f0_q, 1)
            dve.wait_ge(f0_bin, 16)
            for t in range(T):
                dve.wait_ge(f0_prod, t + 1)
                nc.vector.scalar_tensor_tensor(out=TMP[:, t, :], in0=S[t], scalar=adq[:, t:t + 1], in1=fb[:],
                                               op0=ALU.mult, op1=ALU.add).then_inc(f0_y, 1)
            for t in range(T):
                dve.wait_ge(f0_gelu, t + 1)
                nc.vector.tensor_tensor(G[:, t, :], G[:, t, :], XN[:, t, :], ALU.add).then_inc(f0_x1, 1)
                dve.wait_ge(f0_x1, 2 * t + 1)
                nc.vector.tensor_tensor(X[:, t, :], X[:, t, :], G[:, t, :], ALU.add).then_inc(f0_x1, 1)
            dve.wait_ge(f0_x1, 2 * T)

            def add_bias(row, done, n):
                dve.wait_ge(ln_norm, (n + 1) * T)
                for t in range(T):
                    nc.vector.tensor_tensor(X[:, t, :], X[:, t, :], row[:], ALU.add).then_inc(done, 1)
                dve.wait_ge(done, T)

            ln_dve(dve, 3)
            ln_copy_dve(dve, 1)
            dve.wait_ge(a1_boutin, 16)
            add_bias(boutb, a1_badd, 3)

            def into_at(i, a, t, done, steps, o, r):
                return nc.vector.tensor_tensor(AT[:, t, :].rearrange("p (h d) -> p h d", h=HG), o, r, ALU.mult)

            with dve.Fori(0, C) as i:
                turned_weights(i, a1, 3)
                dve.wait_ge(a1_wot_turned, i + 2)
                nc.vector.tensor_copy(WOT[:], TB[1][:]).then_inc(a1_wot, 1)
                qkv_dve(dve, i, a1, 3, 0.25)
                dve.wait_ge(a1_albi, i + HG)
                self_dve(dve, i, a1, 1, lambda j: ALB[:, j, :], into_at)
                dve.wait_ge(a1.masked, i * 32 + 32)
                nc.vector.tensor_scalar(ALB[:], ALB[:], 0.25, None, ALU.mult).then_inc(a1_albi, 1)
                for t in range(T):
                    dve.wait_ge(a1_y, i * T + t + 1)
                    dve.wait_ge(a1_yadd, i * T + t + 1)
                    nc.vector.tensor_tensor(X[:, t, :], X[:, t, :], S[t], ALU.add).then_inc(a1_yadd, 1)
            dve.wait_ge(a1_yadd, C * T + 1)

            dve.wait_ge(x1_nin, 32)
            nc.vector.tensor_tensor(wqk[:], wn[:, 0:1], wn[:, 1:2], ALU.mult).then_inc(x_wqk, 1)
            ln_dve(dve, 4)
            ln_copy_dve(dve, 2)
            NQ, NK = T * GQ, NB * KT_N
            with dve.Fori(0, KVH) as i:
                steps_x = Steps(dve, x_steps, i * (2 + 16))
                for k in range(NK):
                    dve.wait_ge(x_sq, i * (NK + NQ) + max(k - 1, 0) + 1)
                    if k % 2 == 0:
                        dve.wait_ge(x_nat, i * 10 + k // 2 + 1)
                    nc.vector.tensor_tensor_reduce(out=SQJ[:, k % 2, :], in0=KVN[:, k, 0:XD], in1=KVN[:, k, 0:XD],
                                                   scale=1.0, scalar=0.0, op0=ALU.mult, op1=ALU.add,
                                                   accum_out=ssx[:, k:k + 1]).then_inc(x_sq, 1)
                dve.wait_ge(x_sq, i * (NK + NQ) + NK + 1)
                nc.vector.tensor_scalar(ssx[:, 0:NK], ssx[:, 0:NK], 1.0 / XD, 1e-6, ALU.mult, ALU.add).then_inc(x_ms, 1)
                dve.wait_ge(x_r, 2 * i + 1)
                for k in range(NK):
                    nc.vector.tensor_scalar(KVN[:, k, 0:XD], KVN[:, k, 0:XD], rx[:, k:k + 1], None,
                                            ALU.mult).then_inc(x_kn, 1)
                for t in range(T):
                    dve.wait_ge(x_nat, i * 10 + 7 + t)
                    for h in range(GQ):
                        dve.wait_ge(x_sq, i * (NK + NQ) + NK + GQ * t + h)
                        q = QN[:, t, h * XD:(h + 1) * XD]
                        nc.vector.tensor_tensor_reduce(out=SQJ[:, h % 2, :], in0=q, in1=q, scale=1.0, scalar=0.0,
                                                       op0=ALU.mult, op1=ALU.add,
                                                       accum_out=ssx[:, NK + GQ * t + h:NK + GQ * t + h + 1]
                                                       ).then_inc(x_sq, 1)
                dve.wait_ge(x_sq, (i + 1) * (NK + NQ) + 1)
                nc.vector.tensor_scalar(ssx[:, NK:NK + NQ], ssx[:, NK:NK + NQ], 1.0 / XD, 1e-6, ALU.mult,
                                        ALU.add).then_inc(x_ms, 1)
                dve.wait_ge(x_r, 2 * i + 2)
                steps_x(nc.vector.tensor_scalar(cq[:, 0, :], rx[:, NK:NK + NQ], float(XD) ** -0.5, None, ALU.mult))
                steps_x(nc.vector.tensor_scalar(cq[:, 1, :], rx[:, NK:NK + NQ], -float(XD) ** -0.5, None, ALU.mult))

                def row_max(g, h):
                    u = GQ * g + h
                    dve.wait_ge(x_sc, i * 16 + u + 1)
                    steps_x(nc.vector.tensor_reduce(xmx[:, u:u + 1], pair[u % 2][:, 0:KEYS], AX.X, ALU.max))
                    nc.vector.tensor_tensor(xnb[:, u:u + 1], xmx[:, u:u + 1], cq[:, 1, u:u + 1],
                                            ALU.mult).then_inc(x_nb, 1)

                def normalise(g, h):
                    u = GQ * g + h
                    dve.wait_ge(x_exp, i * 16 + u + 2)
                    nc.vector.reciprocal(xri[:, u:u + 1], xsum[:, u:u + 1]).then_inc(x_ri, 1)
                    dve.wait_ge(x_ri, i * 16 + u + 1)
                    nc.vector.tensor_scalar(PX[:, g % 2, h, :], PX[:, g % 2, h, :], xri[:, u:u + 1], None,
                                            ALU.mult).then_inc(x_p, 1)

                for h in range(GQ):
                    row_max(0, h)
                    if h >= 1:
                        normalise(0, h - 1)
                normalise(0, GQ - 1)
                for g in range(T):
                    for k in range(KT_N):
                        m = KT_N * g + k
                        if m % 2 == 1:
                            dve.wait_ge(x_pt, i * 24 + m + 1)
                            nc.vector.tensor_copy(PXT[:, g % 2, k, :], TB[1][:]).then_inc(x_ptv, 1)
                        if g + 1 < T and k < GQ:
                            row_max(g + 1, k)
                        if g + 1 < T and 1 <= k <= GQ:
                            normalise(g + 1, k - 1)
                    dve.wait_ge(x_y, i * T + g + 2)
                    dve.wait_ge(x_ya, i * T + g + 1)
                    nc.vector.tensor_tensor(X[:, g, :], X[:, g, :], OB[1][:], ALU.add).then_inc(x_ya, 1)
            dve.wait_ge(x_ya, KVH * T + 1)

            ln_dve(dve, 5)
            ln_copy_dve(dve, 3)
            dve.wait_ge(f1_bin, 48)
            nc.vector.tensor_copy(mapf[:], mapi[:]).then_inc(g_oexp, 1)
            dve.wait_ge(g_oexp, 1)
            nc.vector.tensor_scalar(oexp[:], expi[:].rearrange("i e r -> i (e r)"), mapf[:, 0:1], None,
                                    ALU.is_equal).then_inc(g_oexp, 1)
            dve.wait_ge(g_lg, 1)
            nc.vector.tensor_tensor(lg[:], OB[1][:, 0:16 * T].rearrange("p (t n) -> p t n", t=T)[:, :, 0:ROUTES],
                                    rbb[:].unsqueeze(1).to_broadcast([P, T, ROUTES]), ALU.add).then_inc(g_lgd, 1)
            dve.wait_ge(g_lgd, 1)
            nc.vector.tensor_reduce(lmx[:], lg[:], AX.X, ALU.max, negate=True).then_inc(g_lgd, 1)
            dve.wait_ge(g_exp, T)
            steps(nc.vector.reciprocal(lsum[:], lsum[:]))
            steps(nc.vector.tensor_tensor(pr[:, :, 0:ROUTES], pr[:, :, 0:ROUTES],
                                          lsum[:].unsqueeze(2).to_broadcast([P, T, ROUTES]), ALU.mult))
            for t in range(T):
                steps(nc.vector.max(top8[:, t, :], pr[:, t, 0:ROUTES]))
                steps(nc.vector.match_replace(rep[:, t, 0:ROUTES], top8[:, t, :], pr[:, t, 0:ROUTES], -1.0))
            nc.vector.scalar_tensor_tensor(out=selp[:, :, 0:ROUTES], in0=rep[:, :, 0:ROUTES], scalar=0.0,
                                           in1=pr[:, :, 0:ROUTES], op0=ALU.is_lt, op1=ALU.mult).then_inc(g_sel, 1)
            add_bias(f1b, f1_bdone, 5)
            dve.wait_ge(g_wexp, 1)
            dve.wait_ge(g_h, 1)
            nc.vector.tensor_tensor(hT[:], OB[0][:], wexp[:], ALU.mult).then_inc(g_hT, 1)
            for t in range(T):
                dve.wait_ge(g_y, t + 1)
                nc.vector.tensor_tensor(X[:, t, :], X[:, t, :], S[t], ALU.add).then_inc(g_out, 1)


_INS = ['x', 'ctx_4096', 'L0_attn_Wq', 'L0_attn_bq', 'L0_attn_Wk', 'L0_attn_bk', 'L0_attn_Wv', 'L0_attn_bv',
        'L0_xattn_x1_scale', 'L0_xattn_x1_zp', 'L0_xattn_x2_scale', 'L0_xattn_x2_zp', 'L0_ffn_W', 'L0_ffn_b',
        'L1_attn_w_qkv', 'L1_attn_b_qkv', 'L1_attn_w_out', 'L1_attn_b_out', 'L1_xattn_Wq', 'L1_xattn_Wk',
        'L1_xattn_Wv', 'L1_xattn_Wo', 'L1_xattn_q_norm_w', 'L1_xattn_k_norm_w', 'L1_ffn_base_W', 'L1_ffn_base_b',
        'L1_ffn_router_W', 'L1_ffn_router_b', 'L1_ffn_A', 'L1_ffn_B', 'L1_ffn_expert_map']


def kernel(**inputs):
    import numpy as _np
    import concourse.bacc as _bacc
    from concourse import mybir as _mybir
    from concourse.bass_utils import run_bass_kernel_spmd as _run

    nc = _bacc.Bacc("TRN2", target_bir_lowering=False, num_devices=1)
    arrays, args = {}, []
    for name in _INS:
        a = _np.ascontiguousarray(inputs[name])
        arrays[f"in_{name}"] = a
        args.append(nc.dram_tensor(f"in_{name}", a.shape, _mybir.dt.from_np(a.dtype), kind="ExternalInput").ap())
    out = nc.dram_tensor("out_0", (2, 256, 512), _mybir.dt.float32, kind="ExternalOutput").ap()
    decoder_program(nc, *args, out)
    r = _run(nc, [arrays], core_ids=[0])
    return r.results[0]["out_0"]
```

```python
from contextlib import ExitStack

import numpy as np

import concourse.bass as bass
from concourse import mybir

F32 = mybir.dt.float32
BF16 = mybir.dt.bfloat16
I32 = mybir.dt.int32
ALU = mybir.AluOpType
ACT = mybir.ActivationFunctionType
AX = mybir.AxisListType

P = 128
D = 512
NB = 2
SEQ = 256
T = NB * SEQ // P
C = D // P
CTX = 512
CT = NB * CTX // P
HD = 16
HG = P // HD
SCALE0 = float(1.0 / np.sqrt(np.float32(32)))
SCALE1 = 0.25
LN_EPS = 1e-5
ROUND = 12582912.0
NEG = -1.0e30

XD = 128
KVH = 8
GQ = 4
KT_N = (CTX + SEQ) // P
KEYS = KT_N * P

NE = 8
RANK = 16
ROUTES = 2 * NE - 1


def decoder_program(
    nc, x, ctx_4096, a0_wq, a0_bq, a0_wk, a0_bk, a0_wv, a0_bv, m0_s1, m0_z1, m0_s2, m0_z2, f0_w, f0_b,
    a1_wqkv, a1_bqkv, a1_wout, a1_bout, x1_wq, x1_wk, x1_wv, x1_wo, x1_qn, x1_kn,
    f1_w, f1_b, f1_rw, f1_rb, f1_a, f1_bm, f1_map, out,
):
    ctx = ExitStack()

    def sb(name, shape, dt=F32):
        return ctx.enter_context(nc.sbuf_tensor(name, shape, dt))

    def sem(name):
        return ctx.enter_context(nc.semaphore(name))

    with ctx:
        X = sb("X", [P, T, D])
        XN = sb("XN", [P, T, D])
        XT = sb("XT", [P, C, T * P])
        CX = sb("CX", [P, CT, D])
        CXT = sb("CXT", [P, C, CT * P])

        shared = sb("shared", [P, 4 * KEYS + 2 * GQ * KEYS * 2])

        def shared_f32(at, n, **kw):
            return shared[:, at:at + n].rearrange("p (a b) -> p a b", **kw)

        def shared_bf16(at, n, **kw):
            return shared[:, at:at + n // 2].bitcast(BF16).rearrange("p (a b) -> p a b", **kw)

        TMP = shared_f32(0, T * D, a=T)
        G = shared_f32(2048, T * D, a=T)
        FW = shared_f32(4096, C * D, a=C)
        CXQ = shared_bf16(6144, CT * D, a=CT)
        XQ = shared_bf16(8192, T * D, a=T)
        XQT = shared_bf16(9216, C * T * P, a=C)
        WQT = shared_bf16(10240, C * D, a=C)
        WQN = shared_bf16(11264, C * D, a=C)
        PX = shared[:, 0:4 * KEYS].rearrange("p (s k) -> p s k", s=4)
        PXH = shared_bf16(3072, 8 * KEYS, a=8).rearrange("p (s h) k -> p s h k", s=2)
        PXL = shared_bf16(6144, 8 * KEYS, a=8).rearrange("p (s h) k -> p s h k", s=2)
        PXT = shared_bf16(9216, 12 * 1024, a=12).rearrange("p (s k) q -> p s k q", s=2)
        XTH = XT[:, 0:2, :].bitcast(BF16).rearrange("p a (b t) -> p (a b) t", b=2)
        XTL = XT[:, 2:4, :].bitcast(BF16).rearrange("p a (b t) -> p (a b) t", b=2)
        CXTH = CXT[:, 0:2, :].bitcast(BF16).rearrange("p a (b t) -> p (a b) t", b=2)
        CXTL = CXT[:, 2:4, :].bitcast(BF16).rearrange("p a (b t) -> p (a b) t", b=2)

        ident = sb("ident", [P, P])
        identb = sb("identb", [P, P], BF16)
        ones = sb("ones", [P, P])
        onesb = sb("onesb", [P, 1], BF16)
        maskq = sb("maskq", [P, 2 * P], BF16)
        maskk = sb("maskk", [P, 3 * P], BF16)
        neghalf = sb("neghalf", [P, 32])
        lnst = sb("lnst", [P, T, 6])
        lnmv = sb("lnmv", [P, T, 2])
        lnve = sb("lnve", [P, T])
        lnrs = sb("lnrs", [P, T])

        W0 = sb("W0", [P, 4, D])
        WT = sb("WT", [P, 4, C, P])
        WO = sb("WO", [P, C, P])
        WOT = sb("WOT", [P, D])
        brow = sb("brow", [P, 4 * P])
        EXT = 64
        KHI, KLO, QLO, ALI, MAX = 0, HD, 2 * HD, 3 * HD, 3 * HD + 3
        ALB = sb("ALB", [P, HG, 2 * P])
        QE = ALB[:].rearrange("p h k -> p (h k)").bitcast(BF16).rearrange("p (a t e) -> p a t e", a=2, t=T)
        KQ = sb("KQ", [P, 4 * T * P])
        QR = KQ[:].bitcast(BF16).rearrange("p (g n) -> p g n", g=4)
        KE = shared_bf16(0, T * HG * EXT, a=T)
        KR = shared_bf16(1024, NB * 1024, a=NB)
        NAT = shared_f32(2048, 4 * T * P, a=4)
        VW = 2 * HD + 1
        VX = shared_bf16(8192, T * HG * (VW + 1), a=T * HG)
        RING = 4
        WID = 3 * P
        units = sb("units", [P, RING * 2 * WID])
        PE32 = units[:].rearrange("p (r h k) -> p r h k", r=RING, h=2)
        PEH = shared_bf16(9216, RING * 2 * WID, a=RING * 2).rearrange("p (r h) k -> p r h k", r=RING)
        PEL = shared_bf16(9216 + RING * WID, RING * 2 * WID, a=RING * 2).rearrange("p (r h) k -> p r h k", r=RING)
        nmax = sb("nmax", [P, 4, 2, HG])
        rinv = sb("rinv", [P, 2, HG])
        osc = sb("osc", [P, P])
        olow = sb("olow", [P, 2, HG, HD])
        att = sb("att", [P, 2 * T * P])
        AT = att[:, 0:T * P].rearrange("p (t f) -> p t f", t=T)
        ATT = att[:, T * P:2 * T * P]
        posk = sb("posk", [P, T])
        albf = sb("albf", [P, 1, T * HG])
        albb = sb("albb", [P, 3, T * HG], BF16)

        qs = sb("qs", [P, 4])
        qsr = sb("qsr", [P, 2])
        qc = sb("qc", [P, 4])
        colr = sb("colr", [1, NB, D])
        rowc = sb("rowc", [P, T])
        fb = sb("fb", [P, D])
        boutb = sb("boutb", [P, D])
        wab = sb("wab", [P, 1])
        wsc = sb("wsc", [P, 2])
        msq0 = sb("msq0", [P, T])
        msq = sb("msq", [P, T])
        mab = sb("mab", [P, T])
        rrs = sb("rrs", [P, T])
        amx = sb("amx", [P, T])
        ascl = sb("ascl", [P, T])
        adq = sb("adq", [P, T])

        WKV = sb("WKV", [P, C, 2 * XD])
        WQ1 = W0
        WO1 = sb("WO1", [P, GQ, D])
        KN = units[:, 0:12 * XD].rearrange("p (k d) -> p k d", k=NB * KT_N)
        VH = units[:, 12 * XD:18 * XD].bitcast(BF16).rearrange("p (k d) -> p k d", k=NB * KT_N)
        VL = units[:, 18 * XD:24 * XD].bitcast(BF16).rearrange("p (k d) -> p k d", k=NB * KT_N)
        WKVP = att[:].bitcast(BF16).rearrange("p (s c d) -> p s c d", s=2, c=C)
        WQP = WT[:].rearrange("p m c f -> p (m c f)").bitcast(BF16).rearrange("p (s c d) -> p s c d", s=2, c=C)
        WOP = CX[:, 4:8, :].rearrange("p a d -> p (a d)").bitcast(BF16).rearrange("p (s h d) -> p s h d", s=2, h=GQ)
        QN = XN
        KTH = KQ[:, 0:NB * KEYS // 2].bitcast(BF16)
        KTL = KQ[:, NB * KEYS // 2:NB * KEYS].bitcast(BF16)
        QTP = ALB[:].rearrange("p h k -> p (h k)").bitcast(BF16).rearrange("p (s t q) -> p s t q", s=2, t=T)
        OTP = sb("OTP", [P, 2, GQ * P], BF16)
        SQJ = sb("SQJ", [P, 2, P])
        ssx = sb("ssx", [P, 32])
        rx = sb("rx", [P, 32])
        cq = sb("cq", [P, 2, T * GQ])
        wn = sb("wn", [P, 2])
        wqk = sb("wqk", [P, 1])
        xmx = sb("xmx", [P, T * GQ])
        xnb = sb("xnb", [P, T * GQ])
        xsum = sb("xsum", [P, T * GQ])
        xri = sb("xri", [P, T * GQ])

        RW = sb("RW", [ROUTES, D])
        AW = sb("AW", [P, D])
        BW = WO[:].rearrange("p c (e r) -> p c e r", e=NE)
        F1T = WT[:].rearrange("p m c f -> p m (c f)")
        RT = sb("RT", [P, C, P + 16])
        BT = units[:, 0:D]
        f1b = boutb
        rbb = sb("rbb", [P, ROUTES])
        mapi = sb("mapi", [ROUTES, 1], I32)
        mapf = sb("mapf", [ROUTES, 1])
        expi = sb("expi", [ROUTES, NE, RANK])
        oexp = sb("oexp", [ROUTES, NE * RANK])
        lg = sb("lg", [P, T, ROUTES])
        lmx = sb("lmx", [P, T])
        lsum = sb("lsum", [P, T])
        pr = sb("pr", [P, T, 16])
        top8 = sb("top8", [P, T, 8])
        rep = sb("rep", [P, T, 16])
        selp = sb("selp", [P, T, 16])
        selT = units[0:ROUTES, 3 * D:3 * D + T * P]
        wexp = units[:, D:D + T * P]
        hT = units[:, 2 * D:2 * D + T * P]

        pair = [ctx.enter_context(nc.psum_tensor(f"pair{i}", [P, 1024], F32)) for i in range(2)]
        S = [pair[0][:, 0:512], pair[0][:, 512:1024], pair[1][:, 0:512], pair[1][:, 512:1024]]
        TB = [ctx.enter_context(nc.psum_tensor(f"turn{i}", [P, 512], F32)) for i in range(2)]
        Sb, TBb = [s.bitcast(BF16) for s in S], [b[:].bitcast(BF16) for b in TB]
        OB = [ctx.enter_context(nc.psum_tensor(f"acc{i}", [P, 512], F32)) for i in range(2)]

        x_in, ctx_in, fw_in, out_done = sem("x_in"), sem("ctx_in"), sem("fw_in"), sem("out_done")
        consts = sem("consts")
        NCONST = 12
        zeroed, identb_done, qs_ready = sem("zeroed"), sem("identb_done"), sem("qscales_ready")
        ln_stat, ln_aggr, ln_var, ln_rstd, ln_norm = (sem(f"ln_{n}") for n in ("stat", "aggr", "var", "rstd", "norm"))
        ln_turned, xt_act, xt_dve = sem("ln_turned"), sem("xt_act"), sem("xt_dve")
        dve_step = sem("dve_step")
        ctx_turned, cxt_ready = sem("ctx_turned"), sem("cxt_ready")


        class Steps:

            def __init__(self, eng, s, base=0):
                self.eng, self.s, self.base, self.n = eng, s, base, 0

            def __call__(self, ins):
                self.n += 1
                ins.then_inc(self.s, 1)
                self.eng.wait_ge(self.s, self.base + self.n)

        LAG = 3

        def self_order(na):
            G, order, done = na * NB, [], 0
            order += [("max", g, r) for g in range(2) for r in range(3)]
            for g in range(G):
                order.append(("turn", g, 0))
                for j in range(HG // 2):
                    order.append(("exp", g, j))
                    if g + 2 < G and j < 3:
                        order.append(("max", g + 2, j))
                    if 4 * g + j >= LAG:
                        order.append(("pv", (4 * g + j - LAG) // 4, (4 * g + j - LAG) % 4))
            return order + [("pv", q // 4, q % 4) for q in range(4 * G - LAG, 4 * G)]

        def fills(na):
            return [o for o in self_order(na) if o[0] in ("max", "exp")]

        class SelfSems:

            def __init__(self, n):
                self.w_in = sem(f"{n}_w_in")
                self.b_in = sem(f"{n}_b_in")
                self.w_turned = sem(f"{n}_w_turned")
                self.wt_act = sem(f"{n}_wt_act")
                self.wt_dve = sem(f"{n}_wt_dve")
                self.proj = sem(f"{n}_proj")
                self.nat = sem(f"{n}_nat")
                self.high = sem(f"{n}_high")
                self.low = sem(f"{n}_low")
                self.turned = sem(f"{n}_turned")
                self.out_act = sem(f"{n}_turned_act")
                self.out_dve = sem(f"{n}_turned_dve")
                self.scores = sem(f"{n}_scores")
                self.max = sem(f"{n}_max")
                self.msplit = sem(f"{n}_max_split")
                self.exps = sem(f"{n}_exps")
                self.phigh = sem(f"{n}_exp_high")
                self.plow = sem(f"{n}_exp_low")
                self.pv = sem(f"{n}_pv")
                self.o = sem(f"{n}_o")
                self.steps = sem(f"{n}_steps")

        a0 = SelfSems("a0")
        a1 = SelfSems("a1")
        a1_albi, a1_turned, a1_att, a1_y, a1_yadd = (sem(f"a1_{n}") for n in ("alibi", "att_turned", "att", "y", "yadd"))
        a1_rows = sem("a1_rows")
        a1_wot_turned, a1_wot, a1_wo_in, a1_badd = (sem(f"a1_{n}") for n in ("wot_turned", "wot", "wo_in", "b_out"))

        def self_pe(pe, i, s, na):
            G, F = na * NB, fills(na)
            NT, NMAX, NEXP = 2 + 2 * G, 3 * G, 4 * G

            def turn(m):
                if m < 2:
                    pe.wait_ge(s.low, i * (na + 2) + 1)
                elif m < 2 + G:
                    pe.wait_ge(s.low, i * (na + 2) + 2 + (m - 2) // NB)
                else:
                    pe.wait_ge(s.msplit, i * G + m - 1 - G)
                if m >= 2:
                    pe.wait_ge(s.out_act if m % 2 == 0 else s.out_dve, i * (NT // 2) + m // 2)
                for pr in range(HG // 2):
                    for tt in range(2):
                        b = m % 2 if m < 2 else (m - 2) % NB
                        e = slice(pr * 2 * EXT, (pr + 1) * 2 * EXT)
                        src = KE[:, 2 * b + tt, e] if m < 2 else QE[:, ((m - 2) % G) // NB, 2 * b + tt, e]
                        o = (2 * pr + tt) * P
                        mm = nc.tensor.transpose(TBb[m % 2][:, o:o + P], src, identb[:])
                mm.then_inc(s.turned, 1)

            def turned_ready(m):
                pe.wait_ge(s.out_act if m % 2 == 0 else s.out_dve, i * (NT // 2) + m // 2 + 1)

            def bank_free(f):
                if f >= 2:
                    kind, g, r = F[f - 2]
                    if kind == "max":
                        pe.wait_ge(s.max, i * NMAX + 3 * g + r + 1)
                    else:
                        pe.wait_ge(s.exps, i * NEXP + 4 * g + r + 1)

            for m in range(2 + G):
                turn(m)
            f = 0
            for kind, g, r in self_order(na):
                b = g % NB
                if kind == "turn":
                    turn(2 + G + g)
                elif kind == "max":
                    if r == 0:
                        turned_ready(b)
                        turned_ready(2 + g)
                    bank_free(f)
                    qt, w = (0, P) if r == 0 else (1, 2 * P)
                    for half in range(2):
                        bank, n = pair[f % 2][:, half * 512:(half + 1) * 512], 512 // w
                        nc.tensor.matmul(bank.rearrange("p (n k) -> p n k", n=n), identb[:],
                                         maskq[:, 2 * P - w:].unsqueeze(1).to_broadcast([P, n, w]),
                                         start=True, stop=False)
                        for x in range(n):
                            h = 2 * x + half + (0 if r == 0 else 4 * (r - 1))
                            rows, o = slice((h % 2) * EXT, (h % 2 + 1) * EXT), (h // 2) * 2 * P
                            mm = nc.tensor.matmul(bank[:, x * w:(x + 1) * w], QR[rows, g, o + qt * P:o + (qt + 1) * P],
                                                  KR[rows, b, o:o + w], start=False, stop=(x == n - 1))
                    mm.then_inc(s.scores, 1)
                    f += 1
                elif kind == "exp":
                    if r == 0:
                        turned_ready(2 + G + g)
                    bank_free(f)
                    for hh in range(2):
                        bank, o, rows = pair[f % 2][:, hh * 512:hh * 512 + WID], r * 2 * P, slice(hh * EXT, (hh + 1) * EXT)
                        nc.tensor.matmul(bank, identb[:], maskk[:], start=True, stop=False)
                        nc.tensor.matmul(bank[:, 0:2 * P], KR[rows, b, o:o + P], QR[rows, g, o:o + 2 * P],
                                         start=False, stop=False)
                        mm = nc.tensor.matmul(bank[:, 2 * P:3 * P], KR[rows, b, o + P:o + 2 * P],
                                              QR[rows, g, o + P:o + 2 * P], start=False, stop=True)
                    mm.then_inc(s.scores, 1)
                    f += 1
                else:
                    q = 4 * g + r
                    if r == 0:
                        pe.wait_ge(s.o, 2 * (i * G + g) + 1)
                    pe.wait_ge(s.plow, i * NEXP + q + 1)
                    for hh in range(2):
                        h = 2 * r + hh
                        for qt in range(2):
                            out = OB[qt][:, h * VW:(h + 1) * VW]
                            for kt in range(qt + 1):
                                o = (qt + kt) * P
                                v = VX[:, (2 * b + kt) * HG + h, 0:VW]
                                nc.tensor.matmul(out, PEH[:, q % RING, hh, o:o + P], v, start=(kt == 0), stop=False)
                                mm = nc.tensor.matmul(out, PEL[:, q % RING, hh, o:o + P], v, start=False,
                                                      stop=(kt == qt))
                    mm.then_inc(s.pv, 1)

        def heads(x):
            return x.rearrange("p (n d) -> p n d", d=HD)

        def rows_of(x, at, step=1):
            return x.rearrange("p t (h e d) -> p (t h) e d", h=HG, d=HD)[:, :, at // HD:at // HD + step + 1:step, :]

        def self_act(act, i, s, na, scale):
            G = na * NB
            NT, NEXP = 2 + 2 * G, 4 * G

            def turned_out(m):
                if m % 2 == 0:
                    act.wait_ge(s.turned, i * NT + m + 1)
                    dst = KR[:, m, :] if m < 2 else QR[:, (m - 2) % G, :]
                    nc.scalar.copy(dst, TBb[m % 2]).then_inc(s.out_act, 1)

            def high(q):
                act.wait_ge(s.exps, i * NEXP + q + 1)
                if q >= RING:
                    act.wait_ge(s.pv, i * NEXP + q - RING + 1)
                nc.scalar.copy(PEH[:, q % RING], PE32[:, q % RING]).then_inc(s.phigh, 1)

            act.wait_ge(s.nat, 2 * i + 3)
            nc.scalar.copy(rows_of(KE, 0, 2), heads(NAT[:, 0]).unsqueeze(2).to_broadcast([P, T * HG, 2, HD])
                           ).then_inc(s.high, 1)
            for a in range(na):
                nc.scalar.activation(rows_of(QE[:, a], 0), heads(NAT[:, 2 + a]).unsqueeze(2).to_broadcast(
                    [P, T * HG, 2, HD]), ACT.Copy, scale=scale).then_inc(s.high, 1)
            nc.scalar.copy(VX[:, :, HD:2 * HD], heads(NAT[:, 1])).then_inc(s.high, 1)
            for m in range(2 + G):
                turned_out(m)
            for kind, g, r in self_order(na):
                q = 4 * g + r
                if kind == "turn":
                    turned_out(2 + G + g)
                elif kind == "exp":
                    f = fills(na).index((kind, g, r))
                    act.wait_ge(s.scores, i * (3 * G + NEXP) + f + 1)
                    if q >= RING:
                        act.wait_ge(s.plow, i * NEXP + q - RING + 1)
                    nc.scalar.activation(PE32[:, q % RING], pair[f % 2].rearrange("p (h k) -> p h k", h=2)[:, :, 0:WID],
                                         ACT.Exp).then_inc(s.exps, 1)
                    if q >= 1:
                        high(q - 1)
            high(4 * G - 1)

        def self_dve(dve, i, s, na, scale, finish):
            G, nw = na * NB, na + 2
            NT, NMAX, NEXP = 2 + 2 * G, 3 * G, 4 * G
            per = 4 if s is a0 else 3
            steps = Steps(dve, s.steps, i * (1 + G + 2 * G * per))

            def turned_out(m):
                if m % 2 == 1:
                    dve.wait_ge(s.turned, i * NT + m + 1)
                    dst = KR[:, m, :] if m < 2 else QR[:, (m - 2) % G, :]
                    nc.vector.tensor_copy(dst.bitcast(F32), TB[m % 2][:]).then_inc(s.out_dve, 1)

            def low(q):
                dve.wait_ge(s.phigh, i * NEXP + q + 1)
                nc.vector.tensor_tensor(PEL[:, q % RING], PE32[:, q % RING], PEH[:, q % RING],
                                        ALU.subtract).then_inc(s.plow, 1)

            dve.wait_ge(s.b_in, i * 16 * nw + 16 * nw)
            for pr in range(2):
                dve.wait_ge(s.proj, 2 * i + pr + 1)
                nc.vector.tensor_tensor(
                    NAT[:, 0:nw, 2 * pr * P:2 * (pr + 1) * P].rearrange("p m (t f) -> p t m f", t=2),
                    pair[pr].rearrange("p (t m f) -> p t m f", t=2, m=4)[:, :, 0:nw, :],
                    brow[:, 0:nw * P].rearrange("p (m f) -> p m f", m=nw).unsqueeze(1).to_broadcast([P, 2, nw, P]),
                    ALU.add).then_inc(s.nat, 1)
            steps(nc.vector.memset(QE[:, 0:na].rearrange("p a t (h e) -> p (a t h) e", h=HG)[:, :, MAX:MAX + 2], 0.0))
            dve.wait_ge(s.high, i * nw + 1)
            nc.vector.tensor_tensor(rows_of(KE, KLO)[:, :, 0], heads(NAT[:, 0]), rows_of(KE, KHI)[:, :, 0],
                                    ALU.subtract).then_inc(s.low, 1)
            for a in range(na):
                dve.wait_ge(s.high, i * nw + 2 + a)
                nc.vector.scalar_tensor_tensor(out=rows_of(QE[:, a], QLO)[:, :, 0], in0=heads(NAT[:, 2 + a]),
                                               scalar=scale, in1=rows_of(QE[:, a], 0)[:, :, 0], op0=ALU.mult,
                                               op1=ALU.subtract).then_inc(s.low, 1)
            dve.wait_ge(s.high, i * nw + nw)
            nc.vector.tensor_tensor(VX[:, :, 0:HD], heads(NAT[:, 1]), VX[:, :, HD:2 * HD],
                                    ALU.subtract).then_inc(s.low, 1)
            for m in range(2 + G):
                turned_out(m)
            for kind, g, r in self_order(na):
                a, b, q = g // NB, g % NB, 4 * g + r
                if kind == "turn":
                    turned_out(2 + G + g)
                elif kind == "max":
                    f = fills(na).index((kind, g, r))
                    n, w = (HG, P) if r == 0 else (HG // 2, 2 * P)
                    dst = nmax[:, g, 0, :] if r == 0 else nmax[:, g, 1, (r - 1) * n:r * n]
                    dst = dst.rearrange("p (x e) -> p e x", e=2)
                    dve.wait_ge(s.scores, i * (NMAX + NEXP) + f + 1)
                    nc.vector.tensor_reduce(dst, pair[f % 2].rearrange("p (e x k) -> p e x k", e=2, k=w), AX.X, ALU.max,
                                            negate=True).then_inc(s.max, 1)
                    if r == 2:
                        rows = QE[:, a, 2 * b:2 * b + 2].rearrange("p t (h e) -> p t h e", h=HG)
                        dve.wait_ge(s.max, i * NMAX + 3 * g + 3)
                        steps(nc.vector.tensor_copy(rows[:, :, :, MAX], nmax[:, g]))
                        nc.vector.tensor_tensor(rows[:, :, :, MAX + 1], nmax[:, g], rows[:, :, :, MAX],
                                                ALU.subtract).then_inc(s.msplit, 1)
                elif kind == "exp":
                    if q >= 2:
                        if q - 2 >= RING:
                            dve.wait_ge(s.pv, i * NEXP + q - 2 - RING + 1)
                        low(q - 2)
                elif kind == "pv":
                    if q + LAG == 4 * G:
                        for x in (4 * G - 2, 4 * G - 1):
                            dve.wait_ge(s.pv, i * NEXP + x - RING + 1)
                            low(x)
                    if r == 3:
                        dve.wait_ge(s.pv, i * NEXP + q + 1)
                        for qt in range(2):
                            o = OB[qt][:, 0:HG * VW].rearrange("p (h e) -> p h e", h=HG)
                            steps(nc.vector.reciprocal(rinv[:, qt, :], o[:, :, 2 * HD]))
                            steps(nc.vector.tensor_copy(olow[:, qt], o[:, :, 0:HD]))
                            steps(nc.vector.tensor_tensor(olow[:, qt], o[:, :, HD:2 * HD], olow[:, qt], ALU.add))
                            finish(i, a, 2 * b + qt, 2 * (i * G + g) + qt, steps, olow[:, qt],
                                   rinv[:, qt, :].unsqueeze(2).to_broadcast([P, HG, HD])).then_inc(s.o, 1)

        def turn_weights(pe, i, s, nw):
            pe.wait_ge(s.w_in, i * 16 * nw + 16 * nw)
            for m in range(nw):
                if m >= 2:
                    pe.wait_ge(s.wt_act if m % 2 == 0 else s.wt_dve, i * (nw - nw // 2 if m % 2 == 0 else nw // 2) + m // 2)
                for c in range(C):
                    mm = nc.tensor.transpose(TB[m % 2][:, c * P:(c + 1) * P], W0[:, m, c * P:(c + 1) * P], ident[:])
                mm.then_inc(s.w_turned, 1)

        def project_qkv(pe, i, s, nw):
            pe.wait_ge(s.wt_act, i * (nw - nw // 2) + (nw - nw // 2))
            pe.wait_ge(s.wt_dve, i * (nw // 2) + nw // 2)
            for t in range(T):
                for c in range(C):
                    mm = nc.tensor.matmul(S[t][:, 0:nw * P].rearrange("p (m f) -> p m f", m=nw),
                                          XT[:, c, t * P:(t + 1) * P], WT[:, 0:nw, c, :], start=(c == 0),
                                          stop=(c == C - 1))
                if t % 2 == 1:
                    mm.then_inc(s.proj, 1)

        m0_norm, m0_turned, m0_xqt = sem("m0_quantised"), sem("m0_turned"), sem("m0_xqt")
        m0_col, m0_colr, m0_prod = sem("m0_colsum"), sem("m0_colrow"), sem("m0_product")
        f0_wabs, f0_wtot, f0_wscale, f0_wq, f0_wturned, f0_wqt = (
            sem(f"f0_{n}") for n in ("wabs", "wtotal", "wscale", "wquant", "wturned", "wqt"))
        f0_ms, f0_rms, f0_q, f0_turned, f0_xqt, f0_prod, f0_y, f0_gelu, f0_sq = (
            sem(f"f0_{n}") for n in ("meansq", "rms", "quantised", "turned", "xqt", "product", "y", "gelu", "squares"))
        xw_kv, xw_q, xw_o = sem("x1_wkv_in"), sem("x1_wq_in"), sem("x1_wo_in")
        x_proj, x_nat, x_ms, x_r, x_kn, x_turned, x_tr = (
            sem(f"x1_{n}") for n in ("proj", "natural", "meansq", "rms", "k_normed", "qk_turned", "qkt"))
        x_sc, x_nb, x_exp, x_p, x_pt, x_pta, x_ptv, x_pv, x_ot, x_y, x_ya, x_steps = (
            sem(f"x1_{n}") for n in ("scores", "neg_bias", "exps", "probs", "p_turned", "pt_act", "pt_dve",
                                     "pv", "ot", "y", "yadd", "steps"))
        x_wqk = sem("x1_wqk")
        x_skv, x_sq_w, x_so, x_wk_st, x_vlo, x_trl, x_phi, x_oth = (
            sem(f"x1_{n}") for n in ("wkv_split", "wq_split", "wo_split", "split_high", "v_low", "qkt_low", "probs_high",
                                     "ot_high"))
        cxt_high, xt_high, xt_low = sem("cxt_high"), sem("xt_high"), sem("xt_low")
        g_in, g_turned, g_wt, g_h, g_hT, g_lg, g_lgd, g_exp, g_sel, g_selturned, g_selT, g_w, g_wexp, g_y, g_oexp = (
            sem(f"f1_{n}") for n in ("in", "turned", "wt", "h", "hT", "logits", "logits_max", "exps", "sel",
                                     "sel_turned", "selT", "w", "wexp", "y", "oexp"))
        ctx_q = sem("ctx_quantised")
        quant, m0_y, f0_mab, f0_x1 = (sem(n) for n in ("quantiser_step", "m0_added", "f0_maxabs", "f0_added"))
        x_sq, x_ri, f1_bdone, g_out = sem("x1_squares"), sem("x1_rsum_inv"), sem("f1_bias_added"), sem("f1_out")

        block = ctx.enter_context(nc.Block())


        def ln_dve(dve, n):
            for t in range(T):
                nc.vector.bn_stats(lnst[:, t, :], X[:, t, :]).then_inc(ln_stat, 1)
            for t in range(T):
                dve.wait_ge(ln_stat, n * T + t + 1)
                nc.vector.bn_aggr(lnmv[:, t, :], lnst[:, t, :]).then_inc(ln_aggr, 1)
            dve.wait_ge(ln_aggr, n * T + T)
            nc.vector.tensor_scalar(lnve[:], lnmv[:, :, 1], LN_EPS, None, ALU.add).then_inc(ln_var, 1)
            dve.wait_ge(ln_rstd, n + 1)
            for t in range(T):
                nc.vector.tensor_scalar(XN[:, t, :], X[:, t, :], lnmv[:, t, 0:1], lnrs[:, t:t + 1], ALU.subtract,
                                        ALU.mult).then_inc(ln_norm, 1)

        def ln_pool(pool, n):
            pool.wait_ge(ln_var, n + 1)
            nc.gpsimd.tensor_tensor(lnrs[:], lnve[:], neghalf[:, 0:T], ALU.pow).then_inc(ln_rstd, 1)

        def ln_pe(pe, n, k):
            pe.wait_ge(ln_norm, n * T + T)
            for c in range(C):
                for t in range(T):
                    mm = nc.tensor.transpose(S[c][:, t * P:(t + 1) * P], XN[:, t, c * P:(c + 1) * P], ident[:])
                mm.then_inc(ln_turned, 1)

        def ln_act(act, k):
            for c in (0, 2):
                act.wait_ge(ln_turned, k * C + c + 1)
                nc.scalar.copy(XT[:, c, :], S[c]).then_inc(xt_act, 1)

        def ln_copy_dve(dve, k):
            for c in (1, 3):
                dve.wait_ge(ln_turned, k * C + c + 1)
                nc.vector.tensor_copy(XT[:, c, :], S[c]).then_inc(xt_dve, 1)

        def ln_split_act(act, k):
            for c in range(C):
                act.wait_ge(ln_turned, k * C + c + 1)
                nc.scalar.copy(XTH[:, c, :], S[c]).then_inc(xt_high, 1)

        def ln_split_dve(dve, k):
            for c in range(C):
                dve.wait_ge(xt_high, c + 1)
                nc.vector.tensor_tensor(XTL[:, c, :], S[c], XTH[:, c, :], ALU.subtract).then_inc(xt_low, 1)

        def split_product(out, high, low, mhigh, mlow, start, stop):
            nc.tensor.matmul(out, high, mhigh, start=start, stop=False)
            nc.tensor.matmul(out, high, mlow, start=False, stop=False)
            return nc.tensor.matmul(out, low, mhigh, start=False, stop=stop)

        def turned_by(m):
            return (x_pta, (m + 1) // 3) if m % 3 == 2 else (x_ptv, m + 1 - (m + 1) // 3)

        def xt_ready(pe, k):
            pe.wait_ge(xt_act, 2 * k + 2)
            pe.wait_ge(xt_dve, 2 * k + 2)

        m0_in, f0_bin, a1_boutin, x1_nin, f1_bin, f1_base_in = (
            sem(f"{n}_in") for n in ("m0s", "f0b", "a1bout", "x1norm", "f1small", "f1base"))

        @block.sync
        def _(sp):
            sp.dma_start(X[:], x.rearrange("b (t p) d -> p (b t) d", p=P)).then_inc(x_in, 16)

            with sp.Fori(0, 2) as i:
                sp.wait_ge(a0.w_turned, i * 4 + 1)
                wq = a0_wq.rearrange("(a i p) d -> a i p d", p=P, i=2)
                sp.dma_start(W0[:, 0, :], a0_wk.rearrange("(i p) d -> i p d", p=P)[i]).then_inc(a0.w_in, 16)
                sp.dma_start(W0[:, 1, :], a0_wv.rearrange("(i p) d -> i p d", p=P)[i]).then_inc(a0.w_in, 16)
                for a in range(2):
                    sp.dma_start(W0[:, 2 + a, :], wq[a][i]).then_inc(a0.w_in, 16)
                sp.wait_ge(a0.nat, 2 * i + 1)
                bq = a0_bq.rearrange("(a i p) -> a i p", p=P, i=2)
                sp.dma_start(brow[:, 0:P], a0_bk.rearrange("(i p) -> i p", p=P)[i].partition_broadcast(P)
                             ).then_inc(a0.b_in, 16)
                sp.dma_start(brow[:, P:2 * P], a0_bv.rearrange("(i p) -> i p", p=P)[i].partition_broadcast(P)
                             ).then_inc(a0.b_in, 16)
                for a in range(2):
                    sp.dma_start(brow[:, (2 + a) * P:(3 + a) * P], bq[a][i].partition_broadcast(P)
                                 ).then_inc(a0.b_in, 16)

            with sp.Fori(0, C) as i:
                sp.wait_ge(a0.w_turned, 9)
                sp.wait_ge(a1.w_turned, i * 3 + 1)
                w = a1_wqkv.rearrange("(m i p) d -> m i p d", m=3, p=P)
                bb = a1_bqkv.rearrange("(m i p) -> m i p", m=3, p=P)
                for m, src in enumerate((1, 2, 0)):
                    sp.dma_start(W0[:, m, :], w[src][i]).then_inc(a1.w_in, 16)
                sp.wait_ge(a1_wot_turned, i + 1)
                sp.dma_start(WO[:], a1_wout.rearrange("(c p) (i f) -> i p c f", p=P, f=P)[i]).then_inc(a1_wo_in, 16)
                sp.wait_ge(a0.nat, 5)
                sp.wait_ge(a1.nat, 2 * i + 1)
                for m, src in enumerate((1, 2, 0)):
                    sp.dma_start(brow[:, m * P:(m + 1) * P], bb[src][i].partition_broadcast(P)).then_inc(a1.b_in, 16)

            sp.wait_ge(a1_badd, T)
            sp.dma_start(f1b[:], f1_b.partition_broadcast(P)).then_inc(f1_base_in, 16)
            sp.wait_ge(a1_wot_turned, C + 1)
            sp.wait_ge(ctx_turned, CT)
            sp.wait_ge(ctx_q, 3)
            sp.dma_start(CX[:, 0:C, :], f1_w.rearrange("(c p) d -> p c d", p=P)).then_inc(g_in, 16)
            sp.dma_start(AW[:], f1_a.rearrange("e r d -> (e r) d")).then_inc(g_in, 16)
            sp.dma_start(RW[:], f1_rw).then_inc(g_in, 16)
            for c in range(C):
                sp.dma_start(BW[:, c], f1_bm.rearrange("e (c p) r -> c p e r", p=P)[c]).then_inc(g_in, 16)

            sp.wait_ge(a1.w_turned, 13)
            with sp.Fori(0, KVH) as i:
                sp.wait_ge(x_skv, i + 1)
                kvw = WKV[:].rearrange("p c (m d) -> p m c d", m=2)
                sp.dma_start(kvw[:, 0], x1_wk.rearrange("(c p) (i d) -> i p c d", p=P, d=XD)[i]).then_inc(xw_kv, 16)
                sp.dma_start(kvw[:, 1], x1_wv.rearrange("(c p) (i d) -> i p c d", p=P, d=XD)[i]).then_inc(xw_kv, 16)
                sp.wait_ge(x_sq_w, i + 1)
                sp.dma_start(WQ1[:], x1_wq.rearrange("(c p) (i d) -> i p c d", p=P, d=GQ * XD)[i]).then_inc(xw_q, 16)
                sp.wait_ge(x_so, i + 1)
                sp.dma_start(WO1[:], x1_wo.rearrange("(i h p) d -> i p h d", h=GQ, p=XD)[i]).then_inc(xw_o, 16)
            for t in range(T):
                sp.wait_ge(g_out, t + 1)
                sp.dma_start(out.rearrange("b (t p) d -> p (b t) d", p=P)[:, t], X[:, t, :]).then_inc(out_done, 16)
            sp.wait_ge(out_done, 16 * T)

        @block.gpsimd
        def _(pool):
            def ones_of_rows(x, at, n):
                return nc.gpsimd.memset(x.rearrange("p t (h e) -> p (t h) e", h=HG)[:, :, at:at + n], 1.0)

            pool.dma_start(CX[:], ctx_4096.rearrange("b (k p) d -> p (b k) d", p=P)).then_inc(ctx_in, 16)
            for n, a in enumerate((m0_s1, m0_z1, m0_s2, m0_z2)):
                pool.dma_start(qs[:, n:n + 1], a.partition_broadcast(P)).then_inc(m0_in, 16)
            pool.dma_start(FW[:], f0_w.rearrange("(c p) d -> p c d", p=P)).then_inc(fw_in, 16)
            pool.dma_start(fb[:], f0_b.partition_broadcast(P)).then_inc(f0_bin, 16)
            pool.dma_start(boutb[:], a1_bout.partition_broadcast(P)).then_inc(a1_boutin, 16)
            pool.dma_start(wn[:, 0:1], x1_qn.rearrange("(p o) -> p o", o=1)).then_inc(x1_nin, 16)
            pool.dma_start(wn[:, 1:2], x1_kn.rearrange("(p o) -> p o", o=1)).then_inc(x1_nin, 16)
            pool.dma_start(rbb[:], f1_rb.partition_broadcast(P)).then_inc(f1_bin, 16)
            pool.dma_start(mapi[:], f1_map.rearrange("(p o) -> p o", o=1)).then_inc(f1_bin, 16)

            masks = G[:, 0:2, :].rearrange("p t d -> p (t d)")[:, 0:5 * P]
            nc.gpsimd.memset(ident[:], 0.0).then_inc(zeroed, 1)
            nc.gpsimd.memset(masks, 0.0).then_inc(zeroed, 1)
            nc.gpsimd.memset(QE.rearrange("p a t e -> p (a t e)"), 0.0).then_inc(zeroed, 1)
            nc.gpsimd.memset(KE.rearrange("p t e -> p (t e)"), 0.0).then_inc(zeroed, 1)
            nc.gpsimd.memset(VX[:], 1.0).then_inc(consts, 1)
            nc.gpsimd.memset(neghalf[:], -0.5).then_inc(consts, 1)
            nc.gpsimd.memset(ones[:], 1.0).then_inc(consts, 1)
            nc.gpsimd.memset(onesb[:], 1.0).then_inc(consts, 1)
            nc.gpsimd.iota(posk[:], [[0, NB], [P, 2]], base=1 - SEQ, channel_multiplier=1,
                           allow_small_or_imprecise_dtypes=True).then_inc(consts, 1)
            nc.gpsimd.iota(expi[:], [[1, NE], [0, RANK]], base=0, channel_multiplier=0,
                           allow_small_or_imprecise_dtypes=True).then_inc(consts, 1)
            pool.wait_ge(zeroed, 4)
            ones_of_rows(QE.rearrange("p a t e -> p (a t) e"), ALI, 3).then_inc(consts, 1)
            ones_of_rows(KE, MAX, 2).then_inc(consts, 1)
            nc.gpsimd.affine_select(out=ident[:], in_=ident[:], compare_op=ALU.not_equal, fill=1.0, base=0,
                                    pattern=[[-1, P]], channel_multiplier=1).then_inc(consts, 1)
            nc.gpsimd.affine_select(out=masks[:, P:2 * P], in_=masks[:, P:2 * P], compare_op=ALU.is_ge, fill=NEG,
                                    base=0, pattern=[[-1, P]], channel_multiplier=1).then_inc(consts, 1)
            for k in (2, 4):
                nc.gpsimd.affine_select(out=masks[:, k * P:(k + 1) * P], in_=masks[:, k * P:(k + 1) * P],
                                        compare_op=ALU.is_ge, fill=NEG, base=0, pattern=[[1, P]],
                                        channel_multiplier=-1).then_inc(consts, 1)
            pool.wait_ge(consts, NCONST)
            nc.gpsimd.tensor_copy(maskq[:], masks[:, 0:2 * P]).then_inc(identb_done, 1)
            nc.gpsimd.tensor_copy(maskk[:], masks[:, 2 * P:5 * P]).then_inc(identb_done, 1)
            nc.gpsimd.tensor_copy(identb[:], ident[:]).then_inc(identb_done, 1)

            ln_pool(pool, 0)
            tmp = CXT[:].rearrange("p c n -> p (c n)")
            pool.wait_ge(ctx_in, 16)
            pool.wait_ge(qs_ready, 1)
            nc.gpsimd.tensor_scalar(tmp, CX[:].rearrange("p c n -> p (c n)"), qsr[:, 1:2], qs[:, 3:4], ALU.mult,
                                    ALU.add).then_inc(ctx_q, 1)
            pool.wait_ge(ctx_q, 1)
            nc.gpsimd.tensor_scalar(tmp, tmp, 0.0, 255.0, ALU.max, ALU.min).then_inc(ctx_q, 1)
            pool.wait_ge(ctx_q, 2)
            nc.gpsimd.tensor_scalar(CXQ[:].rearrange("p c n -> p (c n)"), tmp, ROUND, ROUND + 128.0, ALU.add,
                                    ALU.subtract).then_inc(ctx_q, 1)
            ln_pool(pool, 1)
            fwf = FW[:].rearrange("p c n -> p (c n)")
            pool.wait_ge(f0_wscale, 1)
            nc.gpsimd.tensor_scalar(fwf, fwf, wsc[:, 1:2], 1.0, ALU.mult, ALU.min).then_inc(f0_wq, 1)
            pool.wait_ge(f0_wq, 1)
            nc.gpsimd.tensor_scalar(fwf, fwf, -1.0, ROUND, ALU.max, ALU.add).then_inc(f0_wq, 1)
            pool.wait_ge(f0_wq, 2)
            nc.gpsimd.tensor_scalar(WQN[:].rearrange("p c n -> p (c n)"), fwf, ROUND, None,
                                    ALU.subtract).then_inc(f0_wq, 1)
            ln_pool(pool, 2)
            pool.wait_ge(f0_ms, 1)
            nc.gpsimd.tensor_tensor(rrs[:], msq[:], neghalf[:, 0:T], ALU.pow).then_inc(f0_rms, 1)
            ln_pool(pool, 3)
            pool.wait_ge(f0_x1, 2 * T)
            nc.gpsimd.memset(KE.rearrange("p t e -> p (t e)"), 0.0).then_inc(zeroed, 1)
            nc.gpsimd.memset(VX[:], 1.0).then_inc(a1_rows, 1)
            pool.wait_ge(zeroed, 5)
            ones_of_rows(KE, MAX, 2).then_inc(a1_rows, 1)
            ln_pool(pool, 4)
            pool.sem_inc(x_skv, 1)
            pool.sem_inc(x_sq_w, 1)
            pool.sem_inc(x_so, 1)

            def split_weights(pair_of, src, done, i, n):
                one = ones[:, 0:1].unsqueeze(1).to_broadcast([P, src.shape[1], src.shape[2]])
                nc.gpsimd.tensor_tensor(pair_of[:, 0], src, one, ALU.mult).then_inc(x_wk_st, 1)
                pool.wait_ge(x_wk_st, 3 * i + n)
                nc.gpsimd.tensor_tensor(pair_of[:, 1], src, pair_of[:, 0], ALU.subtract).then_inc(done, 1)

            pool.wait_ge(a1_y, C * T)
            with pool.Fori(0, KVH) as i:
                pool.wait_ge(x_proj, i * 10 + 1)
                pool.wait_ge(xw_kv, i * 32 + 32)
                split_weights(WKVP, WKV[:], x_skv, i, 1)
                pool.wait_ge(xw_q, i * 16 + 16)
                split_weights(WQP, WQ1[:], x_sq_w, i, 2)
                pool.wait_ge(x_ms, 3 * i + 1)
                nc.gpsimd.tensor_tensor(rx[:, 0:12], ssx[:, 0:12], neghalf[:, 0:12], ALU.pow).then_inc(x_r, 1)
                pool.wait_ge(x_ms, 3 * i + 2)
                nc.gpsimd.tensor_tensor(rx[:, 12:16], ssx[:, 12:16], neghalf[:, 0:4], ALU.pow).then_inc(x_r, 1)
                pool.wait_ge(x_ms, 3 * i + 3)
                nc.gpsimd.tensor_tensor(rx[:, 16:28], ssx[:, 16:28], neghalf[:, 0:12], ALU.pow).then_inc(x_r, 1)
                pool.wait_ge(x_y, i * T + 1)
                pool.wait_ge(xw_o, i * 16 + 16)
                split_weights(WOP, WO1[:], x_so, i, 3)
            ln_pool(pool, 5)

        @block.tensor
        def _(pe):
            for s in (a0.w_turned, a1.w_turned, a1_wot_turned, x_proj, x_y):
                pe.sem_inc(s, 1)
            pe.wait_ge(consts, NCONST)
            pe.wait_ge(identb_done, 3)
            ln_pe(pe, 0, 0)
            xt_ready(pe, 0)
            with pe.Fori(0, 2) as i:
                pe.wait_ge(a0.o, i * 8 + 1)
                turn_weights(pe, i, a0, 4)
                project_qkv(pe, i, a0, 4)
                self_pe(pe, i, a0, 2)

            pe.wait_ge(fw_in, 16)
            pe.wait_ge(f0_wabs, 1)
            pe.wait_ge(a0.o, 17)
            nc.tensor.matmul(OB[1][:, 0:1], ones[:], wab[:], start=True, stop=True).then_inc(f0_wtot, 1)
            pe.wait_ge(ctx_in, 16)
            for k in range(CT):
                if k >= 2:
                    pe.wait_ge(cxt_ready, k - 1)
                for c in range(C):
                    mm = nc.tensor.transpose(TB[k % 2][:, c * P:(c + 1) * P], CX[:, k, c * P:(c + 1) * P], ident[:])
                mm.then_inc(ctx_turned, 1)
            pe.wait_ge(m0_norm, T)
            for c in range(C):
                for t in range(T):
                    mm = nc.tensor.transpose(Sb[c][:, t * P:(t + 1) * P], XQ[:, t, c * P:(c + 1) * P], identb[:])
                mm.then_inc(m0_turned, 1)
            pe.wait_ge(ctx_q, 3)
            pe.wait_ge(cxt_ready, CT)
            for b in range(NB):
                for k in range(C):
                    mm = nc.tensor.matmul(TB[b][0:1, :], onesb[:], CXQ[:, C * b + k, :], start=(k == 0),
                                          stop=(k == C - 1))
                mm.then_inc(m0_col, 1)
            pe.wait_ge(m0_xqt, C)
            for t in range(T):
                for c in range(C):
                    mm = nc.tensor.matmul(OB[0][:, t:t + 1], XQT[:, c, t * P:(t + 1) * P], onesb[:],
                                          start=(c == 0), stop=(c == C - 1))
            mm.then_inc(m0_col, 1)
            pe.wait_ge(m0_colr, NB)
            for t in range(T):
                b = t // 2
                for c in range(C):
                    nc.tensor.matmul(S[t], XQT[:, c, t * P:(t + 1) * P], CXQ[:, C * b + c, :], start=(c == 0),
                                     stop=False)
                nc.tensor.matmul(S[t], ones[0:1, :], colr[0:1, b, :], start=False, stop=True).then_inc(m0_prod, 1)
            pe.wait_ge(f0_wq, 3)
            for c in range(C):
                if c >= 2:
                    pe.wait_ge(f0_wqt, c - 1)
                for o in range(C):
                    mm = nc.tensor.transpose(TBb[c % 2][:, o * P:(o + 1) * P], WQN[:, o, c * P:(c + 1) * P], identb[:])
                mm.then_inc(f0_wturned, 1)

            pe.wait_ge(f0_q, T)
            for c in range(C):
                for t in range(T):
                    mm = nc.tensor.transpose(Sb[c][:, t * P:(t + 1) * P], XQ[:, t, c * P:(c + 1) * P], identb[:])
                mm.then_inc(f0_turned, 1)
            pe.wait_ge(f0_xqt, C)
            pe.wait_ge(f0_wqt, C)
            for t in range(T):
                for c in range(C):
                    mm = nc.tensor.matmul(S[t], XQT[:, c, t * P:(t + 1) * P], WQT[:, c, :], start=(c == 0),
                                          stop=(c == C - 1))
                mm.then_inc(f0_prod, 1)

            ln_pe(pe, 3, 1)
            xt_ready(pe, 1)
            with pe.Fori(0, C) as i:
                pe.wait_ge(a1.o, i * 4 + 1)
                pe.wait_ge(a1_yadd, i * T + 1)
                turn_weights(pe, i, a1, 3)
                pe.wait_ge(a1_wo_in, i * 16 + 16)
                pe.wait_ge(a1.wt_dve, i + 1)
                for c in range(C):
                    mm = nc.tensor.transpose(TB[1][:, c * P:(c + 1) * P], WO[:, c, :], ident[:])
                mm.then_inc(a1_wot_turned, 1)
                project_qkv(pe, i, a1, 3)
                pe.wait_ge(a1_wot, i + 1)
                self_pe(pe, i, a1, 1)
                pe.wait_ge(a1.o, i * 4 + 4 + 1)
                for t in range(T):
                    mm = nc.tensor.transpose(TB[0][:, t * P:(t + 1) * P], AT[:, t, :], ident[:])
                mm.then_inc(a1_turned, 1)
                pe.wait_ge(a1_att, i + 1)
                for t in range(T):
                    nc.tensor.matmul(S[t], ATT[:, t * P:(t + 1) * P], WOT[:], start=True, stop=True).then_inc(a1_y, 1)

            ln_pe(pe, 4, 2)
            pe.wait_ge(xt_low, C)
            with pe.Fori(0, KVH) as i:
                def project_q(t, bank):
                    for c in range(C):
                        x0 = t * P
                        mm = split_product(bank, XTH[:, c, x0:x0 + P], XTL[:, c, x0:x0 + P], WQP[:, 0, c, :],
                                           WQP[:, 1, c, :], c == 0, c == C - 1)
                    mm.then_inc(x_proj, 1)

                def turn(m, sources):
                    if m >= 2:
                        pe.wait_ge(x_trl, i * 7 + m - 1)
                    for k, src in enumerate(sources):
                        mm = nc.tensor.transpose(TB[m % 2][:, k * P:(k + 1) * P], src, ident[:])
                    mm.then_inc(x_turned, 1)

                def turn_q(t):
                    turn(3 + t, [QN[:, t, h * XD:(h + 1) * XD] for h in range(GQ)])

                def scores(g, h):
                    u, b = GQ * g + h, g // 2
                    if u == 0:
                        pe.wait_ge(x_vlo, i * 6 + 6)
                    elif u == 1:
                        pe.wait_ge(x_nat, i * 10 + 8)
                    else:
                        pe.wait_ge(x_exp, i * 16 + u)
                    if h == 0:
                        pe.wait_ge(x_trl, i * 7 + 4 + g)
                    qh, ql = QTP[:, 0, g, h * P:(h + 1) * P], QTP[:, 1, g, h * P:(h + 1) * P]
                    for k0, k1 in ((0, 512), (512, KEYS)):
                        mm = split_product(pair[u % 2][:, k0:k1], qh, ql, KTH[:, b * KEYS + k0:b * KEYS + k1],
                                           KTL[:, b * KEYS + k0:b * KEYS + k1], True, True)
                    mm.then_inc(x_sc, 1)

                def turn_probs(g, k):
                    m = KT_N * g + k
                    if k == 0:
                        pe.wait_ge(x_p, i * 16 + GQ * (g + 1))
                    if m >= 2:
                        s_of, n = turned_by(m - 2)
                        pe.wait_ge(s_of, i * (8 if s_of is x_pta else 16) + n)
                    for part, src in enumerate((PXH, PXL)):
                        for h in range(GQ):
                            o = part * 512 + h * P
                            mm = nc.tensor.transpose(TBb[m % 2][:, o:o + P], src[:, g % 2, h, k * P:(k + 1) * P],
                                                     identb[:])
                    mm.then_inc(x_pt, 1)

                def probs_v(g, k):
                    m = KT_N * g + k
                    if k == 0 and g > 0:
                        pe.wait_ge(x_ot, i * T + g + 1)
                    s_of, n = turned_by(m)
                    pe.wait_ge(s_of, i * (8 if s_of is x_pta else 16) + n)
                    kt = KT_N * (g // 2) + k
                    mm = split_product(OB[0][:], VH[:, kt, :], VL[:, kt, :], PXT[:, g % 2, k, 0:512],
                                       PXT[:, g % 2, k, 512:1024], k == 0, k == KT_N - 1)
                    if k == KT_N - 1:
                        mm.then_inc(x_pv, 1)

                def project_out(g, h):
                    if h == 0:
                        pe.wait_ge(x_ot, i * T + g + 2)
                        if g > 0:
                            pe.wait_ge(x_ya, i * T + g + 1)
                        else:
                            pe.wait_ge(x_so, i + 2)
                    mm = split_product(OB[1][:], OTP[:, 0, h * P:(h + 1) * P], OTP[:, 1, h * P:(h + 1) * P],
                                       WOP[:, 0, h, :], WOP[:, 1, h, :], h == 0, h == GQ - 1)
                    if h == GQ - 1:
                        mm.then_inc(x_y, 1)

                pe.wait_ge(x_exp, i * 16 + 1)
                pe.wait_ge(x_skv, i + 2)
                for n in range(6):
                    if n >= 4:
                        pe.wait_ge(x_vlo, i * 6 + n - 3)
                    for m in range(2):
                        kt = 2 * n + m
                        b, k = kt // KT_N, kt % KT_N
                        for c in range(C):
                            if k < CTX // P:
                                t0 = b * CTX + k * P
                                high, low = CXTH[:, c, t0:t0 + P], CXTL[:, c, t0:t0 + P]
                            else:
                                t0 = b * SEQ + (k - CTX // P) * P
                                high, low = XTH[:, c, t0:t0 + P], XTL[:, c, t0:t0 + P]
                            mm = split_product(S[n % 4][:, m * 2 * XD:(m + 1) * 2 * XD], high, low, WKVP[:, 0, c, :],
                                               WKVP[:, 1, c, :], c == 0, c == C - 1)
                    mm.then_inc(x_proj, 1)
                pe.wait_ge(x_sq_w, i + 2)
                for t in range(2):
                    pe.wait_ge(x_vlo, i * 6 + 3 + t)
                    project_q(t, S[2 + t])
                for m in range(3):
                    pe.wait_ge(x_kn, i * 12 + 4 * m + 4)
                    turn(m, [KN[:, 4 * m + k, :] for k in range(4)])
                pe.wait_ge(x_nat, i * 10 + 7)
                turn_q(0)
                scores(0, 0)
                scores(0, 1)
                pe.wait_ge(x_ot, i * T + 1)
                project_q(2, OB[0][:])
                scores(0, 2)
                pe.wait_ge(x_ya, i * T + 1)
                project_q(3, OB[1][:])
                scores(0, 3)
                for t in range(1, T):
                    pe.wait_ge(x_nat, i * 10 + 7 + t)
                    turn_q(t)
                pe.wait_ge(x_trl, i * 7 + 7)
                for g in range(T):
                    for k in range(KT_N):
                        turn_probs(g, k)
                        if g + 1 < T and k < GQ:
                            scores(g + 1, k)
                        if g > 0 and k >= 2:
                            project_out(g - 1, k - 2)
                        if k >= 1:
                            probs_v(g, k - 1)
                    probs_v(g, KT_N - 1)
                for h in range(GQ):
                    project_out(T - 1, h)

            pe.wait_ge(g_in, 16 * (3 + C))
            for m in range(9):
                if m >= 2:
                    pe.wait_ge(g_wt, m - 1)
                for o in range(C):
                    if m < 4:
                        mm = nc.tensor.transpose(TB[m % 2][:, o * P:(o + 1) * P], CX[:, o, m * P:(m + 1) * P], ident[:])
                    elif m < 8 and o == 0:
                        c = m - 4
                        nc.tensor.transpose(TB[m % 2][:, 0:P], AW[:, c * P:(c + 1) * P], ident[:])
                        mm = nc.tensor.transpose(TB[m % 2][:, P:P + ROUTES], RW[:, c * P:(c + 1) * P],
                                                 ident[0:ROUTES, 0:ROUTES])
                    elif m == 8:
                        mm = nc.tensor.transpose(TB[0][:, o * P:(o + 1) * P], BW[:, o].rearrange("p e r -> p (e r)"),
                                                 ident[:])
                mm.then_inc(g_turned, 1)
            ln_pe(pe, 5, 3)
            xt_ready(pe, 2)
            pe.wait_ge(g_wt, 9)
            for t in range(T):
                for c in range(C):
                    mm = nc.tensor.matmul(OB[1][:, t * 16:t * 16 + ROUTES], XT[:, c, t * P:(t + 1) * P],
                                          RT[:, c, P:P + ROUTES], start=(c == 0), stop=(c == C - 1))
            mm.then_inc(g_lg, 1)
            for c in range(C):
                mm = nc.tensor.matmul(OB[0][:], RT[:, c, 0:P], XT[:, c, :], start=(c == 0), stop=(c == C - 1))
            mm.then_inc(g_h, 1)
            for t in range(T):
                for c in range(C):
                    nc.tensor.matmul(S[t], XT[:, c, t * P:(t + 1) * P], F1T[:, c, :], start=(c == 0), stop=False)
            pe.wait_ge(g_sel, 1)
            for t in range(T):
                mm = nc.tensor.transpose(TB[0][0:ROUTES, t * P:(t + 1) * P], selp[:, t, 0:ROUTES], ident[:])
            mm.then_inc(g_selturned, 1)
            pe.wait_ge(g_selT, 1)
            pe.wait_ge(g_oexp, 2)
            nc.tensor.matmul(TB[1][:], oexp[:], selT[:], start=True, stop=True).then_inc(g_w, 1)
            pe.wait_ge(g_hT, 1)
            for t in range(T):
                nc.tensor.matmul(S[t], hT[:, t * P:(t + 1) * P], BT[:], start=False, stop=True).then_inc(g_y, 1)

        @block.scalar
        def _(act):
            def turned_weights(i, s, nw):
                k = nw - nw // 2
                for m in range(0, nw, 2):
                    act.wait_ge(s.w_turned, i * nw + m + 2)
                    nc.scalar.copy(WT[:, m].rearrange("p c f -> p (c f)"), TB[0][:]).then_inc(s.wt_act, 1)

            act.sem_inc(x_exp, 1)
            ln_act(act, 0)
            with act.Fori(0, 2) as i:
                turned_weights(i, a0, 4)
                self_act(act, i, a0, 2, SCALE0)
            act.wait_ge(ctx_q, 3)
            for k in range(CT):
                act.wait_ge(ctx_turned, k + 1)
                nc.scalar.copy(CXTH[:, :, k * P:(k + 1) * P], TB[k % 2][:].rearrange("p (c n) -> p c n", c=C)
                               ).then_inc(cxt_high, 1)
            for c in range(C):
                act.wait_ge(m0_turned, c + 1)
                nc.scalar.copy(XQT[:, c, :], Sb[c][:, 0:512]).then_inc(m0_xqt, 1)
            for c in range(C):
                act.wait_ge(f0_wturned, c + 1)
                nc.scalar.copy(WQT[:, c, :], TBb[c % 2][:, 0:512]).then_inc(f0_wqt, 1)
            for t in range(T):
                act.wait_ge(ln_norm, 2 * T + t + 1)
                nc.scalar.activation(G[:, t, :], XN[:, t, :], ACT.Square, accum_out=msq0[:, t:t + 1]).then_inc(f0_sq, 1)
            for c in range(C):
                act.wait_ge(f0_turned, c + 1)
                nc.scalar.copy(XQT[:, c, :], Sb[c][:, 0:512]).then_inc(f0_xqt, 1)
            for t in range(T):
                act.wait_ge(f0_y, t + 1)
                nc.scalar.activation(G[:, t, :], TMP[:, t, :], ACT.Gelu).then_inc(f0_gelu, 1)

            ln_act(act, 1)
            act.wait_ge(a1_rows, 2)
            with act.Fori(0, C) as i:
                turned_weights(i, a1, 3)
                self_act(act, i, a1, 1, SCALE1)
                act.wait_ge(a1_turned, i + 1)
                nc.scalar.copy(ATT[:], TB[0][:]).then_inc(a1_att, 1)

            ln_split_act(act, 2)
            with act.Fori(0, KVH) as i:
                def natural(n):
                    act.wait_ge(x_proj, i * 10 + n + 2)
                    if n < 6:
                        kv = S[n % 4].rearrange("p (k d) -> p k d", k=2)
                        nc.scalar.copy(KN[:, 2 * n:2 * n + 2, :], kv[:, :, 0:XD])
                        nc.scalar.copy(VH[:, 2 * n:2 * n + 2, :], kv[:, :, XD:2 * XD]).then_inc(x_nat, 1)
                    else:
                        nc.scalar.copy(QN[:, n - 6, :], (S[2], S[3], OB[0][:], OB[1][:])[n - 6]).then_inc(x_nat, 1)

                def turned_high(m):
                    act.wait_ge(x_turned, i * 7 + m + 1)
                    if m < 3:
                        nc.scalar.activation(KTH[:, m * 512:(m + 1) * 512], TB[m % 2][:], ACT.Copy,
                                             scale=wqk[:, 0:1]).then_inc(x_tr, 1)
                    else:
                        nc.scalar.copy(QTP[:, 0, m - 3, :], TB[m % 2][:]).then_inc(x_tr, 1)

                def exps(u):
                    act.wait_ge(x_nb, i * 16 + u + 1)
                    if u >= 4:
                        act.wait_ge(x_p, i * 16 + u - 3)
                    nc.scalar.activation(PX[:, u % 4, :], pair[u % 2][:, 0:KEYS], ACT.Exp, bias=xnb[:, u:u + 1],
                                         scale=cq[:, 0, u:u + 1], accum_out=xsum[:, u:u + 1]).then_inc(x_exp, 1)

                def probs_high(u):
                    g, h = u // GQ, u % GQ
                    act.wait_ge(x_ri, i * 16 + u + 1)
                    if h == 0 and g >= 2:
                        act.wait_ge(x_pt, i * 24 + KT_N * (g - 1))
                    nc.scalar.activation(PXH[:, g % 2, h, :], PX[:, u % 4, :], ACT.Copy,
                                         scale=xri[:, u:u + 1]).then_inc(x_phi, 1)

                for n in range(8):
                    natural(n)
                for m in range(4):
                    turned_high(m)
                exps(0)
                exps(1)
                natural(8)
                probs_high(0)
                exps(2)
                natural(9)
                probs_high(1)
                exps(3)
                turned_high(4)
                probs_high(2)
                turned_high(5)
                probs_high(3)
                turned_high(6)
                for g in range(T):
                    for k in range(KT_N):
                        m = KT_N * g + k
                        if m % 3 == 2:
                            act.wait_ge(x_pt, i * 24 + m + 1)
                            nc.scalar.copy(PXT[:, g % 2, k, :], TBb[m % 2]).then_inc(x_pta, 1)
                        if g + 1 < T and k < GQ:
                            exps(GQ * (g + 1) + k)
                        if g + 1 < T and 1 <= k <= GQ:
                            probs_high(GQ * (g + 1) + k - 1)
                    act.wait_ge(x_pv, i * T + g + 1)
                    nc.scalar.copy(OTP[:, 0, :], OB[0][:]).then_inc(x_oth, 1)

            for m in range(9):
                act.wait_ge(g_turned, m + 1)
                if m < 4:
                    nc.scalar.copy(F1T[:, m, :], TB[m % 2][:]).then_inc(g_wt, 1)
                elif m < 8:
                    nc.scalar.copy(RT[:, m - 4, 0:P + ROUTES], TB[m % 2][:, 0:P + ROUTES]).then_inc(g_wt, 1)
                else:
                    nc.scalar.copy(BT[:], TB[0][:]).then_inc(g_wt, 1)
            ln_act(act, 3)
            act.wait_ge(g_lgd, 2)
            for t in range(T):
                nc.scalar.activation(pr[:, t, 0:ROUTES], lg[:, t, :], ACT.Exp, bias=lmx[:, t:t + 1],
                                     accum_out=lsum[:, t:t + 1]).then_inc(g_exp, 1)
            act.wait_ge(g_selturned, 1)
            nc.scalar.copy(selT[:], TB[0][0:ROUTES, :]).then_inc(g_selT, 1)
            act.wait_ge(g_w, 1)
            nc.scalar.mul(wexp[:], TB[1][:], 2.0).then_inc(g_wexp, 1)

        @block.vector
        def _(dve):
            for s in (a0.nat, a0.o, a1.nat, a1.o, a1_yadd, x_ya, x_sq, x_ot):
                dve.sem_inc(s, 1)
            steps = Steps(dve, dve_step)
            dve.wait_ge(consts, NCONST)
            dve.wait_ge(x_in, 16)
            ln_dve(dve, 0)
            ln_copy_dve(dve, 0)
            dve.wait_ge(m0_in, 64)
            steps(nc.vector.reciprocal(qsr[:, 0:1], qs[:, 0:1]))
            nc.vector.reciprocal(qsr[:, 1:2], qs[:, 2:3]).then_inc(qs_ready, 1)
            steps(nc.vector.tensor_scalar(qc[:, 0:1], qs[:, 1:2], -1.0, 128.0, ALU.mult, ALU.add))
            steps(nc.vector.tensor_scalar(qc[:, 3:4], qs[:, 3:4], -1.0, 128.0, ALU.mult, ALU.add))
            steps(nc.vector.tensor_scalar(qc[:, 1:2], qc[:, 0:1], qc[:, 3:4], float(D), ALU.mult, ALU.mult))
            steps(nc.vector.tensor_tensor(qc[:, 2:3], qs[:, 0:1], qs[:, 2:3], ALU.mult))
            dve.wait_ge(fw_in, 16)
            nc.vector.tensor_reduce(wab[:], FW[:], AX.XY, ALU.add, apply_absolute_value=True).then_inc(f0_wabs, 1)
            alb = albf[:, 0, :].rearrange("p (t h) -> p t h", h=HG)
            for j in range(HG):
                slope = float(np.float32(1.0) / np.power(np.float32(2.0), np.float32((j + 1) * 8.0 / 32)))
                nc.vector.tensor_scalar(alb[:, :, j], posk[:], slope, None, ALU.mult).then_inc(a1_albi, 1)
            dve.wait_ge(a1_albi, HG)
            for part in range(3):
                steps(nc.vector.tensor_copy(albb[:, part, :], albf[:, 0, :]))
                steps(nc.vector.tensor_tensor(albf[:, 0, :], albf[:, 0, :], albb[:, part, :], ALU.subtract))

            def turned_weights(i, s, nw):
                for m in range(1, nw, 2):
                    dve.wait_ge(s.w_turned, i * nw + m + 2)
                    nc.vector.tensor_copy(WT[:, m].rearrange("p c f -> p (c f)"), TB[1][:]).then_inc(s.wt_dve, 1)

            def into_x(i, a, t, done, steps, o, r):
                steps(nc.vector.tensor_tensor(osc[:].rearrange("p (h d) -> p h d", h=HG), o, r, ALU.mult))
                dve.wait_ge(a0.o, done + 1)
                dst = X[:, t, :].rearrange("p (a i f) -> p a i f", a=2, i=2)[:, a, i, :]
                return nc.vector.tensor_tensor(dst, dst, osc[:], ALU.add)

            with dve.Fori(0, 2) as i:
                turned_weights(i, a0, 4)
                self_dve(dve, i, a0, 2, SCALE0, into_x)
            dve.wait_ge(a0.o, 17)

            dve.wait_ge(f0_wtot, 1)
            steps(nc.vector.tensor_scalar(wsc[:, 0:1], OB[1][:, 0:1], 1.0 / (D * D), 1e-5, ALU.mult, ALU.max))
            nc.vector.reciprocal(wsc[:, 1:2], wsc[:, 0:1]).then_inc(f0_wscale, 1)
            def context_low(ks):
                for k in ks:
                    dve.wait_ge(cxt_high, k + 1)
                    nc.vector.tensor_tensor(CXTL[:, :, k * P:(k + 1) * P], TB[k % 2][:].rearrange("p (c n) -> p c n", c=C),
                                            CXTH[:, :, k * P:(k + 1) * P], ALU.subtract).then_inc(cxt_ready, 1)

            ln_dve(dve, 1)
            dve.wait_ge(ln_norm, 2 * T)
            for t in range(T):
                nc.vector.tensor_scalar(TMP[:, t, :], XN[:, t, :], qsr[:, 0:1], qs[:, 1:2], ALU.mult,
                                        ALU.add).then_inc(quant, 1)
            for t in range(T):
                dve.wait_ge(quant, t + 1)
                nc.vector.tensor_scalar(TMP[:, t, :], TMP[:, t, :], 0.0, 255.0, ALU.max, ALU.min).then_inc(quant, 1)
            for t in range(T):
                dve.wait_ge(quant, T + t + 1)
                nc.vector.tensor_scalar(XQ[:, t, :], TMP[:, t, :], ROUND, ROUND + 128.0, ALU.add,
                                        ALU.subtract).then_inc(m0_norm, 1)
            context_low(range(CT))
            for b in range(NB):
                dve.wait_ge(m0_col, b + 1)
                nc.vector.tensor_scalar(colr[0:1, b, :], TB[b][0:1, :], qc[0:1, 0:1], qc[0:1, 1:2], ALU.mult,
                                        ALU.add).then_inc(m0_colr, 1)
            dve.wait_ge(m0_col, NB + 1)
            steps(nc.vector.tensor_scalar(rowc[:], OB[0][:, 0:T], qc[:, 3:4], None, ALU.mult))
            for t in range(T):
                dve.wait_ge(m0_prod, t + 1)
                nc.vector.tensor_scalar(TMP[:, t, :], S[t], rowc[:, t:t + 1], qc[:, 2:3], ALU.add,
                                        ALU.mult).then_inc(m0_y, 1)
                dve.wait_ge(m0_y, 2 * t + 1)
                nc.vector.tensor_tensor(X[:, t, :], X[:, t, :], TMP[:, t, :], ALU.add).then_inc(m0_y, 1)
            dve.wait_ge(m0_y, 2 * T)

            ln_dve(dve, 2)
            for t in range(T):
                dve.wait_ge(ln_norm, 2 * T + t + 1)
                nc.vector.tensor_reduce(mab[:, t:t + 1], XN[:, t, :], AX.X, ALU.max,
                                        apply_absolute_value=True).then_inc(f0_mab, 1)
            dve.wait_ge(f0_sq, T)
            nc.vector.tensor_scalar(msq[:], msq0[:], 1.0 / D, 1e-5, ALU.mult, ALU.add).then_inc(f0_ms, 1)
            dve.wait_ge(f0_rms, 1)
            dve.wait_ge(f0_mab, T)
            steps(nc.vector.tensor_tensor(amx[:], mab[:], rrs[:], ALU.mult))
            steps(nc.vector.tensor_scalar(amx[:], amx[:], 1e-5, None, ALU.max))
            steps(nc.vector.reciprocal(ascl[:], amx[:]))
            steps(nc.vector.tensor_scalar(ascl[:], ascl[:], 127.0, None, ALU.mult))
            steps(nc.vector.tensor_scalar(adq[:], amx[:], 1.0 / 127.0, wsc[:, 0:1], ALU.mult, ALU.mult))
            for t in range(T):
                nc.vector.tensor_scalar(TMP[:, t, :], XN[:, t, :], rrs[:, t:t + 1], ascl[:, t:t + 1], ALU.mult,
                                        ALU.mult).then_inc(quant, 1)
            for t in range(T):
                dve.wait_ge(quant, 2 * T + t + 1)
                nc.vector.tensor_scalar(TMP[:, t, :], TMP[:, t, :], -128.0, 127.0, ALU.max, ALU.min).then_inc(quant, 1)
            for t in range(T):
                dve.wait_ge(quant, 3 * T + t + 1)
                nc.vector.tensor_scalar(XQ[:, t, :], TMP[:, t, :], ROUND, ROUND, ALU.add,
                                        ALU.subtract).then_inc(f0_q, 1)
            dve.wait_ge(f0_bin, 16)
            for t in range(T):
                dve.wait_ge(f0_prod, t + 1)
                nc.vector.scalar_tensor_tensor(out=TMP[:, t, :], in0=S[t], scalar=adq[:, t:t + 1], in1=fb[:],
                                               op0=ALU.mult, op1=ALU.add).then_inc(f0_y, 1)
            for t in range(T):
                dve.wait_ge(f0_gelu, t + 1)
                nc.vector.tensor_tensor(G[:, t, :], G[:, t, :], XN[:, t, :], ALU.add).then_inc(f0_x1, 1)
                dve.wait_ge(f0_x1, 2 * t + 1)
                nc.vector.tensor_tensor(X[:, t, :], X[:, t, :], G[:, t, :], ALU.add).then_inc(f0_x1, 1)
            dve.wait_ge(f0_x1, 2 * T)

            def add_bias(row, done, n):
                dve.wait_ge(ln_norm, (n + 1) * T)
                for t in range(T):
                    nc.vector.tensor_tensor(X[:, t, :], X[:, t, :], row[:], ALU.add).then_inc(done, 1)
                dve.wait_ge(done, T)

            ln_dve(dve, 3)
            ln_copy_dve(dve, 1)
            dve.wait_ge(a1_boutin, 16)
            add_bias(boutb, a1_badd, 3)

            def into_at(i, a, t, done, steps, o, r):
                return nc.vector.tensor_tensor(AT[:, t, :].rearrange("p (h d) -> p h d", h=HG), o, r, ALU.mult)

            ke_rows = KE.rearrange("p t (h e) -> p (t h) e", h=HG)[:, :, ALI:ALI + 3]
            dve.wait_ge(a1_rows, 2)
            for part in range(3):
                nc.vector.tensor_copy(ke_rows[:, :, part], albb[:, part, :]).then_inc(a1_albi, 1)
            dve.wait_ge(a1_albi, HG + 3)
            with dve.Fori(0, C) as i:
                turned_weights(i, a1, 3)
                dve.wait_ge(a1_wot_turned, i + 2)
                nc.vector.tensor_copy(WOT[:], TB[1][:]).then_inc(a1_wot, 1)
                self_dve(dve, i, a1, 1, SCALE1, into_at)
                nc.vector.tensor_scalar(ke_rows, ke_rows, 0.25, None, ALU.mult).then_inc(a1_albi, 1)
                for t in range(T):
                    dve.wait_ge(a1_y, i * T + t + 1)
                    dve.wait_ge(a1_yadd, i * T + t + 1)
                    nc.vector.tensor_tensor(X[:, t, :], X[:, t, :], S[t], ALU.add).then_inc(a1_yadd, 1)
            dve.wait_ge(a1_yadd, C * T + 1)

            dve.wait_ge(x1_nin, 32)
            nc.vector.tensor_tensor(wqk[:], wn[:, 0:1], wn[:, 1:2], ALU.mult).then_inc(x_wqk, 1)
            ln_dve(dve, 4)
            ln_split_dve(dve, 2)
            NQ, NK = T * GQ, NB * KT_N
            with dve.Fori(0, KVH) as i:
                steps_x = Steps(dve, x_steps, i * (4 + 16))

                def squares(n, src):
                    dve.wait_ge(x_sq, i * (NK + NQ) + max(n - 1, 0) + 1)
                    nc.vector.tensor_tensor_reduce(out=SQJ[:, n % 2, :], in0=src, in1=src, scale=1.0, scalar=0.0,
                                                   op0=ALU.mult, op1=ALU.add, accum_out=ssx[:, n:n + 1]
                                                   ).then_inc(x_sq, 1)

                def mean_squares(a, b):
                    dve.wait_ge(x_sq, i * (NK + NQ) + b + 1)
                    nc.vector.tensor_scalar(ssx[:, a:b], ssx[:, a:b], 1.0 / XD, 1e-6, ALU.mult, ALU.add
                                            ).then_inc(x_ms, 1)

                def q_squares(t):
                    dve.wait_ge(x_nat, i * 10 + 7 + t)
                    for h in range(GQ):
                        squares(NK + GQ * t + h, QN[:, t, h * XD:(h + 1) * XD])

                def q_factors(a, b):
                    for sign in range(2):
                        steps_x(nc.vector.tensor_scalar(cq[:, sign, a:b], rx[:, NK + a:NK + b],
                                                        (1 - 2 * sign) * float(XD) ** -0.5, None, ALU.mult))

                def turned_low(m):
                    dve.wait_ge(x_tr, i * 7 + m + 1)
                    if m < 3:
                        ks = slice(m * 512, (m + 1) * 512)
                        nc.vector.scalar_tensor_tensor(out=KTL[:, ks], in0=TB[m % 2][:], scalar=wqk[:, 0:1],
                                                       in1=KTH[:, ks], op0=ALU.mult, op1=ALU.subtract).then_inc(x_trl, 1)
                    else:
                        nc.vector.tensor_tensor(QTP[:, 1, m - 3, :], TB[m % 2][:], QTP[:, 0, m - 3, :],
                                                ALU.subtract).then_inc(x_trl, 1)

                def row_max(u):
                    dve.wait_ge(x_sc, i * 16 + u + 1)
                    steps_x(nc.vector.tensor_reduce(xmx[:, u:u + 1], pair[u % 2][:, 0:KEYS], AX.X, ALU.max))
                    nc.vector.tensor_tensor(xnb[:, u:u + 1], xmx[:, u:u + 1], cq[:, 1, u:u + 1],
                                            ALU.mult).then_inc(x_nb, 1)

                def invert_sum(u):
                    dve.wait_ge(x_exp, i * 16 + u + 2)
                    nc.vector.reciprocal(xri[:, u:u + 1], xsum[:, u:u + 1]).then_inc(x_ri, 1)

                def probs_low(u):
                    g, h = u // GQ, u % GQ
                    dve.wait_ge(x_phi, i * 16 + u + 1)
                    dve.wait_ge(x_ri, i * 16 + u + 1)
                    nc.vector.scalar_tensor_tensor(out=PXL[:, g % 2, h, :], in0=PX[:, u % 4, :], scalar=xri[:, u:u + 1],
                                                   in1=PXH[:, g % 2, h, :], op0=ALU.mult, op1=ALU.subtract
                                                   ).then_inc(x_p, 1)

                for n in range(6):
                    dve.wait_ge(x_nat, i * 10 + n + 1)
                    nc.vector.tensor_tensor(VL[:, 2 * n:2 * n + 2, :],
                                            S[n % 4].rearrange("p (k d) -> p k d", k=2)[:, :, XD:2 * XD],
                                            VH[:, 2 * n:2 * n + 2, :], ALU.subtract).then_inc(x_vlo, 1)
                    squares(2 * n, KN[:, 2 * n, :])
                    squares(2 * n + 1, KN[:, 2 * n + 1, :])
                mean_squares(0, NK)
                q_squares(0)
                mean_squares(NK, NK + GQ)
                dve.wait_ge(x_r, 3 * i + 1)
                for k in range(NK):
                    nc.vector.tensor_scalar(KN[:, k, :], KN[:, k, :], rx[:, k:k + 1], None, ALU.mult).then_inc(x_kn, 1)
                q_squares(1)
                dve.wait_ge(x_r, 3 * i + 2)
                q_factors(0, GQ)
                for m in range(4):
                    turned_low(m)
                row_max(0)
                row_max(1)
                invert_sum(0)
                q_squares(2)
                row_max(2)
                invert_sum(1)
                probs_low(0)
                q_squares(3)
                mean_squares(NK + GQ, NK + NQ)
                row_max(3)
                invert_sum(2)
                probs_low(1)
                turned_low(4)
                invert_sum(3)
                probs_low(2)
                turned_low(5)
                probs_low(3)
                dve.wait_ge(x_r, 3 * i + 3)
                q_factors(GQ, NQ)
                turned_low(6)
                for g in range(T):
                    for k in range(KT_N):
                        m = KT_N * g + k
                        if m % 3 != 2:
                            dve.wait_ge(x_pt, i * 24 + m + 1)
                            nc.vector.tensor_copy(PXT[:, g % 2, k, :].bitcast(F32), TB[m % 2][:]).then_inc(x_ptv, 1)
                        if g + 1 < T:
                            u = GQ * (g + 1)
                            if k < GQ:
                                row_max(u + k)
                            if 1 <= k <= GQ:
                                invert_sum(u + k - 1)
                            if k >= 2:
                                probs_low(u + k - 2)
                    dve.wait_ge(x_oth, i * T + g + 1)
                    nc.vector.tensor_tensor(OTP[:, 1, :], OB[0][:], OTP[:, 0, :], ALU.subtract).then_inc(x_ot, 1)
                    if g > 0:
                        dve.wait_ge(x_y, i * T + g + 1)
                        dve.wait_ge(x_ya, i * T + g)
                        nc.vector.tensor_tensor(X[:, g - 1, :], X[:, g - 1, :], OB[1][:], ALU.add).then_inc(x_ya, 1)
                dve.wait_ge(x_y, i * T + T + 1)
                dve.wait_ge(x_ya, i * T + T)
                nc.vector.tensor_tensor(X[:, T - 1, :], X[:, T - 1, :], OB[1][:], ALU.add).then_inc(x_ya, 1)
            dve.wait_ge(x_ya, KVH * T + 1)

            ln_dve(dve, 5)
            ln_copy_dve(dve, 3)
            dve.wait_ge(f1_bin, 32)
            nc.vector.tensor_copy(mapf[:], mapi[:]).then_inc(g_oexp, 1)
            dve.wait_ge(g_oexp, 1)
            nc.vector.tensor_scalar(oexp[:], expi[:].rearrange("i e r -> i (e r)"), mapf[:, 0:1], None,
                                    ALU.is_equal).then_inc(g_oexp, 1)
            dve.wait_ge(g_lg, 1)
            nc.vector.tensor_tensor(lg[:], OB[1][:, 0:16 * T].rearrange("p (t n) -> p t n", t=T)[:, :, 0:ROUTES],
                                    rbb[:].unsqueeze(1).to_broadcast([P, T, ROUTES]), ALU.add).then_inc(g_lgd, 1)
            dve.wait_ge(g_lgd, 1)
            nc.vector.tensor_reduce(lmx[:], lg[:], AX.X, ALU.max, negate=True).then_inc(g_lgd, 1)
            dve.wait_ge(g_exp, T)
            steps(nc.vector.reciprocal(lsum[:], lsum[:]))
            steps(nc.vector.tensor_tensor(pr[:, :, 0:ROUTES], pr[:, :, 0:ROUTES],
                                          lsum[:].unsqueeze(2).to_broadcast([P, T, ROUTES]), ALU.mult))
            for t in range(T):
                steps(nc.vector.max(top8[:, t, :], pr[:, t, 0:ROUTES]))
                steps(nc.vector.match_replace(rep[:, t, 0:ROUTES], top8[:, t, :], pr[:, t, 0:ROUTES], -1.0))
            nc.vector.scalar_tensor_tensor(out=selp[:, :, 0:ROUTES], in0=rep[:, :, 0:ROUTES], scalar=0.0,
                                           in1=pr[:, :, 0:ROUTES], op0=ALU.is_lt, op1=ALU.mult).then_inc(g_sel, 1)
            dve.wait_ge(f1_base_in, 16)
            add_bias(f1b, f1_bdone, 5)
            dve.wait_ge(g_wexp, 1)
            dve.wait_ge(g_h, 1)
            nc.vector.tensor_tensor(hT[:], OB[0][:], wexp[:], ALU.mult).then_inc(g_hT, 1)
            for t in range(T):
                dve.wait_ge(g_y, t + 1)
                nc.vector.tensor_tensor(X[:, t, :], X[:, t, :], S[t], ALU.add).then_inc(g_out, 1)


_INS = ['x', 'ctx_4096', 'L0_attn_Wq', 'L0_attn_bq', 'L0_attn_Wk', 'L0_attn_bk', 'L0_attn_Wv', 'L0_attn_bv',
        'L0_xattn_x1_scale', 'L0_xattn_x1_zp', 'L0_xattn_x2_scale', 'L0_xattn_x2_zp', 'L0_ffn_W', 'L0_ffn_b',
        'L1_attn_w_qkv', 'L1_attn_b_qkv', 'L1_attn_w_out', 'L1_attn_b_out', 'L1_xattn_Wq', 'L1_xattn_Wk',
        'L1_xattn_Wv', 'L1_xattn_Wo', 'L1_xattn_q_norm_w', 'L1_xattn_k_norm_w', 'L1_ffn_base_W', 'L1_ffn_base_b',
        'L1_ffn_router_W', 'L1_ffn_router_b', 'L1_ffn_A', 'L1_ffn_B', 'L1_ffn_expert_map']


def kernel(**inputs):
    import numpy as _np
    import concourse.bacc as _bacc
    from concourse import mybir as _mybir
    from concourse.bass_utils import run_bass_kernel_spmd as _run

    nc = _bacc.Bacc("TRN2", target_bir_lowering=False, num_devices=1)
    arrays, args = {}, []
    for name in _INS:
        a = _np.ascontiguousarray(inputs[name])
        arrays[f"in_{name}"] = a
        args.append(nc.dram_tensor(f"in_{name}", a.shape, _mybir.dt.from_np(a.dtype), kind="ExternalInput").ap())
    out = nc.dram_tensor("out_0", (2, 256, 512), _mybir.dt.float32, kind="ExternalOutput").ap()
    decoder_program(nc, *args, out)
    r = _run(nc, [arrays], core_ids=[0])
    return r.results[0]["out_0"]
```

```python
from contextlib import ExitStack

import numpy as np

import concourse.bass as bass
from concourse import mybir

F32 = mybir.dt.float32
BF16 = mybir.dt.bfloat16
I32 = mybir.dt.int32
ALU = mybir.AluOpType
ACT = mybir.ActivationFunctionType
AX = mybir.AxisListType

P = 128
D = 512
NB = 2
SEQ = 256
T = NB * SEQ // P
C = D // P
CTX = 512
CT = NB * CTX // P
HD = 16
HG = P // HD
SCALE0 = float(1.0 / np.sqrt(np.float32(32)))
SCALE1 = 0.25
LN_EPS = 1e-5
ROUND = 12582912.0
NEG = -1.0e30

XD = 128
KVH = 8
GQ = 4
KT_N = (CTX + SEQ) // P
KEYS = KT_N * P

NE = 8
RANK = 16
ROUTES = 2 * NE - 1


def decoder_program(
    nc, x, ctx_4096, a0_wq, a0_bq, a0_wk, a0_bk, a0_wv, a0_bv, m0_s1, m0_z1, m0_s2, m0_z2, f0_w, f0_b,
    a1_wqkv, a1_bqkv, a1_wout, a1_bout, x1_wq, x1_wk, x1_wv, x1_wo, x1_qn, x1_kn,
    f1_w, f1_b, f1_rw, f1_rb, f1_a, f1_bm, f1_map, out,
):
    ctx = ExitStack()

    def sb(name, shape, dt=F32):
        return ctx.enter_context(nc.sbuf_tensor(name, shape, dt))

    def sem(name):
        return ctx.enter_context(nc.semaphore(name))

    with ctx:
        X = sb("X", [P, T, D])
        XN = sb("XN", [P, T, D])
        XT = sb("XT", [P, C, T * P])
        CX = sb("CX", [P, CT, D])
        CXT = sb("CXT", [P, C, CT * P])

        shared = sb("shared", [P, 4 * KEYS + 2 * GQ * KEYS * 2])

        def shared_f32(at, n, **kw):
            return shared[:, at:at + n].rearrange("p (a b) -> p a b", **kw)

        def shared_bf16(at, n, **kw):
            return shared[:, at:at + n // 2].bitcast(BF16).rearrange("p (a b) -> p a b", **kw)

        TMP = shared_f32(0, T * D, a=T)
        G = shared_f32(2048, T * D, a=T)
        FW = shared_f32(4096, C * D, a=C)
        CXQ = shared_bf16(6144, CT * D, a=CT)
        XQ = shared_bf16(8192, T * D, a=T)
        XQT = shared_bf16(9216, C * T * P, a=C)
        WQT = shared_bf16(10240, C * D, a=C)
        WQN = shared_bf16(11264, C * D, a=C)
        PX = shared[:, 0:4 * KEYS].rearrange("p (s k) -> p s k", s=4)
        PXH = shared_bf16(3072, 8 * KEYS, a=8).rearrange("p (s h) k -> p s h k", s=2)
        PXL = shared_bf16(6144, 8 * KEYS, a=8).rearrange("p (s h) k -> p s h k", s=2)
        PXT = shared_bf16(9216, 12 * 1024, a=12).rearrange("p (s k) q -> p s k q", s=2)
        XTH = XT[:, 0:2, :].bitcast(BF16).rearrange("p a (b t) -> p (a b) t", b=2)
        XTL = XT[:, 2:4, :].bitcast(BF16).rearrange("p a (b t) -> p (a b) t", b=2)
        CXTH = CXT[:, 0:2, :].bitcast(BF16).rearrange("p a (b t) -> p (a b) t", b=2)
        CXTL = CXT[:, 2:4, :].bitcast(BF16).rearrange("p a (b t) -> p (a b) t", b=2)

        ident = sb("ident", [P, P])
        identb = sb("identb", [P, P], BF16)
        ones = sb("ones", [P, P])
        onesb = sb("onesb", [P, 1], BF16)
        maskq = sb("maskq", [P, 2 * P], BF16)
        maskk = sb("maskk", [P, 3 * P], BF16)
        neghalf = sb("neghalf", [P, 32])
        lnst = sb("lnst", [P, T, 6])
        lnmv = sb("lnmv", [P, T, 2])
        lnve = sb("lnve", [P, T])
        lnrs = sb("lnrs", [P, T])

        W0 = sb("W0", [P, 4, D])
        WT = sb("WT", [P, 4, C, P])
        WO = sb("WO", [P, C, P])
        WOT = sb("WOT", [P, D])
        brow = sb("brow", [P, 4 * P])
        EXT = 64
        KHI, KLO, QLO, ALI, MAX = 0, HD, 2 * HD, 3 * HD, 3 * HD + 3
        ALB = sb("ALB", [P, HG, 2 * P])
        QE = ALB[:].rearrange("p h k -> p (h k)").bitcast(BF16).rearrange("p (a t e) -> p a t e", a=2, t=T)
        KQ = sb("KQ", [P, 4 * T * P])
        QR = KQ[:].bitcast(BF16).rearrange("p (g n) -> p g n", g=4)
        KE = shared_bf16(0, T * HG * EXT, a=T)
        KR = shared_bf16(1024, NB * 1024, a=NB)
        NAT = shared_f32(2048, 4 * T * P, a=4)
        VW = 2 * HD + 1
        VX = shared_bf16(8192, T * HG * (VW + 1), a=T * HG)
        osc = shared_f32(8192 + T * HG * (VW + 1) // 2, 2 * P, a=2)
        RING = 4
        WID = 3 * P
        units = sb("units", [P, RING * 2 * WID])
        PE32 = units[:].rearrange("p (r h k) -> p r h k", r=RING, h=2)
        PEH = shared_bf16(9216, RING * 2 * WID, a=RING * 2).rearrange("p (r h) k -> p r h k", r=RING)
        PEL = shared_bf16(9216 + RING * WID, RING * 2 * WID, a=RING * 2).rearrange("p (r h) k -> p r h k", r=RING)
        nmax = sb("nmax", [P, 4, 2, HG])
        rinv = sb("rinv", [P, 2, HG])
        olow = sb("olow", [P, 2, HG, HD])
        att = sb("att", [P, 2 * T * P])
        AT = att[:, 0:T * P].rearrange("p (t f) -> p t f", t=T)
        ATT = att[:, T * P:2 * T * P]
        posk = sb("posk", [P, T])
        albf = sb("albf", [P, 1, T * HG])
        albb = sb("albb", [P, 3, T * HG], BF16)

        qs = sb("qs", [P, 4])
        qsr = sb("qsr", [P, 2])
        qc = sb("qc", [P, 4])
        colr = sb("colr", [1, NB, D])
        rowc = sb("rowc", [P, T])
        fb = sb("fb", [P, D])
        boutb = sb("boutb", [P, D])
        wab = sb("wab", [P, 1])
        wsc = sb("wsc", [P, 2])
        msq0 = sb("msq0", [P, T])
        msq = sb("msq", [P, T])
        mab = sb("mab", [P, T])
        rrs = sb("rrs", [P, T])
        amx = sb("amx", [P, T])
        ascl = sb("ascl", [P, T])
        adq = sb("adq", [P, T])

        WKV = sb("WKV", [P, C, 2 * XD])
        WQ1 = W0
        WO1 = sb("WO1", [P, GQ, D])
        KN = units[:, 0:12 * XD].rearrange("p (k d) -> p k d", k=NB * KT_N)
        VH = units[:, 12 * XD:18 * XD].bitcast(BF16).rearrange("p (k d) -> p k d", k=NB * KT_N)
        VL = units[:, 18 * XD:24 * XD].bitcast(BF16).rearrange("p (k d) -> p k d", k=NB * KT_N)
        WKVP = att[:].bitcast(BF16).rearrange("p (s c d) -> p s c d", s=2, c=C)
        WQP = WT[:].rearrange("p m c f -> p (m c f)").bitcast(BF16).rearrange("p (s c d) -> p s c d", s=2, c=C)
        WOP = CX[:, 4:8, :].rearrange("p a d -> p (a d)").bitcast(BF16).rearrange("p (s h d) -> p s h d", s=2, h=GQ)
        QN = XN
        KTH = KQ[:, 0:NB * KEYS // 2].bitcast(BF16)
        KTL = KQ[:, NB * KEYS // 2:NB * KEYS].bitcast(BF16)
        QTP = ALB[:].rearrange("p h k -> p (h k)").bitcast(BF16).rearrange("p (s t q) -> p s t q", s=2, t=T)
        OTP = sb("OTP", [P, 2, GQ * P], BF16)
        SQJ = sb("SQJ", [P, 2, P])
        ssx = sb("ssx", [P, 32])
        rx = sb("rx", [P, 32])
        cq = sb("cq", [P, 2, T * GQ])
        wn = sb("wn", [P, 2])
        wqk = sb("wqk", [P, 1])
        xmx = sb("xmx", [P, T * GQ])
        xnb = sb("xnb", [P, T * GQ])
        xsum = sb("xsum", [P, T * GQ])
        xri = sb("xri", [P, T * GQ])

        RW = sb("RW", [ROUTES, D])
        AW = sb("AW", [P, D])
        BW = WO[:].rearrange("p c (e r) -> p c e r", e=NE)
        F1T = WT[:].rearrange("p m c f -> p m (c f)")
        RT = sb("RT", [P, C, P + 16])
        BT = units[:, 0:D]
        f1b = boutb
        rbb = sb("rbb", [P, ROUTES])
        mapi = sb("mapi", [ROUTES, 1], I32)
        mapf = sb("mapf", [ROUTES, 1])
        expi = sb("expi", [ROUTES, NE, RANK])
        oexp = sb("oexp", [ROUTES, NE * RANK])
        lg = sb("lg", [P, T, ROUTES])
        lmx = sb("lmx", [P, T])
        lsum = sb("lsum", [P, T])
        pr = sb("pr", [P, T, 16])
        top8 = sb("top8", [P, T, 8])
        rep = sb("rep", [P, T, 16])
        selp = sb("selp", [P, T, 16])
        selT = units[0:ROUTES, 3 * D:3 * D + T * P]
        wexp = units[:, D:D + T * P]
        hT = units[:, 2 * D:2 * D + T * P]

        pair = [ctx.enter_context(nc.psum_tensor(f"pair{i}", [P, 1024], F32)) for i in range(2)]
        S = [pair[0][:, 0:512], pair[0][:, 512:1024], pair[1][:, 0:512], pair[1][:, 512:1024]]
        TB = [ctx.enter_context(nc.psum_tensor(f"turn{i}", [P, 512], F32)) for i in range(2)]
        Sb, TBb = [s.bitcast(BF16) for s in S], [b[:].bitcast(BF16) for b in TB]
        OB = [ctx.enter_context(nc.psum_tensor(f"acc{i}", [P, 512], F32)) for i in range(2)]

        x_in, ctx_in, fw_in, out_done = sem("x_in"), sem("ctx_in"), sem("fw_in"), sem("out_done")
        consts = sem("consts")
        NCONST = 9
        zeroed, identb_done, qs_ready = sem("zeroed"), sem("identb_done"), sem("qscales_ready")
        ln_stat, ln_aggr, ln_var, ln_rstd, ln_norm = (sem(f"ln_{n}") for n in ("stat", "aggr", "var", "rstd", "norm"))
        ln_turned, xt_act, xt_dve = sem("ln_turned"), sem("xt_act"), sem("xt_dve")
        dve_step = sem("dve_step")
        ctx_turned, cxt_ready = sem("ctx_turned"), sem("cxt_ready")


        class Steps:

            def __init__(self, eng, s, base=0):
                self.eng, self.s, self.base, self.n = eng, s, base, 0

            def __call__(self, ins):
                self.mark(ins)
                self.wait()

            def mark(self, ins):
                self.n += 1
                ins.then_inc(self.s, 1)

            def wait(self):
                self.eng.wait_ge(self.s, self.base + self.n)

        LAG = 3

        AHEAD = {1: {(0, 0): ("weights", 0), (0, 1): ("weights", 1), (1, 0): ("weights", 2), (1, 1): ("project", 0),
                     (1, 2): ("project", 1), (1, 3): ("project", 2)},
                 2: {(0, 0): ("weights", 0), (0, 1): ("weights", 1), (1, 0): ("weights", 2), (1, 1): ("weights", 3),
                     (2, 0): ("project", 0), (2, 2): ("project", 1), (3, 0): ("project", 2), (3, 1): ("project", 3)}}

        def self_order(na, ahead=False):
            G, order, done = na * NB, [], 0
            order += [("max", g, r) for g in range(2) for r in range(3)]
            for g in range(G):
                order.append(("turn", g, 0))
                for j in range(HG // 2):
                    if g + 2 < G:
                        order += [("max", g + 2, r) for r in ((), (0, 1), (), (2,))[j]]
                    order.append(("exp", g, j))
                    if ahead:
                        order.append(AHEAD[na].get((g, j), ("none", 0)) + (0,))
                    if 4 * g + j >= LAG:
                        order.append(("pv", (4 * g + j - LAG) // 4, (4 * g + j - LAG) % 4))
            if ahead and na == 1:
                order.append(("project", 3, 0))
            return order + [("pv", q // 4, q % 4) for q in range(4 * G - LAG, 4 * G)]

        def fills(na):
            return [o for o in self_order(na) if o[0] in ("max", "exp")]

        class SelfSems:

            def __init__(self, n):
                self.w_in = sem(f"{n}_w_in")
                self.b_in = sem(f"{n}_b_in")
                self.w_turned = sem(f"{n}_w_turned")
                self.wt_act = sem(f"{n}_wt_act")
                self.wt_dve = sem(f"{n}_wt_dve")
                self.proj = sem(f"{n}_proj")
                self.nat = sem(f"{n}_nat")
                self.high = sem(f"{n}_high")
                self.low = sem(f"{n}_low")
                self.turned = sem(f"{n}_turned")
                self.out_act = sem(f"{n}_turned_act")
                self.out_dve = sem(f"{n}_turned_dve")
                self.scores = sem(f"{n}_scores")
                self.max = sem(f"{n}_max")
                self.msplit = sem(f"{n}_max_split")
                self.exps = sem(f"{n}_exps")
                self.phigh = sem(f"{n}_exp_high")
                self.plow = sem(f"{n}_exp_low")
                self.pv = sem(f"{n}_pv")
                self.o = sem(f"{n}_o")
                self.steps = sem(f"{n}_steps")

        a0 = SelfSems("a0")
        a1 = SelfSems("a1")
        a1_albi, a1_turned, a1_att, a1_y, a1_yadd = (sem(f"a1_{n}") for n in ("alibi", "att_turned", "att", "y", "yadd"))
        a1_rows = sem("a1_rows")
        a1_wot_turned, a1_wot, a1_wo_in, a1_badd = (sem(f"a1_{n}") for n in ("wot_turned", "wot", "wo_in", "b_out"))

        def ahead_all(na):
            return [("weights", n) for n in range(na + 2)] + [("project", n) for n in range(T)]

        def ahead_bank(na, kind, n):
            return TB[(1, 0, 0, 1)[n] if kind == "weights" or na == 2 else (n + 1) % 2]

        def ahead_pe(pe, i, s, na, kind, n, first=False):
            bank, G, nw = ahead_bank(na, kind, n), na * NB, na + 2
            acts, dves = 2 * (i + 1), (nw // 2) * (i + 1)
            turned = i * (1 + G) + 1 + G // 2
            if kind == "weights":
                if n == 0:
                    pe.wait_ge(s.w_in, (i + 2) * 16 * nw)
                    if not first:
                        pe.wait_ge(s.out_dve, turned)
                elif n == 1 and not first:
                    pe.wait_ge(s.out_act, turned + 1)
                elif n == 2:
                    pe.wait_ge(s.wt_dve, dves + 1)
                elif n == 3:
                    pe.wait_ge(s.wt_act, acts + 1)
                    if not first:
                        pe.wait_ge(s.out_dve, turned + 1)
                for c in range(C):
                    mm = nc.tensor.transpose(bank[:, c * P:(c + 1) * P], W0[:, n, c * P:(c + 1) * P], ident[:])
                mm.then_inc(s.w_turned, 1)
            else:
                if n == 0:
                    pe.wait_ge(s.wt_act, acts + 2)
                    pe.wait_ge(s.wt_dve, dves + nw // 2)
                    if na == 1 and not first:
                        pe.wait_ge(s.out_dve, turned + 1)
                elif n == 1 and na == 2 and not first:
                    pe.wait_ge(s.out_act, turned + 2)
                elif n >= 2:
                    before = (1 if n == 2 else 0) if na == 2 else n - 2
                    pe.wait_ge(s.nat, 4 * (i + 1) + before + 2)
                    if n == 3 and na == 2 and not first:
                        pe.wait_ge(s.out_dve, turned + 2)
                for c in range(C):
                    mm = nc.tensor.matmul(bank[:, 0:nw * P].rearrange("p (m f) -> p m f", m=nw),
                                          XT[:, c, n * P:(n + 1) * P], WT[:, 0:nw, c, :], start=(c == 0),
                                          stop=(c == C - 1))
                mm.then_inc(s.proj, 1)

        def ahead_act(act, i, s, na, kind, n):
            if kind == "weights" and n % 2 == 0:
                act.wait_ge(s.w_turned, (na + 2) * (i + 1) + n + 2)
                nc.scalar.copy(WT[:, n].rearrange("p c f -> p (c f)"), ahead_bank(na, kind, n)[:]).then_inc(s.wt_act, 1)

        def ahead_dve(dve, i, s, na, kind, n):
            bank, nw = ahead_bank(na, kind, n), na + 2
            if kind == "weights" and n % 2 == 1:
                dve.wait_ge(s.w_turned, nw * (i + 1) + n + 2)
                nc.vector.tensor_copy(WT[:, n].rearrange("p c f -> p (c f)"), bank[:]).then_inc(s.wt_dve, 1)
            elif kind == "project":
                dve.wait_ge(s.b_in, (i + 2) * 16 * nw)
                dve.wait_ge(s.proj, 4 * (i + 1) + n + 1)
                nc.vector.tensor_tensor(NAT[:, 0:nw, n * P:(n + 1) * P],
                                        bank[:, 0:nw * P].rearrange("p (m f) -> p m f", m=nw),
                                        brow[:, 0:nw * P].rearrange("p (m f) -> p m f", m=nw), ALU.add
                                        ).then_inc(s.nat, 1)

        def self_pe(pe, i, s, na, ahead=False):
            G, F = na * NB, fills(na)
            NT, NMAX, NEXP = 2 + 2 * G, 3 * G, 4 * G

            def turn(m):
                if m < 2:
                    pe.wait_ge(s.low, i * (na + 2) + 1)
                elif m < 2 + G:
                    pe.wait_ge(s.low, i * (na + 2) + 2 + (m - 2) // NB)
                else:
                    pe.wait_ge(s.msplit, i * G + m - 1 - G)
                r = m - 2 - G
                if ahead and r in (1, 2):
                    pe.wait_ge(s.wt_act, 2 * (i + 1) + r)
                elif ahead and r == 3:
                    pe.wait_ge(s.nat, 4 * (i + 1) + 2)
                elif m >= 2:
                    pe.wait_ge(s.out_act if m % 2 == 0 else s.out_dve, i * (NT // 2) + m // 2)
                for pr in range(HG // 2):
                    for tt in range(2):
                        b = m % 2 if m < 2 else (m - 2) % NB
                        e = slice(pr * 2 * EXT, (pr + 1) * 2 * EXT)
                        src = KE[:, 2 * b + tt, e] if m < 2 else QE[:, ((m - 2) % G) // NB, 2 * b + tt, e]
                        o = (2 * pr + tt) * P
                        mm = nc.tensor.transpose(TBb[m % 2][:, o:o + P], src, identb[:])
                mm.then_inc(s.turned, 1)

            def turned_ready(m):
                pe.wait_ge(s.out_act if m % 2 == 0 else s.out_dve, i * (NT // 2) + m // 2 + 1)

            def bank_free(f):
                if f >= 2:
                    kind, g, r = F[f - 2]
                    if kind == "max":
                        pe.wait_ge(s.max, i * NMAX + 3 * g + r + 1)
                    else:
                        pe.wait_ge(s.exps, i * NEXP + 4 * g + r + 1)

            for m in range(2 + G):
                turn(m)
            f = 0
            for kind, g, r in self_order(na, ahead):
                b = g % NB
                if kind in ("weights", "project"):
                    ahead_pe(pe, i, s, na, kind, g)
                elif kind == "turn":
                    turn(2 + G + g)
                elif kind == "max":
                    if r == 0:
                        turned_ready(b)
                        turned_ready(2 + g)
                    bank_free(f)
                    qt, w = (0, P) if r == 0 else (1, 2 * P)
                    for half in range(2):
                        bank, n = pair[f % 2][:, half * 512:(half + 1) * 512], 512 // w
                        nc.tensor.matmul(bank.rearrange("p (n k) -> p n k", n=n), identb[:],
                                         maskq[:, 2 * P - w:].unsqueeze(1).to_broadcast([P, n, w]),
                                         start=True, stop=False)
                        for x in range(n):
                            h = 2 * x + half + (0 if r == 0 else 4 * (r - 1))
                            rows, o = slice((h % 2) * EXT, (h % 2 + 1) * EXT), (h // 2) * 2 * P
                            mm = nc.tensor.matmul(bank[:, x * w:(x + 1) * w], QR[rows, g, o + qt * P:o + (qt + 1) * P],
                                                  KR[rows, b, o:o + w], start=False, stop=(x == n - 1))
                    mm.then_inc(s.scores, 1)
                    f += 1
                elif kind == "exp":
                    if r == 0:
                        turned_ready(2 + G + g)
                    bank_free(f)
                    for hh in range(2):
                        bank, o, rows = pair[f % 2][:, hh * 512:hh * 512 + WID], r * 2 * P, slice(hh * EXT, (hh + 1) * EXT)
                        nc.tensor.matmul(bank, identb[:], maskk[:], start=True, stop=False)
                        nc.tensor.matmul(bank[:, 0:2 * P], KR[rows, b, o:o + P], QR[rows, g, o:o + 2 * P],
                                         start=False, stop=False)
                        mm = nc.tensor.matmul(bank[:, 2 * P:3 * P], KR[rows, b, o + P:o + 2 * P],
                                              QR[rows, g, o + P:o + 2 * P], start=False, stop=True)
                    mm.then_inc(s.scores, 1)
                    f += 1
                elif kind == "pv":
                    q = 4 * g + r
                    if r == 0:
                        pe.wait_ge(s.o, 2 * (i * G + g) + 1)
                    pe.wait_ge(s.plow, i * NEXP + q + 1)
                    for hh in range(2):
                        h = 2 * r + hh
                        for qt in range(2):
                            out = OB[qt][:, h * VW:(h + 1) * VW]
                            for kt in range(qt + 1):
                                o = (qt + kt) * P
                                v = VX[:, (2 * b + kt) * HG + h, 0:VW]
                                nc.tensor.matmul(out, PEH[:, q % RING, hh, o:o + P], v, start=(kt == 0), stop=False)
                                mm = nc.tensor.matmul(out, PEL[:, q % RING, hh, o:o + P], v, start=False,
                                                      stop=(kt == qt))
                    mm.then_inc(s.pv, 1)

        def heads(x):
            return x.rearrange("p (n d) -> p n d", d=HD)

        def rows_of(x, at, step=1):
            return x.rearrange("p t (h e d) -> p (t h) e d", h=HG, d=HD)[:, :, at // HD:at // HD + step + 1:step, :]

        def self_act(act, i, s, na, scale, ahead=False):
            G = na * NB
            NT, NEXP = 2 + 2 * G, 4 * G

            def turned_out(m):
                if m % 2 == 0:
                    act.wait_ge(s.turned, i * NT + m + 1)
                    dst = KR[:, m, :] if m < 2 else QR[:, (m - 2) % G, :]
                    nc.scalar.copy(dst, TBb[m % 2]).then_inc(s.out_act, 1)

            def high(q):
                act.wait_ge(s.exps, i * NEXP + q + 1)
                if q >= RING:
                    act.wait_ge(s.pv, i * NEXP + q - RING + 1)
                nc.scalar.copy(PEH[:, q % RING], PE32[:, q % RING]).then_inc(s.phigh, 1)

            act.wait_ge(s.nat, 4 * i + 5)
            nc.scalar.copy(rows_of(KE, 0, 2), heads(NAT[:, 0]).unsqueeze(2).to_broadcast([P, T * HG, 2, HD])
                           ).then_inc(s.high, 1)
            for a in range(na):
                nc.scalar.activation(rows_of(QE[:, a], 0), heads(NAT[:, 2 + a]).unsqueeze(2).to_broadcast(
                    [P, T * HG, 2, HD]), ACT.Copy, scale=scale).then_inc(s.high, 1)
            if isinstance(i, int) and i > 0:
                act.wait_ge(s.pv, i * NEXP)
            nc.scalar.copy(VX[:, :, HD:2 * HD], heads(NAT[:, 1])).then_inc(s.high, 1)
            for m in range(2 + G):
                turned_out(m)
            for kind, g, r in self_order(na, ahead):
                q = 4 * g + r
                if kind in ("weights", "project"):
                    ahead_act(act, i, s, na, kind, g)
                elif kind == "turn":
                    turned_out(2 + G + g)
                elif kind == "exp":
                    f = fills(na).index((kind, g, r))
                    act.wait_ge(s.scores, i * (3 * G + NEXP) + f + 1)
                    if q >= RING:
                        act.wait_ge(s.plow, i * NEXP + q - RING + 1)
                    nc.scalar.activation(PE32[:, q % RING], pair[f % 2].rearrange("p (h k) -> p h k", h=2)[:, :, 0:WID],
                                         ACT.Exp).then_inc(s.exps, 1)
                    if q >= 1:
                        high(q - 1)
            high(4 * G - 1)

        def self_steps(s, na):
            return 1 + na * NB * (1 + 2 * (4 if s is a0 else 3))

        def self_pool(pool, i, s, na):
            NEXP = 4 * na * NB
            for q in range(NEXP):
                if q >= RING:
                    pool.wait_ge(s.pv, i * NEXP + q - RING + 1)
                pool.wait_ge(s.phigh, i * NEXP + q + 1)
                nc.gpsimd.tensor_tensor(PEL[:, q % RING], PE32[:, q % RING], PEH[:, q % RING],
                                        ALU.subtract).then_inc(s.plow, 1)

        def self_dve(dve, i, s, na, scale, finish, ahead=False):
            G, nw = na * NB, na + 2
            NT, NMAX, NEXP = 2 + 2 * G, 3 * G, 4 * G
            steps = Steps(dve, s.steps, i * self_steps(s, na))

            def turned_out(m):
                if m % 2 == 1:
                    dve.wait_ge(s.turned, i * NT + m + 1)
                    dst = KR[:, m, :] if m < 2 else QR[:, (m - 2) % G, :]
                    nc.vector.tensor_copy(dst.bitcast(F32), TB[m % 2][:]).then_inc(s.out_dve, 1)

            steps(nc.vector.memset(QE[:, 0:na].rearrange("p a t (h e) -> p (a t h) e", h=HG)[:, :, MAX:MAX + 2], 0.0))
            dve.wait_ge(s.high, i * nw + 1)
            nc.vector.tensor_tensor(rows_of(KE, KLO)[:, :, 0], heads(NAT[:, 0]), rows_of(KE, KHI)[:, :, 0],
                                    ALU.subtract).then_inc(s.low, 1)
            for a in range(na):
                dve.wait_ge(s.high, i * nw + 2 + a)
                nc.vector.scalar_tensor_tensor(out=rows_of(QE[:, a], QLO)[:, :, 0], in0=heads(NAT[:, 2 + a]),
                                               scalar=scale, in1=rows_of(QE[:, a], 0)[:, :, 0], op0=ALU.mult,
                                               op1=ALU.subtract).then_inc(s.low, 1)
            dve.wait_ge(s.high, i * nw + nw)
            nc.vector.tensor_tensor(VX[:, :, 0:HD], heads(NAT[:, 1]), VX[:, :, HD:2 * HD],
                                    ALU.subtract).then_inc(s.low, 1)
            for m in range(2 + G):
                turned_out(m)
            for kind, g, r in self_order(na, ahead):
                a, b, q = g // NB, g % NB, 4 * g + r
                if kind in ("weights", "project"):
                    ahead_dve(dve, i, s, na, kind, g)
                elif kind == "turn":
                    turned_out(2 + G + g)
                elif kind == "max":
                    f = fills(na).index((kind, g, r))
                    n, w = (HG, P) if r == 0 else (HG // 2, 2 * P)
                    dst = nmax[:, g, 0, :] if r == 0 else nmax[:, g, 1, (r - 1) * n:r * n]
                    dst = dst.rearrange("p (x e) -> p e x", e=2)
                    dve.wait_ge(s.scores, i * (NMAX + NEXP) + f + 1)
                    nc.vector.tensor_reduce(dst, pair[f % 2].rearrange("p (e x k) -> p e x k", e=2, k=w), AX.X, ALU.max,
                                            negate=True).then_inc(s.max, 1)
                    if r == 2:
                        rows = QE[:, a, 2 * b:2 * b + 2].rearrange("p t (h e) -> p t h e", h=HG)
                        dve.wait_ge(s.max, i * NMAX + 3 * g + 3)
                        steps(nc.vector.tensor_copy(rows[:, :, :, MAX], nmax[:, g]))
                        nc.vector.tensor_tensor(rows[:, :, :, MAX + 1], nmax[:, g], rows[:, :, :, MAX],
                                                ALU.subtract).then_inc(s.msplit, 1)
                elif kind == "pv":
                    if r == 3:
                        dve.wait_ge(s.pv, i * NEXP + q + 1)
                        out = [OB[qt][:, 0:HG * VW].rearrange("p (h e) -> p h e", h=HG) for qt in range(2)]
                        steps.wait()
                        for qt in range(2):
                            steps.mark(nc.vector.reciprocal(rinv[:, qt, :], out[qt][:, :, 2 * HD]))
                            steps.mark(nc.vector.tensor_copy(olow[:, qt], out[qt][:, :, 0:HD]))
                        steps.wait()
                        for qt in range(2):
                            nc.vector.tensor_tensor(olow[:, qt], out[qt][:, :, HD:2 * HD], olow[:, qt],
                                                    ALU.add).then_inc(s.o, 1)
                        dve.wait_ge(s.o, 2 * (i * G + g) + 3)
                        finish(a, 2 * b, steps)

        m0_norm, m0_turned, m0_xqt = sem("m0_quantised"), sem("m0_turned"), sem("m0_xqt")
        m0_col, m0_colr, m0_prod = sem("m0_colsum"), sem("m0_colrow"), sem("m0_product")
        f0_wabs, f0_wtot, f0_wscale, f0_wq, f0_wturned, f0_wqt = (
            sem(f"f0_{n}") for n in ("wabs", "wtotal", "wscale", "wquant", "wturned", "wqt"))
        f0_ms, f0_rms, f0_q, f0_turned, f0_xqt, f0_prod, f0_y, f0_gelu, f0_sq = (
            sem(f"f0_{n}") for n in ("meansq", "rms", "quantised", "turned", "xqt", "product", "y", "gelu", "squares"))
        xw_kv, xw_q, xw_o = sem("x1_wkv_in"), sem("x1_wq_in"), sem("x1_wo_in")
        x_proj, x_nat, x_ms, x_r, x_kn, x_turned, x_tr = (
            sem(f"x1_{n}") for n in ("proj", "natural", "meansq", "rms", "k_normed", "qk_turned", "qkt"))
        x_sc, x_nb, x_exp, x_p, x_pt, x_pta, x_ptv, x_pv, x_ot, x_y, x_ya, x_steps = (
            sem(f"x1_{n}") for n in ("scores", "neg_bias", "exps", "probs", "p_turned", "pt_act", "pt_dve",
                                     "pv", "ot", "y", "yadd", "steps"))
        x_wqk = sem("x1_wqk")
        x_skv, x_sq_w, x_so, x_wk_st, x_vlo, x_trl, x_phi, x_oth = (
            sem(f"x1_{n}") for n in ("wkv_split", "wq_split", "wo_split", "split_high", "v_low", "qkt_low", "probs_high",
                                     "ot_high"))
        x_php = sem("x1_probs_high_pool")
        cxt_high, xt_high, xt_low = sem("cxt_high"), sem("xt_high"), sem("xt_low")
        g_in, g_turned, g_wt, g_h, g_hT, g_lg, g_lgd, g_exp, g_sel, g_selturned, g_selT, g_w, g_wexp, g_y, g_oexp = (
            sem(f"f1_{n}") for n in ("in", "turned", "wt", "h", "hT", "logits", "logits_max", "exps", "sel",
                                     "sel_turned", "selT", "w", "wexp", "y", "oexp"))
        ctx_q = sem("ctx_quantised")
        quant, m0_y, f0_mab, f0_x1 = (sem(n) for n in ("quantiser_step", "m0_added", "f0_maxabs", "f0_added"))
        x_sq, x_ri, f1_bdone, g_out = sem("x1_squares"), sem("x1_rsum_inv"), sem("f1_bias_added"), sem("f1_out")

        block = ctx.enter_context(nc.Block())


        def ln_dve(dve, n):
            for t in range(T):
                nc.vector.bn_stats(lnst[:, t, :], X[:, t, :]).then_inc(ln_stat, 1)
            for t in range(T):
                dve.wait_ge(ln_stat, n * T + t + 1)
                nc.vector.bn_aggr(lnmv[:, t, :], lnst[:, t, :]).then_inc(ln_aggr, 1)
            dve.wait_ge(ln_aggr, n * T + T)
            nc.vector.tensor_scalar(lnve[:], lnmv[:, :, 1], LN_EPS, None, ALU.add).then_inc(ln_var, 1)
            dve.wait_ge(ln_rstd, n + 1)
            for t in range(T):
                nc.vector.tensor_scalar(XN[:, t, :], X[:, t, :], lnmv[:, t, 0:1], lnrs[:, t:t + 1], ALU.subtract,
                                        ALU.mult).then_inc(ln_norm, 1)

        def ln_pool(pool, n):
            pool.wait_ge(ln_var, n + 1)
            nc.gpsimd.tensor_tensor(lnrs[:], lnve[:], neghalf[:, 0:T], ALU.pow).then_inc(ln_rstd, 1)

        def ln_pe(pe, n, k):
            pe.wait_ge(ln_norm, n * T + T)
            for c in range(C):
                for t in range(T):
                    mm = nc.tensor.transpose(S[c][:, t * P:(t + 1) * P], XN[:, t, c * P:(c + 1) * P], ident[:])
                mm.then_inc(ln_turned, 1)

        def ln_act(act, k):
            for c in (0, 2):
                act.wait_ge(ln_turned, k * C + c + 1)
                nc.scalar.copy(XT[:, c, :], S[c]).then_inc(xt_act, 1)

        def ln_copy_dve(dve, k):
            for c in (1, 3):
                dve.wait_ge(ln_turned, k * C + c + 1)
                nc.vector.tensor_copy(XT[:, c, :], S[c]).then_inc(xt_dve, 1)

        def ln_split_act(act, k):
            for c in range(C):
                act.wait_ge(ln_turned, k * C + c + 1)
                nc.scalar.copy(XTH[:, c, :], S[c]).then_inc(xt_high, 1)

        def ln_split_dve(dve, k):
            for c in range(C):
                dve.wait_ge(xt_high, c + 1)
                nc.vector.tensor_tensor(XTL[:, c, :], S[c], XTH[:, c, :], ALU.subtract).then_inc(xt_low, 1)

        def split_product(out, high, low, mhigh, mlow, start, stop):
            nc.tensor.matmul(out, high, mhigh, start=start, stop=False)
            nc.tensor.matmul(out, high, mlow, start=False, stop=False)
            return nc.tensor.matmul(out, low, mhigh, start=False, stop=stop)

        def turned_by(m):
            return (x_ptv, m // 3 + 1) if m % 3 == 0 else (x_pta, m - m // 3)

        def high_by(u):
            return (x_php if u % 4 in (1, 2) else x_phi), 2 * (u // 4) + (1, 1, 2, 2)[u % 4]

        def k_tiles(m):
            return {0: (0, 4), 1: (4, 6), 6: (10, 12), 7: (6, 10)}[m]

        def turning_bank(m):
            return TB[m % 2] if m < 6 else OB[m - 6]

        def unit_at(g, k):
            u = {0: GQ * g + 6, 2: GQ * g + 7, 3: GQ * g + 8, 5: GQ * g + 9}.get(k, T * GQ)
            return u if u < T * GQ else None

        def unit_summed(g, k):
            u = {0: GQ * g + 5, 2: GQ * g + 6, 3: GQ * g + 7, 5: GQ * g + 8}.get(k, T * GQ)
            return u if u < T * GQ else None

        def unit_ending(g, k):
            u = {0: GQ * g + 4, 1: GQ * g + 5, 3: GQ * g + 6, 4: GQ * g + 7}.get(k, T * GQ)
            return u if u < T * GQ else None

        def xt_ready(pe, k):
            pe.wait_ge(xt_act, 2 * k + 2)
            pe.wait_ge(xt_dve, 2 * k + 2)

        m0_in, f0_bin, a1_boutin, x1_nin, f1_bin, f1_base_in = (
            sem(f"{n}_in") for n in ("m0s", "f0b", "a1bout", "x1norm", "f1small", "f1base"))

        @block.sync
        def _(sp):
            sp.dma_start(X[:], x.rearrange("b (t p) d -> p (b t) d", p=P)).then_inc(x_in, 16)
            for n, a in enumerate((m0_s1, m0_z1, m0_s2, m0_z2)):
                sp.dma_start(qs[:, n:n + 1], a.partition_broadcast(P)).then_inc(m0_in, 16)

            with sp.Fori(0, 2) as i:
                sp.wait_ge(a0.w_turned, i * 4 + 1)
                wq = a0_wq.rearrange("(a i p) d -> a i p d", p=P, i=2)
                sp.dma_start(W0[:, 0, :], a0_wk.rearrange("(i p) d -> i p d", p=P)[i]).then_inc(a0.w_in, 16)
                sp.dma_start(W0[:, 1, :], a0_wv.rearrange("(i p) d -> i p d", p=P)[i]).then_inc(a0.w_in, 16)
                for a in range(2):
                    sp.dma_start(W0[:, 2 + a, :], wq[a][i]).then_inc(a0.w_in, 16)
                sp.wait_ge(a0.nat, 4 * i + 1)
                bq = a0_bq.rearrange("(a i p) -> a i p", p=P, i=2)
                sp.dma_start(brow[:, 0:P], a0_bk.rearrange("(i p) -> i p", p=P)[i].partition_broadcast(P)
                             ).then_inc(a0.b_in, 16)
                sp.dma_start(brow[:, P:2 * P], a0_bv.rearrange("(i p) -> i p", p=P)[i].partition_broadcast(P)
                             ).then_inc(a0.b_in, 16)
                for a in range(2):
                    sp.dma_start(brow[:, (2 + a) * P:(3 + a) * P], bq[a][i].partition_broadcast(P)
                                 ).then_inc(a0.b_in, 16)

            with sp.Fori(0, C) as i:
                sp.wait_ge(a0.w_turned, 9)
                sp.wait_ge(a1.w_turned, i * 3 + 1)
                w = a1_wqkv.rearrange("(m i p) d -> m i p d", m=3, p=P)
                bb = a1_bqkv.rearrange("(m i p) -> m i p", m=3, p=P)
                for m, src in enumerate((1, 2, 0)):
                    sp.dma_start(W0[:, m, :], w[src][i]).then_inc(a1.w_in, 16)
                sp.wait_ge(a1_wot_turned, i + 1)
                sp.dma_start(WO[:], a1_wout.rearrange("(c p) (i f) -> i p c f", p=P, f=P)[i]).then_inc(a1_wo_in, 16)
                sp.wait_ge(a0.nat, 9)
                sp.wait_ge(a1.nat, 4 * i + 1)
                for m, src in enumerate((1, 2, 0)):
                    sp.dma_start(brow[:, m * P:(m + 1) * P], bb[src][i].partition_broadcast(P)).then_inc(a1.b_in, 16)

            sp.wait_ge(a1_badd, T)
            sp.dma_start(f1b[:], f1_b.partition_broadcast(P)).then_inc(f1_base_in, 16)
            sp.wait_ge(a1_wot_turned, C + 1)
            sp.wait_ge(ctx_turned, CT)
            sp.wait_ge(ctx_q, 3)
            sp.dma_start(CX[:, 0:C, :], f1_w.rearrange("(c p) d -> p c d", p=P)).then_inc(g_in, 16)
            sp.dma_start(AW[:], f1_a.rearrange("e r d -> (e r) d")).then_inc(g_in, 16)
            sp.dma_start(RW[:], f1_rw).then_inc(g_in, 16)
            for c in range(C):
                sp.dma_start(BW[:, c], f1_bm.rearrange("e (c p) r -> c p e r", p=P)[c]).then_inc(g_in, 16)

            sp.wait_ge(a1.w_turned, 13)
            with sp.Fori(0, KVH) as i:
                sp.wait_ge(x_skv, i + 1)
                kvw = WKV[:].rearrange("p c (m d) -> p m c d", m=2)
                sp.dma_start(kvw[:, 0], x1_wk.rearrange("(c p) (i d) -> i p c d", p=P, d=XD)[i]).then_inc(xw_kv, 16)
                sp.dma_start(kvw[:, 1], x1_wv.rearrange("(c p) (i d) -> i p c d", p=P, d=XD)[i]).then_inc(xw_kv, 16)
                sp.wait_ge(x_sq_w, i + 1)
                sp.dma_start(WQ1[:], x1_wq.rearrange("(c p) (i d) -> i p c d", p=P, d=GQ * XD)[i]).then_inc(xw_q, 16)
                sp.wait_ge(x_so, i + 1)
                sp.dma_start(WO1[:], x1_wo.rearrange("(i h p) d -> i p h d", h=GQ, p=XD)[i]).then_inc(xw_o, 16)
            for t in range(T):
                sp.wait_ge(g_out, t + 1)
                sp.dma_start(out.rearrange("b (t p) d -> p (b t) d", p=P)[:, t], X[:, t, :]).then_inc(out_done, 16)
            sp.wait_ge(out_done, 16 * T)

        @block.gpsimd
        def _(pool):
            def ones_of_rows(x, at, n):
                return nc.gpsimd.memset(x.rearrange("p t (h e) -> p (t h) e", h=HG)[:, :, at:at + n], 1.0)

            masks = G[:, 0:2, :].rearrange("p t d -> p (t d)")[:, 0:5 * P]
            nc.gpsimd.memset(ident[:], 0.0).then_inc(zeroed, 1)
            nc.gpsimd.memset(masks, 0.0).then_inc(zeroed, 1)
            nc.gpsimd.memset(neghalf[:], -0.5).then_inc(consts, 1)
            pool.wait_ge(zeroed, 2)
            nc.gpsimd.affine_select(out=ident[:], in_=ident[:], compare_op=ALU.not_equal, fill=1.0, base=0,
                                    pattern=[[-1, P]], channel_multiplier=1).then_inc(consts, 1)
            nc.gpsimd.iota(posk[:], [[0, NB], [P, 2]], base=1 - SEQ, channel_multiplier=1,
                           allow_small_or_imprecise_dtypes=True).then_inc(consts, 1)
            nc.gpsimd.affine_select(out=masks[:, P:2 * P], in_=masks[:, P:2 * P], compare_op=ALU.is_ge, fill=NEG,
                                    base=0, pattern=[[-1, P]], channel_multiplier=1).then_inc(consts, 1)
            for k in (2, 4):
                nc.gpsimd.affine_select(out=masks[:, k * P:(k + 1) * P], in_=masks[:, k * P:(k + 1) * P],
                                        compare_op=ALU.is_ge, fill=NEG, base=0, pattern=[[1, P]],
                                        channel_multiplier=-1).then_inc(consts, 1)
            pool.wait_ge(consts, 6)
            nc.gpsimd.tensor_copy(maskq[:], masks[:, 0:2 * P]).then_inc(identb_done, 1)
            nc.gpsimd.tensor_copy(maskk[:], masks[:, 2 * P:5 * P]).then_inc(identb_done, 1)
            nc.gpsimd.tensor_copy(identb[:], ident[:]).then_inc(identb_done, 1)
            ln_pool(pool, 0)

            pool.dma_start(FW[:], f0_w.rearrange("(c p) d -> p c d", p=P)).then_inc(fw_in, 16)
            pool.dma_start(CX[:], ctx_4096.rearrange("b (k p) d -> p (b k) d", p=P)).then_inc(ctx_in, 16)
            pool.dma_start(fb[:], f0_b.partition_broadcast(P)).then_inc(f0_bin, 16)
            pool.dma_start(boutb[:], a1_bout.partition_broadcast(P)).then_inc(a1_boutin, 16)
            pool.dma_start(wn[:, 0:1], x1_qn.rearrange("(p o) -> p o", o=1)).then_inc(x1_nin, 16)
            pool.dma_start(wn[:, 1:2], x1_kn.rearrange("(p o) -> p o", o=1)).then_inc(x1_nin, 16)
            pool.dma_start(rbb[:], f1_rb.partition_broadcast(P)).then_inc(f1_bin, 16)
            pool.dma_start(mapi[:], f1_map.rearrange("(p o) -> p o", o=1)).then_inc(f1_bin, 16)

            nc.gpsimd.memset(ones[:], 1.0).then_inc(consts, 1)
            nc.gpsimd.memset(onesb[:], 1.0).then_inc(consts, 1)
            nc.gpsimd.iota(expi[:], [[1, NE], [0, RANK]], base=0, channel_multiplier=0,
                           allow_small_or_imprecise_dtypes=True).then_inc(consts, 1)
            tmp = CXT[:].rearrange("p c n -> p (c n)")
            pool.wait_ge(ctx_in, 16)
            pool.wait_ge(qs_ready, 1)
            nc.gpsimd.tensor_scalar(tmp, CX[:].rearrange("p c n -> p (c n)"), qsr[:, 1:2], qs[:, 3:4], ALU.mult,
                                    ALU.add).then_inc(ctx_q, 1)
            pool.wait_ge(ctx_q, 1)
            nc.gpsimd.tensor_scalar(tmp, tmp, 0.0, 255.0, ALU.max, ALU.min).then_inc(ctx_q, 1)
            pool.wait_ge(ctx_q, 2)
            nc.gpsimd.tensor_scalar(CXQ[:].rearrange("p c n -> p (c n)"), tmp, ROUND, ROUND + 128.0, ALU.add,
                                    ALU.subtract).then_inc(ctx_q, 1)
            with pool.Fori(0, 2) as i:
                self_pool(pool, i, a0, 2)
            ln_pool(pool, 1)
            fwf = FW[:].rearrange("p c n -> p (c n)")
            pool.wait_ge(f0_wscale, 1)
            nc.gpsimd.tensor_scalar(fwf, fwf, wsc[:, 1:2], 1.0, ALU.mult, ALU.min).then_inc(f0_wq, 1)
            pool.wait_ge(f0_wq, 1)
            nc.gpsimd.tensor_scalar(fwf, fwf, -1.0, ROUND, ALU.max, ALU.add).then_inc(f0_wq, 1)
            pool.wait_ge(f0_wq, 2)
            nc.gpsimd.tensor_scalar(WQN[:].rearrange("p c n -> p (c n)"), fwf, ROUND, None,
                                    ALU.subtract).then_inc(f0_wq, 1)
            ln_pool(pool, 2)
            pool.wait_ge(f0_ms, 1)
            nc.gpsimd.tensor_tensor(rrs[:], msq[:], neghalf[:, 0:T], ALU.pow).then_inc(f0_rms, 1)
            ln_pool(pool, 3)
            pool.wait_ge(f0_x1, 2 * T)
            nc.gpsimd.memset(KE.rearrange("p t e -> p (t e)"), 0.0).then_inc(zeroed, 1)
            nc.gpsimd.memset(VX[:], 1.0).then_inc(a1_rows, 1)
            pool.wait_ge(zeroed, 3)
            ones_of_rows(KE, MAX, 2).then_inc(a1_rows, 1)
            with pool.Fori(0, C) as i:
                self_pool(pool, i, a1, 1)
            ln_pool(pool, 4)
            pool.sem_inc(x_skv, 1)
            pool.sem_inc(x_sq_w, 1)
            pool.sem_inc(x_so, 1)

            def split_weights(pair_of, src, done, i, n):
                one = ones[:, 0:1].unsqueeze(1).to_broadcast([P, src.shape[1], src.shape[2]])
                nc.gpsimd.tensor_tensor(pair_of[:, 0], src, one, ALU.mult).then_inc(x_wk_st, 1)
                pool.wait_ge(x_wk_st, 3 * i + n)
                nc.gpsimd.tensor_tensor(pair_of[:, 1], src, pair_of[:, 0], ALU.subtract).then_inc(done, 1)

            pool.wait_ge(a1_y, C * T)
            with pool.Fori(0, KVH) as i:
                pool.wait_ge(x_proj, i * 10 + 1)
                pool.wait_ge(xw_kv, i * 32 + 32)
                split_weights(WKVP, WKV[:], x_skv, i, 1)
                pool.wait_ge(xw_q, i * 16 + 16)
                split_weights(WQP, WQ1[:], x_sq_w, i, 2)
                pool.wait_ge(x_y, i * T + 1)
                pool.wait_ge(xw_o, i * 16 + 16)
                split_weights(WOP, WO1[:], x_so, i, 3)
                NK = 2 * KT_N

                def rms_factors(n):
                    a, b = ((0, KT_N), (NK, NK + 2 * GQ), (NK + 2 * GQ, NK + T * GQ), (KT_N, NK))[n]
                    pool.wait_ge(x_ms, 4 * i + n + 1)
                    nc.gpsimd.tensor_tensor(rx[:, a:b], ssx[:, a:b], neghalf[:, 0:b - a], ALU.pow).then_inc(x_r, 1)

                for n in range(3):
                    rms_factors(n)
                for u in range(T * GQ):
                    g, h = u // GQ, u % GQ
                    if high_by(u)[0] is x_php:
                        if g >= 2 and h == 1:
                            pool.wait_ge(x_pt, i * 24 + KT_N * (g - 1))
                        pool.wait_ge(x_ri, i * 16 + u + 1)
                        nc.gpsimd.tensor_tensor(PXH[:, g % 2, h, :], PX[:, u % 4, :],
                                                xri[:, u:u + 1].to_broadcast([P, KEYS]), ALU.mult).then_inc(x_php, 1)
                    if u == 2:
                        rms_factors(3)
            ln_pool(pool, 5)

        @block.tensor
        def _(pe):
            for s in (a0.w_turned, a1.w_turned, a1_wot_turned, x_proj, x_y):
                pe.sem_inc(s, 1)
            pe.wait_ge(consts, 2)
            ln_pe(pe, 0, 0)
            pe.wait_ge(identb_done, 3)
            xt_ready(pe, 0)
            for kind, n in ahead_all(2):
                ahead_pe(pe, -1, a0, 2, kind, n, first=True)
            for i in range(2):
                self_pe(pe, i, a0, 2, ahead=(i == 0))

            pe.wait_ge(consts, NCONST)
            pe.wait_ge(fw_in, 16)
            pe.wait_ge(f0_wabs, 1)
            pe.wait_ge(a0.o, 17)
            nc.tensor.matmul(OB[1][:, 0:1], ones[:], wab[:], start=True, stop=True).then_inc(f0_wtot, 1)
            pe.wait_ge(ctx_in, 16)
            for k in range(CT):
                if k >= 2:
                    pe.wait_ge(cxt_ready, k - 1)
                for c in range(C):
                    mm = nc.tensor.transpose(TB[k % 2][:, c * P:(c + 1) * P], CX[:, k, c * P:(c + 1) * P], ident[:])
                mm.then_inc(ctx_turned, 1)
            pe.wait_ge(m0_norm, T)
            for c in range(C):
                for t in range(T):
                    mm = nc.tensor.transpose(Sb[c][:, t * P:(t + 1) * P], XQ[:, t, c * P:(c + 1) * P], identb[:])
                mm.then_inc(m0_turned, 1)
            pe.wait_ge(ctx_q, 3)
            pe.wait_ge(cxt_ready, CT)
            for b in range(NB):
                for k in range(C):
                    mm = nc.tensor.matmul(TB[b][0:1, :], onesb[:], CXQ[:, C * b + k, :], start=(k == 0),
                                          stop=(k == C - 1))
                mm.then_inc(m0_col, 1)
            pe.wait_ge(m0_xqt, C)
            for t in range(T):
                for c in range(C):
                    mm = nc.tensor.matmul(OB[0][:, t:t + 1], XQT[:, c, t * P:(t + 1) * P], onesb[:],
                                          start=(c == 0), stop=(c == C - 1))
            mm.then_inc(m0_col, 1)
            pe.wait_ge(m0_colr, NB)
            for t in range(T):
                b = t // 2
                for c in range(C):
                    nc.tensor.matmul(S[t], XQT[:, c, t * P:(t + 1) * P], CXQ[:, C * b + c, :], start=(c == 0),
                                     stop=False)
                nc.tensor.matmul(S[t], ones[0:1, :], colr[0:1, b, :], start=False, stop=True).then_inc(m0_prod, 1)
            pe.wait_ge(f0_wq, 3)
            for c in range(C):
                if c >= 2:
                    pe.wait_ge(f0_wqt, c - 1)
                for o in range(C):
                    mm = nc.tensor.transpose(TBb[c % 2][:, o * P:(o + 1) * P], WQN[:, o, c * P:(c + 1) * P], identb[:])
                mm.then_inc(f0_wturned, 1)

            pe.wait_ge(f0_q, T)
            for c in range(C):
                for t in range(T):
                    mm = nc.tensor.transpose(Sb[c][:, t * P:(t + 1) * P], XQ[:, t, c * P:(c + 1) * P], identb[:])
                mm.then_inc(f0_turned, 1)
            pe.wait_ge(f0_xqt, C)
            pe.wait_ge(f0_wqt, C)
            for t in range(T):
                for c in range(C):
                    mm = nc.tensor.matmul(S[t], XQT[:, c, t * P:(t + 1) * P], WQT[:, c, :], start=(c == 0),
                                          stop=(c == C - 1))
                mm.then_inc(f0_prod, 1)

            ln_pe(pe, 3, 1)
            xt_ready(pe, 1)
            def layer1_step(i, ahead):
                pe.wait_ge(a1_wo_in, i * 16 + 16)
                pe.wait_ge(a1.nat, 4 * i + 5)
                for c in range(C):
                    mm = nc.tensor.transpose(TB[1][:, c * P:(c + 1) * P], WO[:, c, :], ident[:])
                mm.then_inc(a1_wot_turned, 1)
                pe.wait_ge(a1.o, i * 4 + 1)
                pe.wait_ge(a1_yadd, i * T + 1)
                pe.wait_ge(a1_wot, i + 1)
                self_pe(pe, i, a1, 1, ahead)
                pe.wait_ge(a1.steps, (i + 1) * self_steps(a1, 1))
                if ahead:
                    pe.wait_ge(a1.nat, 4 * i + 9)
                for t in range(T):
                    mm = nc.tensor.transpose(TB[0][:, t * P:(t + 1) * P], AT[:, t, :], ident[:])
                mm.then_inc(a1_turned, 1)
                pe.wait_ge(a1_att, i + 1)
                for t in range(T):
                    nc.tensor.matmul(S[t], ATT[:, t * P:(t + 1) * P], WOT[:], start=True, stop=True).then_inc(a1_y, 1)

            for kind, n in ahead_all(1):
                ahead_pe(pe, -1, a1, 1, kind, n, first=True)
            with pe.Fori(0, C - 1) as i:
                layer1_step(i, True)
            layer1_step(C - 1, False)

            ln_pe(pe, 4, 2)
            pe.wait_ge(xt_low, C)
            with pe.Fori(0, KVH) as i:
                def project_q(t, bank):
                    for c in range(C):
                        x0 = t * P
                        mm = split_product(bank, XTH[:, c, x0:x0 + P], XTL[:, c, x0:x0 + P], WQP[:, 0, c, :],
                                           WQP[:, 1, c, :], c == 0, c == C - 1)
                    mm.then_inc(x_proj, 1)

                def turn(m):
                    if 2 <= m < 2 + T:
                        t = m - 2
                        pe.wait_ge(x_nat, i * 10 + 3 + t + 1)
                        sources = [QN[:, t, h * XD:(h + 1) * XD] for h in range(GQ)]
                    else:
                        pe.wait_ge(x_kn, 2 * i + m // 4 + 1)
                        k0, k1 = k_tiles(m)
                        sources = [KN[:, k, :] for k in range(k0, k1)]
                    if m >= 6:
                        pe.wait_ge(x_vlo, i * 6 + 6)
                    elif m >= 2:
                        pe.wait_ge(x_trl, i * 8 + m - 1)
                    for k, src in enumerate(sources):
                        mm = nc.tensor.transpose(turning_bank(m)[:, k * P:(k + 1) * P], src, ident[:])
                    mm.then_inc(x_turned, 1)

                def project_kv(n):
                    if n == 0:
                        pe.wait_ge(x_skv, i + 2)
                        pe.wait_ge(x_ot, i * T + 1)
                    elif n == 1:
                        pe.wait_ge(x_ya, i * T + 1)
                    else:
                        pe.wait_ge(x_vlo, i * 6 + n - 1)
                    for m in range(2):
                        kt = 2 * n + m
                        b, k = kt // KT_N, kt % KT_N
                        for c in range(C):
                            if k < CTX // P:
                                t0 = b * CTX + k * P
                                high, low = CXTH[:, c, t0:t0 + P], CXTL[:, c, t0:t0 + P]
                            else:
                                t0 = b * SEQ + (k - CTX // P) * P
                                high, low = XTH[:, c, t0:t0 + P], XTL[:, c, t0:t0 + P]
                            mm = split_product(OB[n % 2][:, m * 2 * XD:(m + 1) * 2 * XD], high, low, WKVP[:, 0, c, :],
                                               WKVP[:, 1, c, :], c == 0, c == C - 1)
                    mm.then_inc(x_proj, 1)

                def scores(g, h):
                    u, b = GQ * g + h, g // 2
                    if u < 2:
                        pe.wait_ge(x_nat, i * 10 + 2 * u + 5)
                        pe.wait_ge(x_trl, i * 8 + 4)
                    else:
                        pe.wait_ge(x_exp, i * 16 + u)
                    if g == 2 and h == 0:
                        pe.wait_ge(x_trl, i * 8 + 8)
                    qh, ql = QTP[:, 0, g, h * P:(h + 1) * P], QTP[:, 1, g, h * P:(h + 1) * P]
                    for k0, k1 in ((0, 512), (512, KEYS)):
                        mm = split_product(pair[u % 2][:, k0:k1], qh, ql, KTH[:, b * KEYS + k0:b * KEYS + k1],
                                           KTL[:, b * KEYS + k0:b * KEYS + k1], True, True)
                    mm.then_inc(x_sc, 1)

                def turn_probs(g, k):
                    m = KT_N * g + k
                    if k == 0:
                        pe.wait_ge(x_p, i * 16 + GQ * (g + 1))
                    if m >= 2:
                        s_of, n = turned_by(m - 2)
                        pe.wait_ge(s_of, i * (16 if s_of is x_pta else 8) + n)
                    for part, src in enumerate((PXH, PXL)):
                        for h in range(GQ):
                            o = part * 512 + h * P
                            mm = nc.tensor.transpose(TBb[m % 2][:, o:o + P], src[:, g % 2, h, k * P:(k + 1) * P],
                                                     identb[:])
                    mm.then_inc(x_pt, 1)

                def probs_v(g, k):
                    m = KT_N * g + k
                    if k == 0 and g == 0:
                        pe.wait_ge(x_trl, i * 8 + 7)
                    elif k == 0:
                        pe.wait_ge(x_ot, i * T + g + 1)
                    s_of, n = turned_by(m)
                    pe.wait_ge(s_of, i * (16 if s_of is x_pta else 8) + n)
                    kt = KT_N * (g // 2) + k
                    mm = split_product(OB[0][:], VH[:, kt, :], VL[:, kt, :], PXT[:, g % 2, k, 0:512],
                                       PXT[:, g % 2, k, 512:1024], k == 0, k == KT_N - 1)
                    if k == KT_N - 1:
                        mm.then_inc(x_pv, 1)

                def project_out(g, h):
                    if h == 0:
                        pe.wait_ge(x_ot, i * T + g + 2)
                        if g > 0:
                            pe.wait_ge(x_ya, i * T + g + 1)
                        else:
                            pe.wait_ge(x_so, i + 2)
                    mm = split_product(OB[1][:], OTP[:, 0, h * P:(h + 1) * P], OTP[:, 1, h * P:(h + 1) * P],
                                       WOP[:, 0, h, :], WOP[:, 1, h, :], h == 0, h == GQ - 1)
                    if h == GQ - 1:
                        mm.then_inc(x_y, 1)

                for n in range(3):
                    project_kv(n)
                pe.wait_ge(x_exp, i * 16 + 1)
                pe.wait_ge(x_sq_w, i + 2)
                project_q(0, S[0])
                project_q(1, S[1])
                turn(0)
                turn(1)
                project_q(2, S[2])
                turn(2)
                turn(3)
                project_q(3, S[3])
                turn(4)
                for u in range(6):
                    scores(u // GQ, u % GQ)
                    if u == 0:
                        turn(5)
                    elif u == 1:
                        project_kv(3)
                    elif u == 3:
                        project_kv(4)
                        project_kv(5)
                pe.wait_ge(x_trl, i * 8 + 6)
                for g in range(T):
                    for k in range(KT_N):
                        turn_probs(g, k)
                        u = unit_at(g, k)
                        if u is not None:
                            scores(u // GQ, u % GQ)
                        if g == 0 and k < 2:
                            turn(6 + k)
                        if g > 0 and k >= 3:
                            project_out(g - 1, k - 3)
                            if k == KT_N - 1:
                                project_out(g - 1, GQ - 1)
                        m = KT_N * g + k - 2
                        if m >= 0:
                            probs_v(m // KT_N, m % KT_N)
                probs_v(T - 1, KT_N - 2)
                probs_v(T - 1, KT_N - 1)
                for h in range(GQ):
                    project_out(T - 1, h)

            pe.wait_ge(g_in, 16 * (3 + C))
            for m in range(9):
                if m >= 2:
                    pe.wait_ge(g_wt, m - 1)
                for o in range(C):
                    if m < 4:
                        mm = nc.tensor.transpose(TB[m % 2][:, o * P:(o + 1) * P], CX[:, o, m * P:(m + 1) * P], ident[:])
                    elif m < 8 and o == 0:
                        c = m - 4
                        nc.tensor.transpose(TB[m % 2][:, 0:P], AW[:, c * P:(c + 1) * P], ident[:])
                        mm = nc.tensor.transpose(TB[m % 2][:, P:P + ROUTES], RW[:, c * P:(c + 1) * P],
                                                 ident[0:ROUTES, 0:ROUTES])
                    elif m == 8:
                        mm = nc.tensor.transpose(TB[0][:, o * P:(o + 1) * P], BW[:, o].rearrange("p e r -> p (e r)"),
                                                 ident[:])
                mm.then_inc(g_turned, 1)
            ln_pe(pe, 5, 3)
            xt_ready(pe, 2)
            pe.wait_ge(g_wt, 9)
            for t in range(T):
                for c in range(C):
                    mm = nc.tensor.matmul(OB[1][:, t * 16:t * 16 + ROUTES], XT[:, c, t * P:(t + 1) * P],
                                          RT[:, c, P:P + ROUTES], start=(c == 0), stop=(c == C - 1))
            mm.then_inc(g_lg, 1)
            for c in range(C):
                mm = nc.tensor.matmul(OB[0][:], RT[:, c, 0:P], XT[:, c, :], start=(c == 0), stop=(c == C - 1))
            mm.then_inc(g_h, 1)
            for t in range(T):
                for c in range(C):
                    nc.tensor.matmul(S[t], XT[:, c, t * P:(t + 1) * P], F1T[:, c, :], start=(c == 0), stop=False)
            pe.wait_ge(g_sel, 1)
            for t in range(T):
                mm = nc.tensor.transpose(TB[0][0:ROUTES, t * P:(t + 1) * P], selp[:, t, 0:ROUTES], ident[:])
            mm.then_inc(g_selturned, 1)
            pe.wait_ge(g_selT, 1)
            pe.wait_ge(g_oexp, 2)
            nc.tensor.matmul(TB[1][:], oexp[:], selT[:], start=True, stop=True).then_inc(g_w, 1)
            pe.wait_ge(g_hT, 1)
            for t in range(T):
                nc.tensor.matmul(S[t], hT[:, t * P:(t + 1) * P], BT[:], start=False, stop=True).then_inc(g_y, 1)

        @block.scalar
        def _(act):
            act.sem_inc(x_exp, 1)
            ln_act(act, 0)
            for kind, n in ahead_all(2):
                ahead_act(act, -1, a0, 2, kind, n)
            for i in range(2):
                self_act(act, i, a0, 2, SCALE0, ahead=(i == 0))
            act.wait_ge(fw_in, 16)
            nc.scalar.activation(G[:].rearrange("p t d -> p (t d)"), FW[:].rearrange("p c d -> p (c d)"), ACT.Abs,
                                 accum_out=wab[:]).then_inc(f0_wabs, 1)
            act.wait_ge(ctx_q, 3)
            for k in range(CT):
                act.wait_ge(ctx_turned, k + 1)
                nc.scalar.copy(CXTH[:, :, k * P:(k + 1) * P], TB[k % 2][:].rearrange("p (c n) -> p c n", c=C)
                               ).then_inc(cxt_high, 1)
            for c in range(C):
                act.wait_ge(m0_turned, c + 1)
                nc.scalar.copy(XQT[:, c, :], Sb[c][:, 0:512]).then_inc(m0_xqt, 1)
            for c in range(C):
                act.wait_ge(f0_wturned, c + 1)
                nc.scalar.copy(WQT[:, c, :], TBb[c % 2][:, 0:512]).then_inc(f0_wqt, 1)
            for t in range(T):
                act.wait_ge(ln_norm, 2 * T + t + 1)
                nc.scalar.activation(G[:, t, :], XN[:, t, :], ACT.Square, accum_out=msq0[:, t:t + 1]).then_inc(f0_sq, 1)
            for c in range(C):
                act.wait_ge(f0_turned, c + 1)
                nc.scalar.copy(XQT[:, c, :], Sb[c][:, 0:512]).then_inc(f0_xqt, 1)
            for t in range(T):
                act.wait_ge(f0_y, t + 1)
                nc.scalar.activation(G[:, t, :], TMP[:, t, :], ACT.Gelu).then_inc(f0_gelu, 1)

            ln_act(act, 1)
            act.wait_ge(a1_rows, 2)
            def layer1_step(i, ahead):
                self_act(act, i, a1, 1, SCALE1, ahead)
                act.wait_ge(a1_turned, i + 1)
                nc.scalar.copy(ATT[:], TB[0][:]).then_inc(a1_att, 1)

            for kind, n in ahead_all(1):
                ahead_act(act, -1, a1, 1, kind, n)
            with act.Fori(0, C - 1) as i:
                layer1_step(i, True)
            layer1_step(C - 1, False)

            ln_split_act(act, 2)
            with act.Fori(0, KVH) as i:
                def natural(n):
                    act.wait_ge(x_proj, i * 10 + n + 2)
                    if 3 <= n < 7:
                        nc.scalar.copy(QN[:, n - 3, :], S[n - 3]).then_inc(x_nat, 1)
                    else:
                        n = n if n < 3 else n - T
                        kv = OB[n % 2][:].rearrange("p (k d) -> p k d", k=2)
                        nc.scalar.copy(KN[:, 2 * n:2 * n + 2, :], kv[:, :, 0:XD])
                        nc.scalar.copy(VH[:, 2 * n:2 * n + 2, :], kv[:, :, XD:2 * XD]).then_inc(x_nat, 1)

                def turned_high(m):
                    act.wait_ge(x_turned, i * 8 + m + 1)
                    if 2 <= m < 2 + T:
                        nc.scalar.copy(QTP[:, 0, m - 2, :], turning_bank(m)[:]).then_inc(x_tr, 1)
                    else:
                        k0, k1 = k_tiles(m)
                        nc.scalar.activation(KTH[:, k0 * P:k1 * P], turning_bank(m)[:, 0:(k1 - k0) * P], ACT.Copy,
                                             scale=wqk[:, 0:1]).then_inc(x_tr, 1)

                def exps(u):
                    act.wait_ge(x_nb, i * 16 + u + 1)
                    if u >= 4:
                        act.wait_ge(x_p, i * 16 + u - 3)
                    nc.scalar.activation(PX[:, u % 4, :], pair[u % 2][:, 0:KEYS], ACT.Exp, bias=xnb[:, u:u + 1],
                                         scale=cq[:, 0, u:u + 1], accum_out=xsum[:, u:u + 1]).then_inc(x_exp, 1)

                def probs_high(u):
                    g, h = u // GQ, u % GQ
                    if high_by(u)[0] is not x_phi:
                        return
                    act.wait_ge(x_ri, i * 16 + u + 1)
                    if h == 0 and g >= 2:
                        act.wait_ge(x_pt, i * 24 + KT_N * (g - 1))
                    nc.scalar.activation(PXH[:, g % 2, h, :], PX[:, u % 4, :], ACT.Copy,
                                         scale=xri[:, u:u + 1]).then_inc(x_phi, 1)

                def out_high(g):
                    act.wait_ge(x_pv, i * T + g + 1)
                    nc.scalar.copy(OTP[:, 0, :], OB[0][:]).then_inc(x_oth, 1)

                for n in range(5):
                    natural(n)
                turned_high(0)
                turned_high(1)
                natural(5)
                turned_high(2)
                turned_high(3)
                natural(6)
                turned_high(4)
                exps(0)
                turned_high(5)
                exps(1)
                probs_high(0)
                natural(7)
                exps(2)
                exps(3)
                natural(8)
                probs_high(3)
                natural(9)
                exps(4)
                exps(5)
                probs_high(4)
                for g in range(T):
                    for k in range(KT_N):
                        m = KT_N * g + k
                        if m % 3 != 0:
                            act.wait_ge(x_pt, i * 24 + m + 1)
                            nc.scalar.copy(PXT[:, g % 2, k, :], TBb[m % 2]).then_inc(x_pta, 1)
                        if unit_at(g, k) is not None:
                            exps(unit_at(g, k))
                        if unit_summed(g, k) is not None:
                            probs_high(unit_summed(g, k))
                        if g == 0 and k < 2:
                            turned_high(6 + k)
                        if g > 0 and k == 1:
                            out_high(g - 1)
                out_high(T - 1)

            for m in range(9):
                act.wait_ge(g_turned, m + 1)
                if m < 4:
                    nc.scalar.copy(F1T[:, m, :], TB[m % 2][:]).then_inc(g_wt, 1)
                elif m < 8:
                    nc.scalar.copy(RT[:, m - 4, 0:P + ROUTES], TB[m % 2][:, 0:P + ROUTES]).then_inc(g_wt, 1)
                else:
                    nc.scalar.copy(BT[:], TB[0][:]).then_inc(g_wt, 1)
            ln_act(act, 3)
            act.wait_ge(g_lgd, 2)
            for t in range(T):
                nc.scalar.activation(pr[:, t, 0:ROUTES], lg[:, t, :], ACT.Exp, bias=lmx[:, t:t + 1],
                                     accum_out=lsum[:, t:t + 1]).then_inc(g_exp, 1)
            act.wait_ge(g_selturned, 1)
            nc.scalar.copy(selT[:], TB[0][0:ROUTES, :]).then_inc(g_selT, 1)
            act.wait_ge(g_w, 1)
            nc.scalar.mul(wexp[:], TB[1][:], 2.0).then_inc(g_wexp, 1)

        @block.vector
        def _(dve):
            for s in (a0.nat, a0.o, a1.nat, a1.o, a1_yadd, x_ya, x_sq, x_ot):
                dve.sem_inc(s, 1)
            steps = Steps(dve, dve_step)
            q_all, k_all = QE.rearrange("p a t (h e) -> p (a t h) e", h=HG), KE.rearrange("p t (h e) -> p (t h) e", h=HG)
            nc.vector.memset(VX[:], 1.0)
            steps(nc.vector.memset(q_all, 0.0))
            steps(nc.vector.memset(q_all[:, :, ALI:ALI + 3], 1.0))
            steps(nc.vector.memset(k_all, 0.0))
            steps(nc.vector.memset(k_all[:, :, MAX:MAX + 2], 1.0))
            dve.wait_ge(m0_in, 64)
            steps(nc.vector.reciprocal(qsr[:, 0:1], qs[:, 0:1]))
            nc.vector.reciprocal(qsr[:, 1:2], qs[:, 2:3]).then_inc(qs_ready, 1)
            steps(nc.vector.tensor_scalar(qc[:, 0:1], qs[:, 1:2], -1.0, 128.0, ALU.mult, ALU.add))
            steps(nc.vector.tensor_scalar(qc[:, 3:4], qs[:, 3:4], -1.0, 128.0, ALU.mult, ALU.add))
            steps(nc.vector.tensor_scalar(qc[:, 1:2], qc[:, 0:1], qc[:, 3:4], float(D), ALU.mult, ALU.mult))
            steps(nc.vector.tensor_tensor(qc[:, 2:3], qs[:, 0:1], qs[:, 2:3], ALU.mult))
            dve.wait_ge(x_in, 16)
            ln_dve(dve, 0)
            ln_copy_dve(dve, 0)
            dve.wait_ge(consts, 3)
            alb = albf[:, 0, :].rearrange("p (t h) -> p t h", h=HG)
            for j in range(HG):
                slope = float(np.float32(1.0) / np.power(np.float32(2.0), np.float32((j + 1) * 8.0 / 32)))
                nc.vector.tensor_scalar(alb[:, :, j], posk[:], slope, None, ALU.mult).then_inc(a1_albi, 1)
            dve.wait_ge(a1_albi, HG)
            for part in range(3):
                steps(nc.vector.tensor_copy(albb[:, part, :], albf[:, 0, :]))
                steps(nc.vector.tensor_tensor(albf[:, 0, :], albf[:, 0, :], albb[:, part, :], ALU.subtract))

            def divided(qt, dst):
                return nc.vector.tensor_tensor(dst.rearrange("p (h d) -> p h d", h=HG), olow[:, qt],
                                               rinv[:, qt, :].unsqueeze(2).to_broadcast([P, HG, HD]), ALU.mult)

            def into_x(i):
                def finish(a, t, steps):
                    for qt in range(2):
                        steps.mark(divided(qt, osc[:, qt, :]))
                    steps.wait()
                    for qt in range(2):
                        dst = X[:, t + qt, :].rearrange("p (a i f) -> p a i f", a=2, i=2)[:, a, i, :]
                        steps.mark(nc.vector.tensor_tensor(dst, dst, osc[:, qt, :], ALU.add))
                return finish

            for kind, n in ahead_all(2):
                ahead_dve(dve, -1, a0, 2, kind, n)
            for i in range(2):
                self_dve(dve, i, a0, 2, SCALE0, into_x(i), ahead=(i == 0))
            dve.wait_ge(a0.steps, 2 * self_steps(a0, 2))

            dve.wait_ge(consts, NCONST)
            dve.wait_ge(f0_wtot, 1)
            steps(nc.vector.tensor_scalar(wsc[:, 0:1], OB[1][:, 0:1], 1.0 / (D * D), 1e-5, ALU.mult, ALU.max))
            nc.vector.reciprocal(wsc[:, 1:2], wsc[:, 0:1]).then_inc(f0_wscale, 1)
            def context_low(ks):
                for k in ks:
                    dve.wait_ge(cxt_high, k + 1)
                    nc.vector.tensor_tensor(CXTL[:, :, k * P:(k + 1) * P], TB[k % 2][:].rearrange("p (c n) -> p c n", c=C),
                                            CXTH[:, :, k * P:(k + 1) * P], ALU.subtract).then_inc(cxt_ready, 1)

            ln_dve(dve, 1)
            dve.wait_ge(ln_norm, 2 * T)
            for t in range(T):
                nc.vector.tensor_scalar(TMP[:, t, :], XN[:, t, :], qsr[:, 0:1], qs[:, 1:2], ALU.mult,
                                        ALU.add).then_inc(quant, 1)
            for t in range(T):
                dve.wait_ge(quant, t + 1)
                nc.vector.tensor_scalar(TMP[:, t, :], TMP[:, t, :], 0.0, 255.0, ALU.max, ALU.min).then_inc(quant, 1)
            for t in range(T):
                dve.wait_ge(quant, T + t + 1)
                nc.vector.tensor_scalar(XQ[:, t, :], TMP[:, t, :], ROUND, ROUND + 128.0, ALU.add,
                                        ALU.subtract).then_inc(m0_norm, 1)
            context_low(range(CT))
            for b in range(NB):
                dve.wait_ge(m0_col, b + 1)
                nc.vector.tensor_scalar(colr[0:1, b, :], TB[b][0:1, :], qc[0:1, 0:1], qc[0:1, 1:2], ALU.mult,
                                        ALU.add).then_inc(m0_colr, 1)
            dve.wait_ge(m0_col, NB + 1)
            steps(nc.vector.tensor_scalar(rowc[:], OB[0][:, 0:T], qc[:, 3:4], None, ALU.mult))
            for t in range(T):
                dve.wait_ge(m0_prod, t + 1)
                nc.vector.tensor_scalar(TMP[:, t, :], S[t], rowc[:, t:t + 1], qc[:, 2:3], ALU.add,
                                        ALU.mult).then_inc(m0_y, 1)
                dve.wait_ge(m0_y, 2 * t + 1)
                nc.vector.tensor_tensor(X[:, t, :], X[:, t, :], TMP[:, t, :], ALU.add).then_inc(m0_y, 1)
            dve.wait_ge(m0_y, 2 * T)

            ln_dve(dve, 2)
            for t in range(T):
                dve.wait_ge(ln_norm, 2 * T + t + 1)
                nc.vector.tensor_reduce(mab[:, t:t + 1], XN[:, t, :], AX.X, ALU.max,
                                        apply_absolute_value=True).then_inc(f0_mab, 1)
            dve.wait_ge(f0_sq, T)
            nc.vector.tensor_scalar(msq[:], msq0[:], 1.0 / D, 1e-5, ALU.mult, ALU.add).then_inc(f0_ms, 1)
            dve.wait_ge(f0_rms, 1)
            dve.wait_ge(f0_mab, T)
            steps(nc.vector.tensor_tensor(amx[:], mab[:], rrs[:], ALU.mult))
            steps(nc.vector.tensor_scalar(amx[:], amx[:], 1e-5, None, ALU.max))
            steps(nc.vector.reciprocal(ascl[:], amx[:]))
            steps(nc.vector.tensor_scalar(ascl[:], ascl[:], 127.0, None, ALU.mult))
            steps(nc.vector.tensor_scalar(adq[:], amx[:], 1.0 / 127.0, wsc[:, 0:1], ALU.mult, ALU.mult))
            for t in range(T):
                nc.vector.tensor_scalar(TMP[:, t, :], XN[:, t, :], rrs[:, t:t + 1], ascl[:, t:t + 1], ALU.mult,
                                        ALU.mult).then_inc(quant, 1)
            for t in range(T):
                dve.wait_ge(quant, 2 * T + t + 1)
                nc.vector.tensor_scalar(TMP[:, t, :], TMP[:, t, :], -128.0, 127.0, ALU.max, ALU.min).then_inc(quant, 1)
            for t in range(T):
                dve.wait_ge(quant, 3 * T + t + 1)
                nc.vector.tensor_scalar(XQ[:, t, :], TMP[:, t, :], ROUND, ROUND, ALU.add,
                                        ALU.subtract).then_inc(f0_q, 1)
            dve.wait_ge(f0_bin, 16)
            for t in range(T):
                dve.wait_ge(f0_prod, t + 1)
                nc.vector.scalar_tensor_tensor(out=TMP[:, t, :], in0=S[t], scalar=adq[:, t:t + 1], in1=fb[:],
                                               op0=ALU.mult, op1=ALU.add).then_inc(f0_y, 1)
            for t in range(T):
                dve.wait_ge(f0_gelu, t + 1)
                nc.vector.tensor_tensor(G[:, t, :], G[:, t, :], XN[:, t, :], ALU.add).then_inc(f0_x1, 1)
                dve.wait_ge(f0_x1, 2 * t + 1)
                nc.vector.tensor_tensor(X[:, t, :], X[:, t, :], G[:, t, :], ALU.add).then_inc(f0_x1, 1)
            dve.wait_ge(f0_x1, 2 * T)

            def add_bias(row, done, n):
                dve.wait_ge(ln_norm, (n + 1) * T)
                for t in range(T):
                    nc.vector.tensor_tensor(X[:, t, :], X[:, t, :], row[:], ALU.add).then_inc(done, 1)
                dve.wait_ge(done, T)

            ln_dve(dve, 3)
            ln_copy_dve(dve, 1)
            dve.wait_ge(a1_boutin, 16)
            add_bias(boutb, a1_badd, 3)

            def into_at(a, t, steps):
                for qt in range(2):
                    steps.mark(divided(qt, AT[:, t + qt, :]))

            ke_rows = KE.rearrange("p t (h e) -> p (t h) e", h=HG)[:, :, ALI:ALI + 3]
            dve.wait_ge(a1_rows, 2)
            for part in range(3):
                nc.vector.tensor_copy(ke_rows[:, :, part], albb[:, part, :]).then_inc(a1_albi, 1)
            dve.wait_ge(a1_albi, HG + 3)
            def layer1_step(i, ahead):
                dve.wait_ge(a1_wot_turned, i + 2)
                nc.vector.tensor_copy(WOT[:], TB[1][:]).then_inc(a1_wot, 1)
                self_dve(dve, i, a1, 1, SCALE1, into_at, ahead)
                nc.vector.tensor_scalar(ke_rows, ke_rows, 0.25, None, ALU.mult).then_inc(a1_albi, 1)
                for t in range(T):
                    dve.wait_ge(a1_y, i * T + t + 1)
                    dve.wait_ge(a1_yadd, i * T + t + 1)
                    nc.vector.tensor_tensor(X[:, t, :], X[:, t, :], S[t], ALU.add).then_inc(a1_yadd, 1)

            for kind, n in ahead_all(1):
                ahead_dve(dve, -1, a1, 1, kind, n)
            with dve.Fori(0, C - 1) as i:
                layer1_step(i, True)
            layer1_step(C - 1, False)
            dve.wait_ge(a1_yadd, C * T + 1)

            dve.wait_ge(x1_nin, 32)
            nc.vector.tensor_tensor(wqk[:], wn[:, 0:1], wn[:, 1:2], ALU.mult).then_inc(x_wqk, 1)
            ln_dve(dve, 4)
            ln_split_dve(dve, 2)
            NQ, NK = T * GQ, NB * KT_N
            with dve.Fori(0, KVH) as i:
                steps_x = Steps(dve, x_steps, i * (4 + 16))

                squared = []

                def squares(n, src):
                    squared.append(n)
                    dve.wait_ge(x_sq, i * (NK + NQ) + max(len(squared) - 2, 0) + 1)
                    nc.vector.tensor_tensor_reduce(out=SQJ[:, len(squared) % 2, :], in0=src, in1=src, scale=1.0, scalar=0.0,
                                                   op0=ALU.mult, op1=ALU.add, accum_out=ssx[:, n:n + 1]
                                                   ).then_inc(x_sq, 1)

                def mean_squares(a, b):
                    dve.wait_ge(x_sq, i * (NK + NQ) + len(squared) + 1)
                    nc.vector.tensor_scalar(ssx[:, a:b], ssx[:, a:b], 1.0 / XD, 1e-6, ALU.mult, ALU.add
                                            ).then_inc(x_ms, 1)

                def q_squares(t):
                    dve.wait_ge(x_nat, i * 10 + 3 + t + 1)
                    for h in range(GQ):
                        squares(NK + GQ * t + h, QN[:, t, h * XD:(h + 1) * XD])

                def q_factors(a, b):
                    for sign in range(2):
                        steps_x(nc.vector.tensor_scalar(cq[:, sign, a:b], rx[:, NK + a:NK + b],
                                                        (1 - 2 * sign) * float(XD) ** -0.5, None, ALU.mult))

                def turned_low(m):
                    dve.wait_ge(x_tr, i * 8 + m + 1)
                    if 2 <= m < 2 + T:
                        nc.vector.tensor_tensor(QTP[:, 1, m - 2, :], turning_bank(m)[:], QTP[:, 0, m - 2, :],
                                                ALU.subtract).then_inc(x_trl, 1)
                    else:
                        k0, k1 = k_tiles(m)
                        ks = slice(k0 * P, k1 * P)
                        nc.vector.scalar_tensor_tensor(out=KTL[:, ks], in0=turning_bank(m)[:, 0:(k1 - k0) * P],
                                                       scalar=wqk[:, 0:1], in1=KTH[:, ks], op0=ALU.mult,
                                                       op1=ALU.subtract).then_inc(x_trl, 1)

                def kv_low(n):
                    dve.wait_ge(x_nat, i * 10 + (n if n < 3 else n + T) + 1)
                    nc.vector.tensor_tensor(VL[:, 2 * n:2 * n + 2, :],
                                            OB[n % 2][:].rearrange("p (k d) -> p k d", k=2)[:, :, XD:2 * XD],
                                            VH[:, 2 * n:2 * n + 2, :], ALU.subtract).then_inc(x_vlo, 1)
                    squares(2 * n, KN[:, 2 * n, :])
                    squares(2 * n + 1, KN[:, 2 * n + 1, :])

                def normalise_k(b):
                    dve.wait_ge(x_r, 4 * i + 1 + 3 * b)
                    ks = slice(b * KT_N, (b + 1) * KT_N)
                    nc.vector.tensor_tensor(KN[:, ks, :], KN[:, ks, :], rx[:, ks].unsqueeze(2).to_broadcast(
                        [P, KT_N, XD]), ALU.mult).then_inc(x_kn, 1)

                def row_max(u):
                    dve.wait_ge(x_sc, i * 16 + u + 1)
                    steps_x(nc.vector.tensor_reduce(xmx[:, u:u + 1], pair[u % 2][:, 0:KEYS], AX.X, ALU.max))
                    nc.vector.tensor_tensor(xnb[:, u:u + 1], xmx[:, u:u + 1], cq[:, 1, u:u + 1],
                                            ALU.mult).then_inc(x_nb, 1)

                def invert_sum(u):
                    dve.wait_ge(x_exp, i * 16 + u + 2)
                    nc.vector.reciprocal(xri[:, u:u + 1], xsum[:, u:u + 1]).then_inc(x_ri, 1)

                def probs_low(u):
                    g, h = u // GQ, u % GQ
                    high, n = high_by(u)
                    dve.wait_ge(high, i * 8 + n)
                    dve.wait_ge(x_ri, i * 16 + u + 1)
                    nc.vector.scalar_tensor_tensor(out=PXL[:, g % 2, h, :], in0=PX[:, u % 4, :], scalar=xri[:, u:u + 1],
                                                   in1=PXH[:, g % 2, h, :], op0=ALU.mult, op1=ALU.subtract
                                                   ).then_inc(x_p, 1)

                def out_low(g):
                    dve.wait_ge(x_oth, i * T + g + 1)
                    nc.vector.tensor_tensor(OTP[:, 1, :], OB[0][:], OTP[:, 0, :], ALU.subtract).then_inc(x_ot, 1)

                def add_out(g):
                    dve.wait_ge(x_y, i * T + g + 2)
                    dve.wait_ge(x_ya, i * T + g + 1)
                    nc.vector.tensor_tensor(X[:, g, :], X[:, g, :], OB[1][:], ALU.add).then_inc(x_ya, 1)

                for n in range(3):
                    kv_low(n)
                mean_squares(0, KT_N)
                q_squares(0)
                normalise_k(0)
                q_squares(1)
                mean_squares(NK, NK + 2 * GQ)
                turned_low(0)
                turned_low(1)
                q_squares(2)
                dve.wait_ge(x_r, 4 * i + 2)
                q_factors(0, 2 * GQ)
                turned_low(2)
                turned_low(3)
                q_squares(3)
                mean_squares(NK + 2 * GQ, NK + NQ)
                turned_low(4)
                row_max(0)
                turned_low(5)
                row_max(1)
                invert_sum(0)
                kv_low(3)
                row_max(2)
                invert_sum(1)
                probs_low(0)
                row_max(3)
                invert_sum(2)
                probs_low(1)
                kv_low(4)
                invert_sum(3)
                probs_low(2)
                probs_low(3)
                kv_low(5)
                mean_squares(KT_N, NK)
                row_max(4)
                row_max(5)
                invert_sum(4)
                normalise_k(1)
                dve.wait_ge(x_r, 4 * i + 3)
                q_factors(2 * GQ, NQ)
                for g in range(T):
                    for k in range(KT_N):
                        m = KT_N * g + k
                        if m % 3 == 0:
                            dve.wait_ge(x_pt, i * 24 + m + 1)
                            nc.vector.tensor_copy(PXT[:, g % 2, k, :].bitcast(F32), TB[m % 2][:]).then_inc(x_ptv, 1)
                        if unit_at(g, k) is not None:
                            row_max(unit_at(g, k))
                        if unit_summed(g, k) is not None:
                            invert_sum(unit_summed(g, k))
                        if unit_ending(g, k) is not None:
                            probs_low(unit_ending(g, k))
                        if g == 0 and k < 2:
                            turned_low(6 + k)
                        if g > 0 and k == 1:
                            out_low(g - 1)
                        if g > 1 and k == 0:
                            add_out(g - 2)
                add_out(T - 2)
                out_low(T - 1)
                add_out(T - 1)
            dve.wait_ge(x_ya, KVH * T + 1)

            ln_dve(dve, 5)
            ln_copy_dve(dve, 3)
            dve.wait_ge(f1_bin, 32)
            nc.vector.tensor_copy(mapf[:], mapi[:]).then_inc(g_oexp, 1)
            dve.wait_ge(g_oexp, 1)
            nc.vector.tensor_scalar(oexp[:], expi[:].rearrange("i e r -> i (e r)"), mapf[:, 0:1], None,
                                    ALU.is_equal).then_inc(g_oexp, 1)
            dve.wait_ge(g_lg, 1)
            nc.vector.tensor_tensor(lg[:], OB[1][:, 0:16 * T].rearrange("p (t n) -> p t n", t=T)[:, :, 0:ROUTES],
                                    rbb[:].unsqueeze(1).to_broadcast([P, T, ROUTES]), ALU.add).then_inc(g_lgd, 1)
            dve.wait_ge(g_lgd, 1)
            nc.vector.tensor_reduce(lmx[:], lg[:], AX.X, ALU.max, negate=True).then_inc(g_lgd, 1)
            dve.wait_ge(g_exp, T)
            steps(nc.vector.reciprocal(lsum[:], lsum[:]))
            steps(nc.vector.tensor_tensor(pr[:, :, 0:ROUTES], pr[:, :, 0:ROUTES],
                                          lsum[:].unsqueeze(2).to_broadcast([P, T, ROUTES]), ALU.mult))
            for t in range(T):
                steps(nc.vector.max(top8[:, t, :], pr[:, t, 0:ROUTES]))
                steps(nc.vector.match_replace(rep[:, t, 0:ROUTES], top8[:, t, :], pr[:, t, 0:ROUTES], -1.0))
            nc.vector.scalar_tensor_tensor(out=selp[:, :, 0:ROUTES], in0=rep[:, :, 0:ROUTES], scalar=0.0,
                                           in1=pr[:, :, 0:ROUTES], op0=ALU.is_lt, op1=ALU.mult).then_inc(g_sel, 1)
            dve.wait_ge(f1_base_in, 16)
            add_bias(f1b, f1_bdone, 5)
            dve.wait_ge(g_wexp, 1)
            dve.wait_ge(g_h, 1)
            nc.vector.tensor_tensor(hT[:], OB[0][:], wexp[:], ALU.mult).then_inc(g_hT, 1)
            for t in range(T):
                dve.wait_ge(g_y, t + 1)
                nc.vector.tensor_tensor(X[:, t, :], X[:, t, :], S[t], ALU.add).then_inc(g_out, 1)


_INS = ['x', 'ctx_4096', 'L0_attn_Wq', 'L0_attn_bq', 'L0_attn_Wk', 'L0_attn_bk', 'L0_attn_Wv', 'L0_attn_bv',
        'L0_xattn_x1_scale', 'L0_xattn_x1_zp', 'L0_xattn_x2_scale', 'L0_xattn_x2_zp', 'L0_ffn_W', 'L0_ffn_b',
        'L1_attn_w_qkv', 'L1_attn_b_qkv', 'L1_attn_w_out', 'L1_attn_b_out', 'L1_xattn_Wq', 'L1_xattn_Wk',
        'L1_xattn_Wv', 'L1_xattn_Wo', 'L1_xattn_q_norm_w', 'L1_xattn_k_norm_w', 'L1_ffn_base_W', 'L1_ffn_base_b',
        'L1_ffn_router_W', 'L1_ffn_router_b', 'L1_ffn_A', 'L1_ffn_B', 'L1_ffn_expert_map']


def kernel(**inputs):
    import numpy as _np
    import concourse.bacc as _bacc
    from concourse import mybir as _mybir
    from concourse.bass_utils import run_bass_kernel_spmd as _run

    nc = _bacc.Bacc("TRN2", target_bir_lowering=False, num_devices=1)
    arrays, args = {}, []
    for name in _INS:
        a = _np.ascontiguousarray(inputs[name])
        arrays[f"in_{name}"] = a
        args.append(nc.dram_tensor(f"in_{name}", a.shape, _mybir.dt.from_np(a.dtype), kind="ExternalInput").ap())
    out = nc.dram_tensor("out_0", (2, 256, 512), _mybir.dt.float32, kind="ExternalOutput").ap()
    decoder_program(nc, *args, out)
    r = _run(nc, [arrays], core_ids=[0])
    return r.results[0]["out_0"]
```
